# Optimizing a Trainium2 kernel written in Bass

```python
import numpy as np
import jax
import jax.numpy as jnp

def _softmax(x, axis=-1):
    return jax.nn.softmax(x, axis=axis)

def _gelu(x):
    return jax.nn.gelu(x, approximate=True)

def _silu(x):
    return jax.nn.silu(x)

def _sigmoid(x):
    return jax.nn.sigmoid(x)

def _layernorm(x, axis=-1, eps=1e-05):
    m = jnp.mean(x, axis=axis, keepdims=True)
    v = jnp.var(x, axis=axis, keepdims=True)
    return (x - m) / jnp.sqrt(v + eps)

def _scatter_add(tgt, idx, src, axis=0):
    return tgt.at[idx].add(src)

def _segment_sum(src, seg, n):
    return jax.ops.segment_sum(src, seg, n)
kernel_name = 'mk_flamingo_gated_d2_seqx_r4_b09ec0'

def setup_inputs(seed: int=0):
    np.random.seed(seed)
    _w = jnp.asarray

    def _rec_inputs():
        import jax
        import jax.numpy as jnp
        _rk = jax.random.key(seed)
        x = -0.0005146 + 1 * jax.random.normal(jax.random.fold_in(_rk, 1), (32, 256, 256), jnp.float32)
        _lenS = 256 - jax.random.randint(jax.random.fold_in(_rk, 7), (32,), 0, max(1, 256 // 4) + 1, jnp.int32)
        _lenS2 = 120 - jax.random.randint(jax.random.fold_in(_rk, 8), (32,), 0, max(1, 120 // 4) + 1, jnp.int32)
        _ctx_1024P = jax.random.normal(jax.random.fold_in(_rk, 11), (32, 16, 256), jnp.float32)
        _ctx_1024c = jax.random.dirichlet(jax.random.fold_in(_rk, 511), 0.3 * jnp.ones((16,), jnp.float32), (32, 120))
        _ctx_1024t = jnp.einsum('bsk,bkd->bsd', _ctx_1024c, _ctx_1024P)
        _ctx_1024t = _ctx_1024t * jax.lax.rsqrt(jnp.mean(jnp.square(_ctx_1024t)) + 1e-12) * 0.953939
        ctx_1024 = -0.000125008 + 0.999885 * (_ctx_1024t + 0.3 * jax.random.normal(jax.random.fold_in(_rk, 611), (32, 120, 256), jnp.float32))
        _validS = jnp.arange(256)[None, :] < _lenS[:, None]
        _validS2 = jnp.arange(120)[None, :] < _lenS2[:, None]
        _causal = jnp.tril(jnp.ones((256, 256), dtype=bool))
        mask_BxS2_bf1 = jnp.ones((32, 120), dtype=bool)
        _g = jax.random.normal(jax.random.fold_in(_rk, 9001), (2, 2), jnp.float32)
        _g = jnp.sign(_g) * jnp.maximum(jnp.abs(_g), 1.0) + (_g == 0) * 1.0
        g_xattn = _g[0]
        g_ffn = _g[1]
        return (x, ctx_1024, mask_BxS2_bf1, g_xattn, g_ffn)
    x, ctx_1024, mask_BxS2_bf1, g_xattn, g_ffn = _rec_inputs()

    def _L0_xattn_setup():
        import jax, jax.numpy as jnp
        import numpy as np
        H, DH = (8, 64)
        EPS = 1e-05

        def _ln(x, g, b):
            m = x.mean(-1, keepdims=True)
            v = ((x - m) ** 2).mean(-1, keepdims=True)
            return (x - m) / jnp.sqrt(v + EPS) * g + b
        key = jax.random.key(seed)
        ks = jax.random.split(key, 5)
        B, N, L, D = (4, 2048, 128, 256)
        inner = H * DH
        return {'x': jax.random.normal(ks[0], (B, N, D), jnp.float32), 'latents': jax.random.normal(ks[1], (B, L, D), jnp.float32), 'mask': jnp.ones((B, N), dtype=bool), 'g_x': jnp.ones((D,), jnp.float32), 'b_x': jnp.zeros((D,), jnp.float32), 'g_l': jnp.ones((D,), jnp.float32), 'b_l': jnp.zeros((D,), jnp.float32), 'w_q': jax.random.normal(ks[2], (D, inner), jnp.float32) * D ** (-0.5), 'w_kv': jax.random.normal(ks[3], (D, 2 * inner), jnp.float32) * D ** (-0.5), 'w_out': jax.random.normal(ks[4], (inner, D), jnp.float32) * inner ** (-0.5), 'g_o': jnp.ones((D,), jnp.float32), 'b_o': jnp.zeros((D,), jnp.float32)}
    _L0_xattn_all = _L0_xattn_setup()
    _L0_xattn_in = {k: v for k, v in _L0_xattn_all.items() if k in ('g_x', 'b_x', 'g_l', 'b_l', 'w_q', 'w_kv', 'w_out', 'g_o', 'b_o')}
    del _L0_xattn_all

    def _L0_ffn_setup():
        import jax, jax.numpy as jnp
        import numpy as np
        E = 8
        K = 2
        CAPACITY_FACTOR = 1.25
        key = jax.random.key(seed)
        ks = jax.random.split(key, 4)
        B, T, C, H = (8, 512, 256, 1024)
        x = jax.random.normal(ks[0], (B, T, C), jnp.float32)
        Wr = jax.random.normal(ks[1], (C, E), jnp.float32) * 0.02
        br = jnp.zeros((E,), jnp.float32)
        W1 = jax.random.normal(ks[2], (E, C, H), jnp.float32) * 0.02
        b1 = jnp.zeros((E, H), jnp.float32)
        W2 = jax.random.normal(ks[3], (E, H, C), jnp.float32) * 0.02
        b2 = jnp.zeros((E, C), jnp.float32)
        return {'x': x, 'Wr': Wr, 'br': br, 'W1': W1, 'b1': b1, 'W2': W2, 'b2': b2}
    _L0_ffn_all = _L0_ffn_setup()
    _L0_ffn_in = {k: v for k, v in _L0_ffn_all.items() if k in ('Wr', 'br', 'W1', 'b1', 'W2', 'b2')}
    del _L0_ffn_all

    def _L1_xattn_setup():
        import jax, jax.numpy as jnp
        import numpy as np
        DIM = 256
        NUM_HEADS = 16
        HEAD_DIM = DIM // NUM_HEADS
        B, L = (4, 1024)

        def _heads(x):
            Bb, Ll, _ = x.shape
            return x.reshape(Bb, Ll, NUM_HEADS, HEAD_DIM).transpose(0, 2, 1, 3)
        key = jax.random.key(seed)
        ks = jax.random.split(key, 11)
        s = 1.0 / np.sqrt(DIM)
        inp = {'q_seq': jax.random.normal(ks[0], (B, L, DIM), jnp.float32), 'k_seq': jax.random.normal(ks[1], (B, L, DIM), jnp.float32), 'v_seq': jax.random.normal(ks[2], (B, L, DIM), jnp.float32), 'Wq': jax.random.normal(ks[3], (DIM, DIM), jnp.float32) * s, 'bq': jax.random.normal(ks[4], (DIM,), jnp.float32) * s, 'Wk': jax.random.normal(ks[5], (DIM, DIM), jnp.float32) * s, 'bk': jax.random.normal(ks[6], (DIM,), jnp.float32) * s, 'Wv': jax.random.normal(ks[7], (DIM, DIM), jnp.float32) * s, 'bv': jax.random.normal(ks[8], (DIM,), jnp.float32) * s, 'Wo': jax.random.normal(ks[9], (DIM, DIM), jnp.float32) * s, 'bo': jax.random.normal(ks[10], (DIM,), jnp.float32) * s, 'extract_common': 1}
        return inp
    _L1_xattn_all = _L1_xattn_setup()
    _L1_xattn_in = {k: v for k, v in _L1_xattn_all.items() if k in ('Wq', 'bq', 'Wk', 'bk', 'Wv', 'bv', 'Wo', 'bo')}
    del _L1_xattn_all

    def _L1_ffn_setup():
        import jax, jax.numpy as jnp
        import numpy as np
        from jax import lax
        H = 256
        E = 8
        E_MLP = E - 4
        TOP_K = 2
        I = 128
        KC = 4
        SHARED_SCALE = 1.0
        key = jax.random.key(seed)
        ks = jax.random.split(key, 8)
        B, S = (4, 1024)
        s_h = 1.0 / np.sqrt(H)
        s_i = 1.0 / np.sqrt(I)
        return {'hidden_states': jax.random.normal(ks[0], (B, S, H), dtype=jnp.float32), 'Wr': jax.random.normal(ks[1], (H, E), dtype=jnp.float32) * s_h, 'router_bias': jnp.zeros((E,), dtype=jnp.float32), 'Wg': jax.random.normal(ks[2], (E_MLP, H, I), dtype=jnp.float32) * s_h, 'Wu': jax.random.normal(ks[3], (E_MLP, H, I), dtype=jnp.float32) * s_h, 'Wd': jax.random.normal(ks[4], (E_MLP, I, H), dtype=jnp.float32) * s_i, 'conv_w': jax.random.normal(ks[5], (KC, 1, H), dtype=jnp.float32) * (1.0 / np.sqrt(KC)), 'conv_b': jnp.zeros((H,), dtype=jnp.float32)}
    _L1_ffn_all = _L1_ffn_setup()
    _L1_ffn_in = {k: v for k, v in _L1_ffn_all.items() if k in ('Wr', 'router_bias', 'Wg', 'Wu', 'Wd', 'conv_w', 'conv_b')}
    del _L1_ffn_all
    return {'x': x, 'ctx_1024': ctx_1024, 'mask_BxS2_bf1': mask_BxS2_bf1, 'g_xattn': g_xattn, 'g_ffn': g_ffn, 'L0_xattn_g_x': _L0_xattn_in['g_x'], 'L0_xattn_b_x': _L0_xattn_in['b_x'], 'L0_xattn_g_l': _L0_xattn_in['g_l'], 'L0_xattn_b_l': _L0_xattn_in['b_l'], 'L0_xattn_w_q': _L0_xattn_in['w_q'], 'L0_xattn_w_kv': _L0_xattn_in['w_kv'], 'L0_xattn_w_out': _L0_xattn_in['w_out'], 'L0_xattn_g_o': _L0_xattn_in['g_o'], 'L0_xattn_b_o': _L0_xattn_in['b_o'], 'L0_ffn_Wr': _L0_ffn_in['Wr'], 'L0_ffn_br': _L0_ffn_in['br'], 'L0_ffn_W1': _L0_ffn_in['W1'], 'L0_ffn_b1': _L0_ffn_in['b1'], 'L0_ffn_W2': _L0_ffn_in['W2'], 'L0_ffn_b2': _L0_ffn_in['b2'], 'L1_xattn_Wq': _L1_xattn_in['Wq'], 'L1_xattn_bq': _L1_xattn_in['bq'], 'L1_xattn_Wk': _L1_xattn_in['Wk'], 'L1_xattn_bk': _L1_xattn_in['bk'], 'L1_xattn_Wv': _L1_xattn_in['Wv'], 'L1_xattn_bv': _L1_xattn_in['bv'], 'L1_xattn_Wo': _L1_xattn_in['Wo'], 'L1_xattn_bo': _L1_xattn_in['bo'], 'L1_ffn_Wr': _L1_ffn_in['Wr'], 'L1_ffn_router_bias': _L1_ffn_in['router_bias'], 'L1_ffn_Wg': _L1_ffn_in['Wg'], 'L1_ffn_Wu': _L1_ffn_in['Wu'], 'L1_ffn_Wd': _L1_ffn_in['Wd'], 'L1_ffn_conv_w': _L1_ffn_in['conv_w'], 'L1_ffn_conv_b': _L1_ffn_in['conv_b']}

def reference(x, ctx_1024, mask_BxS2_bf1, g_xattn, g_ffn, L0_xattn_g_x, L0_xattn_b_x, L0_xattn_g_l, L0_xattn_b_l, L0_xattn_w_q, L0_xattn_w_kv, L0_xattn_w_out, L0_xattn_g_o, L0_xattn_b_o, L0_ffn_Wr, L0_ffn_br, L0_ffn_W1, L0_ffn_b1, L0_ffn_W2, L0_ffn_b2, L1_xattn_Wq, L1_xattn_bq, L1_xattn_Wk, L1_xattn_bk, L1_xattn_Wv, L1_xattn_bv, L1_xattn_Wo, L1_xattn_bo, L1_ffn_Wr, L1_ffn_router_bias, L1_ffn_Wg, L1_ffn_Wu, L1_ffn_Wd, L1_ffn_conv_w, L1_ffn_conv_b):
    import jax
    import jax.numpy as jnp

    def _L0_xattn_ref(x, latents, mask, g_x, b_x, g_l, b_l, w_q, w_kv, w_out, g_o, b_o):
        import jax, jax.numpy as jnp
        import numpy as np
        H, DH = (8, 64)
        EPS = 1e-05

        def _ln(x, g, b):
            m = x.mean(-1, keepdims=True)
            v = ((x - m) ** 2).mean(-1, keepdims=True)
            return (x - m) / jnp.sqrt(v + EPS) * g + b
        B, Lq = (latents.shape[0], latents.shape[1])
        scale = DH ** (-0.5)
        xn = _ln(x, g_x, b_x)
        ln = _ln(latents, g_l, b_l)
        q = ln @ w_q
        kv_in = jnp.concatenate([xn, ln], axis=1)
        k, v = jnp.split(kv_in @ w_kv, 2, axis=-1)
        split = lambda t: t.reshape(t.shape[0], t.shape[1], H, DH).transpose(0, 2, 1, 3)
        q, k, v = (split(q) * scale, split(k), split(v))
        sim = jnp.einsum('bhid,bhjd->bhij', q, k)
        m = jnp.concatenate([mask, jnp.ones((B, Lq), dtype=bool)], axis=1)[:, None, None, :]
        sim = jnp.where(m, sim, -jnp.finfo(sim.dtype).max)
        attn = jax.nn.softmax(sim, axis=-1)
        out = jnp.einsum('bhij,bhjd->bhid', attn, v)
        out = out.transpose(0, 2, 1, 3).reshape(B, Lq, H * DH)
        return _ln(out @ w_out, g_o, b_o)

    def _L0_ffn_ref(x, Wr, br, W1, b1, W2, b2):
        import jax, jax.numpy as jnp
        import numpy as np
        E = 8
        K = 2
        CAPACITY_FACTOR = 1.25
        B, T, C = x.shape
        cap = max(1, int(T / E * CAPACITY_FACTOR))
        probs = jax.nn.softmax(x @ Wr + br, axis=-1)
        topk_p, topk_e = jax.lax.top_k(probs, K)
        e_flat = topk_e.reshape(B, T * K)
        p_flat = topk_p.reshape(B, T * K)
        oh = jax.nn.one_hot(e_flat, E, dtype=jnp.int32)
        pos_all = jnp.cumsum(oh, axis=1) - oh
        pos = jnp.take_along_axis(pos_all, e_flat[:, :, None], axis=2)[:, :, 0]
        keep = pos < cap
        b_idx = jnp.arange(B)[:, None]
        flat_idx = (e_flat * B + b_idx) * cap + jnp.minimum(pos, cap - 1)
        x_rep = jnp.broadcast_to(x[:, :, None, :], (B, T, K, C)).reshape(B, T * K, C)
        buf = jnp.zeros((E * B * cap, C), x.dtype).at[flat_idx.reshape(-1)].add((x_rep * keep[:, :, None].astype(x.dtype)).reshape(-1, C))
        buf = buf.reshape(E, B * cap, C)
        h = jax.nn.relu(jnp.einsum('enc,ech->enh', buf, W1) + b1[:, None, :])
        y = jnp.einsum('enh,ehc->enc', h, W2) + b2[:, None, :]
        y_tok = y.reshape(E * B * cap, C)[flat_idx.reshape(-1)].reshape(B, T * K, C)
        y_tok = y_tok * (p_flat * keep.astype(x.dtype))[:, :, None]
        return y_tok.reshape(B, T, K, C).sum(axis=2)

    def _L1_xattn_ref(q_seq, k_seq, v_seq, Wq, bq, Wk, bk, Wv, bv, Wo, bo, extract_common):
        import jax, jax.numpy as jnp
        import numpy as np
        DIM = 256
        NUM_HEADS = 16
        HEAD_DIM = DIM // NUM_HEADS
        B, L = (4, 1024)

        def _heads(x):
            Bb, Ll, _ = x.shape
            return x.reshape(Bb, Ll, NUM_HEADS, HEAD_DIM).transpose(0, 2, 1, 3)
        Q = _heads(q_seq @ Wq.T + bq)
        K = _heads(k_seq @ Wk.T + bk)
        V = _heads(v_seq @ Wv.T + bv)
        K_probs = jax.nn.softmax(K, axis=2)
        context = jnp.einsum('bhld,bhle->bhde', K_probs, V)
        attended = jnp.einsum('bhld,bhde->bhle', Q, context)
        if extract_common:
            target = attended
        else:
            target = V - attended
        Bb, _, Ll, _ = target.shape
        target = target.transpose(0, 2, 1, 3).reshape(Bb, Ll, DIM)
        return target @ Wo.T + bo

    def _L1_ffn_ref(hidden_states, Wr, router_bias, Wg, Wu, Wd, conv_w, conv_b):
        import jax, jax.numpy as jnp
        import numpy as np
        from jax import lax
        H = 256
        E = 8
        E_MLP = E - 4
        TOP_K = 2
        I = 128
        KC = 4
        SHARED_SCALE = 1.0
        B, S, Hd = hidden_states.shape
        T = B * S
        x = hidden_states.reshape(T, Hd)
        scores = jax.nn.sigmoid(x @ Wr)
        _, idx = lax.top_k(scores + router_bias, TOP_K)
        w = jnp.take_along_axis(scores, idx, axis=-1)
        w = w / (jnp.sum(w, axis=-1, keepdims=True) + 1e-09)
        cw = jnp.zeros((T, E), dtype=x.dtype).at[jnp.arange(T)[:, None], idx].add(w)
        g = jnp.einsum('th,ehi->tei', x, Wg)
        u = jnp.einsum('th,ehi->tei', x, Wu)
        hid = jax.nn.silu(g) * u
        mlp_out = jnp.einsum('tei,eih->teh', hid, Wd)
        routed = jnp.einsum('te,teh->th', cw[:, :E_MLP], mlp_out)
        routed = routed + cw[:, E_MLP:E_MLP + 1] * x
        routed = routed + cw[:, E_MLP + 2:E_MLP + 3] * x
        routed = routed + cw[:, E_MLP + 3:E_MLP + 4] * jax.nn.relu(x)
        routed = routed.reshape(B, S, Hd)
        shared = lax.conv_general_dilated(hidden_states, conv_w, window_strides=(1,), padding=[(KC - 1, 0)], dimension_numbers=('NHC', 'HIO', 'NHC'), feature_group_count=Hd) + conv_b
        return routed + SHARED_SCALE * shared
    x = x + jnp.tanh(g_xattn[0]) * _L0_xattn_ref(ctx_1024, _layernorm(x, axis=-1), mask_BxS2_bf1, L0_xattn_g_x, L0_xattn_b_x, L0_xattn_g_l, L0_xattn_b_l, L0_xattn_w_q, L0_xattn_w_kv, L0_xattn_w_out, L0_xattn_g_o, L0_xattn_b_o)
    x = x + jnp.tanh(g_ffn[0]) * _L0_ffn_ref(_layernorm(x, axis=-1), L0_ffn_Wr, L0_ffn_br, L0_ffn_W1, L0_ffn_b1, L0_ffn_W2, L0_ffn_b2)
    x = x + jnp.tanh(g_xattn[1]) * _L1_xattn_ref(_layernorm(x, axis=-1), ctx_1024, ctx_1024, L1_xattn_Wq, L1_xattn_bq, L1_xattn_Wk, L1_xattn_bk, L1_xattn_Wv, L1_xattn_bv, L1_xattn_Wo, L1_xattn_bo, 1)
    x = x + jnp.tanh(g_ffn[1]) * _L1_ffn_ref(_layernorm(x, axis=-1), L1_ffn_Wr, L1_ffn_router_bias, L1_ffn_Wg, L1_ffn_Wu, L1_ffn_Wd, L1_ffn_conv_w, L1_ffn_conv_b)
    return x

_drawn_inputs = setup_inputs


def setup_inputs(seed=0):
    import zlib

    import numpy as np

    out = dict(_drawn_inputs(seed))
    spreads = {'g_ffn': (-1.0, 0.2),
     'L0_xattn_g_x': (1.0, 0.2),
     'L0_xattn_b_x': (0.0, 0.1),
     'L0_xattn_g_l': (1.0, 0.2),
     'L0_xattn_b_l': (0.0, 0.1),
     'L0_xattn_g_o': (1.0, 0.2),
     'L0_xattn_b_o': (0.0, 0.1),
     'L0_ffn_br': (0.0, 0.328),
     'L0_ffn_b1': (0.0, 0.746),
     'L0_ffn_b2': (0.0, 0.448),
     'L1_ffn_router_bias': (0.0, 0.1),
     'L1_ffn_conv_b': (0.0, 0.1)}
    factors = {'L0_ffn_W1': 2.961, 'L1_xattn_bk': 8.0}
    for name, (base, spread) in spreads.items():
        noise = np.random.default_rng([zlib.crc32(name.encode()), seed]).standard_normal(out[name].shape)
        drawn = base * np.exp(spread * noise) if base else spread * noise
        out[name] = jnp.asarray(drawn.astype(out[name].dtype))
    for name, factor in factors.items():
        out[name] = (out[name] * factor).astype(out[name].dtype)
    return out
```

```python
from contextlib import ExitStack

import numpy as np

import concourse.bass as bass
from concourse import mybir

F32 = mybir.dt.float32
F32R = mybir.dt.float32r
BF16 = mybir.dt.bfloat16
U8 = mybir.dt.uint8
U16 = mybir.dt.uint16
U32 = mybir.dt.uint32
ALU = mybir.AluOpType
ACT = mybir.ActivationFunctionType
AX = mybir.AxisListType

B, S, D = 32, 256, 256
C = 120
P = 128
KD = D // P
QT = S // P
H0, DH = 8, 64
INNER = H0 * DH
KI = INNER // P
NKV = C + S
EPS = 1e-5
E0, CAP = 8, max(1, int(S / 8 * 1.25))
SLOTS = B * CAP
HID = 1024
KH = HID // P
HD1 = 16
E1, EM = 8, 4
KC = 4
MASKED = 1e30
NOWHERE = 1 << 20
PASSES = ((0, 0), (0, 1), (1, 0))


def at_least(eng, sem, value):
    if not (isinstance(value, int) and value <= 0):
        eng.wait_ge(sem, value)


def by_itself(eng, waited):
    eng.sem_inc(waited, 1)


def batches(eng, step):
    step(0, 0)
    step(1, 1)
    with eng.Fori(1, B // 2 - 1) as pair:
        step(pair * 2, 0)
        step(pair * 2 + 1, 1)
    step(B - 2, 0)
    step(B - 1, 1)


def split_product(nc, out, stationary, moving, tiles, start=True, stop=True):
    todo = [(a, b, t) for t in range(tiles) for a, b in PASSES]
    for n, (a, b, t) in enumerate(todo):
        last = nc.tensor.matmul(out, stationary(a, t), moving(b, t),
                                start=start and n == 0, stop=stop and n == len(todo) - 1)
    return last


def zero_semaphores(nc, sems):
    with nc.Block() as block:
        @block.gpsimd
        def _(pool):
            nums = sorted(s.num for s in sems)
            first = nums[0]
            for num, following in zip(nums, nums[1:] + [-1]):
                if following != num + 1:
                    pool.sem_clear(range(first, num + 1))
                    first = following


def attend(nc, t, keep):
    ctx = ExitStack()
    with ctx:
        def sb(name, shape, dt=F32):
            return ctx.enter_context(nc.sbuf_tensor(name, shape, dt))

        def pb(name, shape):
            return ctx.enter_context(nc.psum_tensor(name, shape, F32))

        sems = []

        def sem(name):
            sems.append(ctx.enter_context(nc.semaphore(name)))
            return sems[-1]

        stage_kv = sb("a_stage_kv", [P, KD, 2 * INNER])
        wq = sb("a_wq", [P, 2, KD, INNER], F32R)
        wkv = sb("a_wkv", [P, 2, KD, 2 * INNER], F32R)
        wo = sb("a_wo", [P, 2, KI, D], F32R)
        wr = sb("a_wr", [P, KD, E0])
        ident = sb("a_ident", [P, P])
        tri = sb("a_tri", [P, 2, P], BF16)
        headrow_f = sb("a_headrow_f", [P, H0, P], BF16)
        headrow = sb("a_headrow", [P, H0, P], F32R)
        firstrow = sb("a_firstrow", [P, P], BF16)
        iota_e = sb("a_iota_e", [P, E0])
        slot0 = sb("a_slot0", [P, B, E0])
        mask_u8 = sb("a_mask_u8", [P, B, C], U8)
        mask_t8 = sb("a_mask_t8", [C, B], U8)
        mask_bias = sb("a_mask_bias", [C, B])
        mask_row = sb("a_mask_row", [P, 2, C], BF16)
        aff = sb("a_aff", [P, 4, KD])
        go = sb("a_go", [P, D])
        bo = sb("a_bo", [P, D])
        br = sb("a_br", [P, E0])
        gate = sb("a_gate", [P, 4])
        tgate = sb("a_tgate", [P, 4])
        minus_half = sb("a_minus_half", [P, 4])
        zeros = sb("a_zeros", [P, 2 * D])
        xn = sb("a_xn", [P, 2, QT, D])
        cn = sb("a_cn", [P, 2, D])
        xr = sb("a_xr", [P, 2, QT, D])
        stats = sb("a_stats", [P, 3, 6])
        mv = sb("a_mv", [P, 3, 2])
        var = sb("a_var", [P, 3])
        rs = sb("a_rs", [P, 3])
        xh = sb("a_xh", [P, 3, D])
        kvin = sb("a_kvin", [P, KD, NKV])
        kvin2 = sb("a_kvin2", [P, 2, KD, NKV], F32R)
        qT = sb("a_qT", [P, 2, 2, KI, S], F32R)
        kT = sb("a_kT", [P, 2, 2, KI, NKV], F32R)
        vo = sb("a_vo", [P, 2, 2, 3, KI, 3, DH], F32R)
        nmax = sb("a_nmax", [P, 2, QT, H0])
        nmaxT = sb("a_nmaxT", [P, 2, S], F32R)
        prob = sb("a_prob", [P, 2, 3, S])
        prob2 = sb("a_prob2", [P, 2, 2, 3, S], F32R)
        rden = sb("a_rden", [P, S])
        att = sb("a_att", [P, KI, S])
        att2 = sb("a_att2", [P, 2, KI, S], F32R)
        y1 = sb("a_y1", [P, QT, D])
        xb = sb("a_xb", [P, QT, D])
        x1 = sb("a_x1", [P, 2, QT, D])
        stage_q = att[:].rearrange("p m s -> p (m s)").rearrange("p (k n) -> p k n", k=KD)
        stage_o = x1[:].rearrange("p a k d -> p (a k) d")
        stats1 = sb("a_stats1", [P, QT, 6])
        mv1 = sb("a_mv1", [P, QT, 2])
        var1 = sb("a_var1", [P, QT])
        rs1 = sb("a_rs1", [P, QT])
        stats2 = sb("a_stats2", [P, QT, 6])
        mv2 = sb("a_mv2", [P, QT, 2])
        var2 = sb("a_var2", [P, QT])
        rs2 = sb("a_rs2", [P, QT])
        x2h = sb("a_x2h", [P, QT, D])
        rT = sb("a_rT", [P, KD, S])
        lg = sb("a_lg", [P, QT, E0])
        lmax = sb("a_lmax", [P, QT])
        le = sb("a_le", [P, QT, E0])
        lsum = sb("a_lsum", [P, QT])
        pr = sb("a_pr", [P, QT, E0])
        top = sb("a_top", [P, QT, E0])
        topi = sb("a_topi", [P, QT, E0], U32)
        topf = sb("a_topf", [P, QT, 2])
        oh = sb("a_oh", [P, QT, 2, E0])
        ohs = sb("a_ohs", [P, QT, E0], BF16)
        at_e = sb("a_at_e", [P, QT, 2, E0])
        pos = sb("a_pos", [P, QT, 2])
        at_b = sb("a_at_b", [P, QT, 2, E0])
        base = sb("a_base", [P, QT, 2])
        kept = sb("a_kept", [P, QT, 2])
        slot = sb("a_slot", [P, QT, 2])
        slot_s = sb("a_slot_s", [P, QT, 2])
        wsel = sb("a_wsel", [P, QT, 2])
        sidx = sb("a_sidx", [P, QT * 2], U32)

        score_x = pb("a_score_x", [P, QT, S])
        score_c = pb("a_score_c", [P, 512])
        ctxv = pb("a_ctxv", [P, 512])
        probe = [pb(f"a_probe{i}", [P, 512]) for i in range(2)]
        proj = [pb(f"a_proj{i}", [P, 512]) for i in range(2)]
        misc = pb("a_misc", [P, 512])

        w_in = [sem(f"a_w_in{i}") for i in range(3)]
        small_in = sem("a_small_in")
        w_high, w_low = sem("a_w_high"), sem("a_w_low")
        const_ok = sem("a_const_ok")
        const_g = sem("a_const_g")
        waited = sem("a_waited")
        gate_ok = sem("a_gate_ok")
        zero_ok = sem("a_zero_ok")
        zeroed = sem("a_zeroed")
        xn_in = [sem(f"a_xn_in{i}") for i in range(2)]
        cn_in = [sem(f"a_cn_in{i}") for i in range(2)]
        xr_in = [sem(f"a_xr_in{i}") for i in range(2)]
        stats_ok, mv_ok, var_ok, rs_ok, xh_ok = (sem("a_" + s) for s in
                                                 ("stats_ok", "mv_ok", "var_ok", "rs_ok", "xh_ok"))
        xT_ok, kvin_ok, kvin_high, kvin_low = (sem("a_" + s) for s in
                                               ("xT_ok", "kvin_ok", "kvin_high", "kvin_low"))
        proj_ok, proj_high, proj_low = (sem("a_" + s) for s in ("proj_ok", "proj_high", "proj_low"))
        mrow_ok, probe_ok, nmax_ok, nmT_ok, nmT_out = (sem("a_" + s) for s in
                                                       ("mrow_ok", "probe_ok", "nmax_ok", "nmT_ok", "nmT_out"))
        score_ok, exp_ok, prob_high, prob_low = (sem("a_" + s) for s in
                                                 ("score_ok", "exp_ok", "prob_high", "prob_low"))
        ctxv_ok, rden_ok, att_ok, att_high, att_low = (sem("a_" + s) for s in
                                                       ("ctxv_ok", "rden_ok", "att_ok", "att_high", "att_low"))
        out_ok, stats1_ok, mv1_ok, var1_ok, rs1_ok = (sem("a_" + s) for s in
                                                      ("out_ok", "stats1_ok", "mv1_ok", "var1_ok", "rs1_ok"))
        y1_ok, xb_ok, x1_ok = (sem("a_" + s) for s in ("y1_ok", "xb_ok", "x1_ok"))
        x1_out = [sem(f"a_x1_out{i}") for i in range(2)]
        stats2_ok, mv2_ok, var2_ok, rs2_ok, x2h_ok = (sem("a_" + s) for s in
                                                      ("stats2_ok", "mv2_ok", "var2_ok", "rs2_ok", "x2h_ok"))
        rT_ok, rT_out, logit_ok, count_ok = (sem("a_" + s) for s in ("rT_ok", "rT_out", "logit_ok", "count_ok"))
        soft, le_ok, route = (sem("a_" + s) for s in ("soft", "le_ok", "route"))
        sent = keep["sent"]

        N_SOFT = 14
        N_ROUTE = 11

        def projection(p, u, plane):
            if u < 2:
                return (proj[u % 2][:].rearrange("p (m s) -> p m s", m=2), qT[:, p, plane, 2 * u:2 * u + 2],
                        DH ** -0.5)
            if u < 6:
                return proj[u % 2][:, 0:NKV], kT[:, p, plane, u - 2], 1.0
            i, rows = ((2, C), (0, P), (1, P))[u - 6]
            return (proj[u % 2][0:rows].rearrange("p (m v d) -> p m v d", m=KI, v=2),
                    vo[0:rows, p, plane, i, :, 0:3:2], 1.0)

        ctx.callback(zero_semaphores, nc, sems)
        block = ctx.enter_context(nc.Block())

        @block.sync
        def _(eng):
            eng.dma_start(stage_q, t["w_q"].rearrange("(k p) n -> p k n", p=P)).then_inc(w_in[0], 16)
            eng.dma_start(stage_kv[:], t["w_kv"].rearrange("(k p) n -> p k n", p=P)).then_inc(w_in[1], 16)

            def load(b, p):
                at_least(eng, xh_ok, 3 * (b - 1))
                eng.dma_start(xn[:, p], t["x"][bass.ds(b, 1)].rearrange("o (k p) d -> p (o k) d", p=P)) \
                    .then_inc(xn_in[p], 16)
                eng.dma_start(cn[0:C, p], t["ctx"][bass.ds(b, 1)].rearrange("o c d -> c (o d)")) \
                    .then_inc(cn_in[p], 16)

            load(0, 0)
            load(1, 1)
            small = [(ident[:], t["ident"]), (tri[:].bitcast(U16), t["tri"]), (headrow_f[:].bitcast(U16), t["headrow"]),
                     (firstrow[:].bitcast(U16), t["firstrow"]), (iota_e[:], t["iota_e"]), (slot0[:], t["slot0"]),
                     (mask_u8[:], t["mask"].partition_broadcast(P)), (mask_t8[:], t["mask_t"]),
                     (go[:], t["g_o"].partition_broadcast(P)), (bo[:], t["b_o"].partition_broadcast(P)),
                     (br[:], t["br"].partition_broadcast(P)),
                     (gate[:, 0:2], t["g_xattn"].partition_broadcast(P)),
                     (gate[:, 2:4], t["g_ffn"].partition_broadcast(P)),
                     (wr[:], t["Wr0"].rearrange("(k p) n -> p k n", p=P))]
            small += [(aff[:, i], t[name]) for i, name in enumerate(("g_l", "b_l", "g_x", "b_x"))]
            assert len(small) == N_SMALL
            for dst, src in small:
                eng.dma_start(dst, src).then_inc(small_in, 16)
            eng.dma_start(stage_o, t["w_out"].rearrange("(k p) n -> p k n", p=P)).then_inc(w_in[2], 16)
            eng.wait_ge(zero_ok, 1)
            rows = P * 10
            with eng.Fori(0, E0 * SLOTS // rows) as n:
                eng.dma_start(t["slots"][bass.ts(n, rows)].rearrange("(p r t) d -> p r (t d)", p=P, t=2),
                              zeros[:].unsqueeze(1).to_broadcast([P, 5, 2 * D])) \
                    .then_inc(zeroed, 16)

            def step(b, p):
                at_least(eng, x1_ok, QT * (b - 1))
                eng.dma_start(xr[:, p], t["x"][bass.ds(b, 1)].rearrange("o (k p) d -> p (o k) d", p=P)) \
                    .then_inc(xr_in[p], 16)
                if not isinstance(b, int) or b + 2 < B:
                    load(b + 2, p)
                if not (isinstance(b, int) and b < 1):
                    store(b - 1, 1 - p)

            def store(b, p):
                eng.wait_ge(x1_ok, QT * (b + 1))
                eng.dma_start(t["x1"][bass.ds(b, 1)].rearrange("o (k p) d -> p (o k) d", p=P), x1[:, p]) \
                    .then_inc(x1_out[p], 16)

            batches(eng, step)
            store(B - 1, 1)
            for p in range(2):
                eng.wait_ge(x1_out[p], 16 * (B // 2))

        @block.gpsimd
        def _(eng):
            nc.gpsimd.memset(zeros[:], 0.0).then_inc(zero_ok, 1)
            nc.gpsimd.memset(minus_half[:], -0.5).then_inc(const_g, 1)
            nc.gpsimd.memset(var[:], 1.0).then_inc(const_g, 1)
            eng.wait_ge(const_g, 2)

            def rsqrt(b, mean_var, mean_var_ok, n, v, v_ok, r, r_ok, scales):
                eng.wait_ge(mean_var_ok, n * (b + 1))
                at_least(eng, r_ok, b)
                by_itself(eng, waited)
                for lo, hi, rows, mul, add in scales:
                    nc.gpsimd.tensor_scalar(v[0:rows, lo:hi], mean_var[0:rows, lo:hi, 1], mul, add,
                                            ALU.mult, ALU.add).then_inc(v_ok, 1)
                eng.wait_ge(v_ok, len(scales) * (b + 1))
                nc.gpsimd.tensor_tensor(r[:], v[:], minus_half[:, 0:v.shape[1]], ALU.pow).then_inc(r_ok, 1)

            def norm(b):
                at_least(eng, xh_ok, 3 * b)
                rsqrt(b, mv, mv_ok, 3, var, var_ok, rs, rs_ok,
                      ((0, 2, P, 1.0 + EPS, EPS * EPS), (2, 3, C, 1.0, EPS)))

            def kvin_lower(b):
                eng.wait_ge(kvin_high, b + 1)
                at_least(eng, proj_ok, 9 * b)
                nc.gpsimd.tensor_tensor(kvin2[:, 1], kvin[:], kvin2[:, 0].bitcast(F32), ALU.subtract) \
                    .then_inc(kvin_low, 1)

            def prob_lower(b, h):
                eng.wait_ge(prob_high, H0 * b + h + 1)
                at_least(eng, ctxv_ok, H0 * b + h - 1)
                nc.gpsimd.tensor_tensor(prob2[:, h % 2, 1], prob[:, h % 2],
                                        prob2[:, h % 2, 0].bitcast(F32), ALU.subtract).then_inc(prob_low, 1)

            def att_lower(b, m):
                eng.wait_ge(att_high, KI * b + m + 1)
                at_least(eng, out_ok, b)
                nc.gpsimd.tensor_tensor(att2[:, 1, m], att[:, m], att2[:, 0, m].bitcast(F32),
                                        ALU.subtract).then_inc(att_low, 1)

            def residual(b, p):
                eng.wait_ge(xr_in[p], 16 * (b // 2 + 1))
                at_least(eng, x1_ok, QT * b)
                nc.gpsimd.tensor_tensor(xb[:], xr[:, p], bo[:].unsqueeze(1).to_broadcast([P, QT, D]),
                                        ALU.add).then_inc(xb_ok, 1)

            def norm1(b):
                at_least(eng, x1_ok, QT * b)
                rsqrt(b, mv1, mv1_ok, QT, var1, var1_ok, rs1, rs1_ok, ((0, QT, P, 1.0, EPS),))

            def norm2(b):
                rsqrt(b, mv2, mv2_ok, QT, var2, var2_ok, rs2, rs2_ok, ((0, QT, P, 1.0, EPS),))

            def dispatch(b):
                eng.wait_ge(route, N_ROUTE * (b + 1))
                by_itself(eng, waited)
                for n in range(QT * 2):
                    nc.gpsimd.indirect_dma_start(
                        out=t["slots"], out_offset=bass.IndirectOffsetOnAxis(ap=sidx[:, n:n + 1], axis=0),
                        in_=x2h[:, n // 2], in_offset=None, bounds_check=E0 * SLOTS - 1,
                        oob_is_err=False).then_inc(sent, 16)

            norm(0)
            kvin_lower(0)
            eng.wait_ge(zeroed, 16 * (E0 * SLOTS // (P * 10)))
            eng.wait_ge(const_ok, N_CONST)

            def step(b, p):
                first, last = isinstance(b, int) and b == 0, isinstance(b, int) and b == B - 1
                prob_lower(b, 0)
                if not last:
                    norm(b + 1)
                if not first:
                    residual(b - 1, 1 - p)
                    norm1(b - 1)
                prob_lower(b, 1)
                if not last:
                    kvin_lower(b + 1)
                if not first:
                    norm2(b - 1)
                for h in range(2, H0):
                    prob_lower(b, h)
                    if h % 2 == 1 and h > 2:
                        att_lower(b, h // 2 - 1)
                    if h == 6 and not first:
                        dispatch(b - 1)
                att_lower(b, KI - 1)

            batches(eng, step)
            residual(B - 1, 1)
            norm1(B - 1)
            norm2(B - 1)
            dispatch(B - 1)
            eng.wait_ge(sent, 16 * 2 * QT * B)

        @block.scalar
        def _(eng):
            eng.wait_ge(small_in, 16 * N_SMALL)
            nc.scalar.activation(tgate[:], gate[:], ACT.Tanh).then_inc(gate_ok, 1)
            eng.wait_ge(w_in[0], 16)
            nc.scalar.activation(wq[:, 0], stage_q, ACT.Copy).then_inc(w_high, 1)
            eng.wait_ge(w_in[1], 16)
            nc.scalar.activation(wkv[:, 0], stage_kv[:], ACT.Copy).then_inc(w_high, 1)
            eng.wait_ge(w_in[2], 16)
            nc.scalar.activation(wo[:, 0], stage_o, ACT.Copy).then_inc(w_high, 1)

            def affine(b):
                at_least(eng, kvin_low, b)
                eng.wait_ge(xT_ok, 2 * b + 1)
                for k in range(KD):
                    nc.scalar.activation(kvin[:, k, C:NKV], proj[0][:, k * S:(k + 1) * S], ACT.Identity,
                                         bias=aff[:, 1, k:k + 1], scale=aff[:, 0, k:k + 1]).then_inc(kvin_ok, 1)
                eng.wait_ge(xT_ok, 2 * b + 2)
                for k in range(KD):
                    nc.scalar.activation(kvin[:, k, 0:C], proj[1][:, k * C:(k + 1) * C], ACT.Identity,
                                         bias=aff[:, 3, k:k + 1], scale=aff[:, 2, k:k + 1]).then_inc(kvin_ok, 1)

            def high(b, p, u):
                eng.wait_ge(proj_ok, 9 * b + u + 1)
                src, dst, scale = projection(p, u, 0)
                if u == 0:
                    at_least(eng, score_ok, 2 * H0 * (b - 1))
                if u == 6:
                    at_least(eng, ctxv_ok, H0 * (b - 1))
                nc.scalar.activation(dst, src, ACT.Copy, scale=scale).then_inc(proj_high, 1)

            def maxima(b, p):
                eng.wait_ge(nmT_ok, b + 1)
                at_least(eng, score_ok, 2 * H0 * (b - 1))
                for row in (0, 64):
                    nc.scalar.activation(nmaxT[row:row + H0, p], misc[0:H0, 0:S], ACT.Copy).then_inc(nmT_out, 1)

            def exps(b, h):
                at_least(eng, prob_low, H0 * b + h - 1)
                eng.wait_ge(score_ok, 2 * (H0 * b + h) + 1)
                nc.scalar.activation(prob[:, h % 2, 0:2], score_x[:], ACT.Exp).then_inc(exp_ok, 1)
                eng.wait_ge(score_ok, 2 * (H0 * b + h) + 2)
                by_itself(eng, waited)
                nc.scalar.activation(prob[0:C, h % 2, 2], score_c[0:C, 0:S], ACT.Exp,
                                     bias=mask_bias[:, bass.ds(b, 1)]).then_inc(exp_ok, 1)

            def att_higher(b, m):
                eng.wait_ge(att_ok, H0 * b + 2 * m + 2)
                at_least(eng, out_ok, b)
                nc.scalar.activation(att2[:, 0, m], att[:, m], ACT.Copy).then_inc(att_high, 1)

            def router_in(b):
                eng.wait_ge(rT_ok, b + 1)
                nc.scalar.activation(rT[:], misc[:], ACT.Copy).then_inc(rT_out, 1)

            def router_exp(b):
                eng.wait_ge(soft, N_SOFT * b + 3)
                nc.scalar.activation(le[:], lg[:], ACT.Exp).then_inc(le_ok, 1)

            affine(0)
            eng.wait_ge(const_ok, N_CONST)
            for u in range(9):
                high(0, 0, u)
            maxima(0, 0)

            def step(b, p):
                first, last = isinstance(b, int) and b == 0, isinstance(b, int) and b == B - 1
                for h in range(H0):
                    exps(b, h)
                    if not last:
                        if h == 1:
                            affine(b + 1)
                        for u in {2: (0, 1), 3: (2, 3), 4: (4, 5), 5: (6,), 6: (7,), 7: (8,)}.get(h, ()):
                            high(b + 1, 1 - p, u)
                    if not first:
                        if h == 3:
                            router_in(b - 1)
                        if h == 5:
                            router_exp(b - 1)
                    if h % 2 == 1 and h > 2:
                        att_higher(b, h // 2 - 1)
                if not last:
                    maxima(b + 1, 1 - p)
                att_higher(b, KI - 1)

            batches(eng, step)
            router_in(B - 1)
            router_exp(B - 1)

        @block.vector
        def _(eng):
            nc.vector.memset(prob[:], 0.0).then_inc(const_ok, 1)
            nc.vector.memset(nmaxT[:].bitcast(F32), 0.0).then_inc(const_ok, 1)
            nc.vector.memset(vo[:, :, 0].bitcast(F32), 1.0).then_inc(const_ok, 1)
            nc.vector.memset(vo[:, :, 1].bitcast(F32), 0.0).then_inc(const_ok, 1)
            eng.wait_ge(small_in, 16 * N_SMALL)
            nc.vector.tensor_copy(headrow[:], headrow_f[:]).then_inc(const_ok, 1)
            nc.vector.tensor_scalar(mask_bias[:], mask_t8[:], -1.0, MASKED, ALU.add, ALU.mult).then_inc(const_ok, 1)
            eng.wait_ge(gate_ok, 1)
            nc.vector.tensor_scalar(go[:], go[:], tgate[:, 0:1], None, ALU.mult).then_inc(const_ok, 1)
            nc.vector.tensor_scalar(bo[:], bo[:], tgate[:, 0:1], None, ALU.mult).then_inc(const_ok, 1)
            eng.wait_ge(const_ok, N_CONST)
            nc.vector.tensor_copy(keep["gate"][:], tgate[:]).then_inc(w_low, 1)

            def stat(b, p):
                eng.wait_ge(xn_in[p], 16 * (b // 2 + 1))
                eng.wait_ge(cn_in[p], 16 * (b // 2 + 1))
                at_least(eng, xh_ok, 3 * b)
                for k in range(QT):
                    nc.vector.bn_stats(stats[:, k], xn[:, p, k]).then_inc(stats_ok, 1)
                nc.vector.bn_stats(stats[0:C, 2], cn[0:C, p]).then_inc(stats_ok, 1)
                for k, rows in ((0, P), (1, P), (2, C)):
                    eng.wait_ge(stats_ok, 3 * b + k + 1)
                    by_itself(eng, waited)
                    nc.vector.bn_aggr(mv[0:rows, k], stats[0:rows, k]).then_inc(mv_ok, 1)

            def normalise(b, p):
                eng.wait_ge(rs_ok, b + 1)
                at_least(eng, xT_ok, 2 * b)
                for k in range(QT):
                    nc.vector.tensor_scalar(xh[:, k], xn[:, p, k], mv[:, k, 0:1], rs[:, k:k + 1],
                                            ALU.subtract, ALU.mult).then_inc(xh_ok, 1)
                nc.vector.tensor_scalar(xh[0:C, 2], cn[0:C, p], mv[0:C, 2, 0:1], rs[0:C, 2:3],
                                        ALU.subtract, ALU.mult).then_inc(xh_ok, 1)

            def kvin_higher(b):
                eng.wait_ge(kvin_ok, 4 * (b + 1))
                at_least(eng, proj_ok, 9 * b)
                nc.vector.tensor_copy(kvin2[:, 0], kvin[:]).then_inc(kvin_high, 1)

            def lower(b, p, u):
                eng.wait_ge(proj_high, 9 * b + u + 1)
                src, dst, scale = projection(p, u, 1)
                high = projection(p, u, 0)[1].bitcast(F32)
                if scale == 1.0:
                    low = nc.vector.tensor_tensor(dst, src, high, ALU.subtract)
                else:
                    low = nc.vector.scalar_tensor_tensor(dst, src, scale, high, ALU.mult, ALU.subtract)
                low.then_inc(proj_low, 1)

            def mask_line(b, p):
                at_least(eng, probe_ok, 16 * (b - 1))
                nc.vector.tensor_scalar(mask_row[:, p], mask_u8[:, bass.ds(b, 1)].rearrange("p o c -> p (o c)"),
                                        -1.0, MASKED, ALU.add, ALU.mult).then_inc(mrow_ok, 1)

            def row_max(b, p, u):
                eng.wait_ge(probe_ok, 16 * b + u + 1)
                if u == 0:
                    at_least(eng, nmT_ok, b - 1)
                nc.vector.tensor_reduce(nmax[:, p, u % 2, u // 2:u // 2 + 1], probe[u % 2][:, 0:NKV], AX.X,
                                        ALU.max, negate=True).then_inc(nmax_ok, 1)

            def prob_higher(b, h):
                eng.wait_ge(exp_ok, 2 * (H0 * b + h) + 2)
                at_least(eng, ctxv_ok, H0 * b + h - 1)
                nc.vector.tensor_copy(prob2[:, h % 2, 0], prob[:, h % 2]).then_inc(prob_high, 1)

            def divide(b, h):
                mine, sums = (slice(0, 64), slice(64, 128)) if h % 2 == 0 else (slice(64, 128), slice(0, 64))
                eng.wait_ge(ctxv_ok, H0 * b + h + 1)
                nc.vector.reciprocal(rden[mine], ctxv[sums, 0:S]).then_inc(rden_ok, 1)
                eng.wait_ge(rden_ok, H0 * b + h + 1)
                at_least(eng, att_low, KI * (b - 1) + h // 2 + 1)
                nc.vector.tensor_tensor(att[mine, h // 2], ctxv[mine, 0:S], rden[mine], ALU.mult) \
                    .then_inc(att_ok, 1)

            def out_stat(b):
                eng.wait_ge(out_ok, b + 1)
                for k in range(QT):
                    nc.vector.bn_stats(stats1[:, k], misc[:, k * D:(k + 1) * D]).then_inc(stats1_ok, 1)
                for k in range(QT):
                    eng.wait_ge(stats1_ok, QT * b + k + 1)
                    by_itself(eng, waited)
                    nc.vector.bn_aggr(mv1[:, k], stats1[:, k]).then_inc(mv1_ok, 1)

            def out_norm(b, p):
                eng.wait_ge(rs1_ok, b + 1)
                for k in range(QT):
                    nc.vector.scalar_tensor_tensor(y1[:, k], misc[:, k * D:(k + 1) * D], mv1[:, k, 0:1], go[:],
                                                   ALU.subtract, ALU.mult).then_inc(y1_ok, 1)
                eng.wait_ge(xb_ok, b + 1)
                at_least(eng, x1_out[p], 16 * (b // 2))
                for k in range(QT):
                    eng.wait_ge(y1_ok, QT * b + k + 1)
                    nc.vector.scalar_tensor_tensor(x1[:, p, k], y1[:, k], rs1[:, k:k + 1], xb[:, k],
                                                   ALU.mult, ALU.add).then_inc(x1_ok, 1)

            def x1_stat(b, p):
                for k in range(QT):
                    eng.wait_ge(x1_ok, QT * b + k + 1)
                    nc.vector.bn_stats(stats2[:, k], x1[:, p, k]).then_inc(stats2_ok, 1)
                for k in range(QT):
                    eng.wait_ge(stats2_ok, QT * b + k + 1)
                    by_itself(eng, waited)
                    nc.vector.bn_aggr(mv2[:, k], stats2[:, k]).then_inc(mv2_ok, 1)

            def x1_norm(b, p):
                eng.wait_ge(rs2_ok, b + 1)
                at_least(eng, sent, 16 * 2 * QT * b)
                for k in range(QT):
                    nc.vector.tensor_scalar(x2h[:, k], x1[:, p, k], mv2[:, k, 0:1], rs2[:, k:k + 1],
                                            ALU.subtract, ALU.mult).then_inc(x2h_ok, 1)

            def choose(b):
                step = 0

                def then(instruction):
                    nonlocal step
                    step += 1
                    instruction.then_inc(soft, 1)
                    eng.wait_ge(soft, N_SOFT * b + step)

                eng.wait_ge(logit_ok, b + 1)
                then(nc.vector.tensor_tensor(lg[:], misc[:, 0:QT * E0].rearrange("p (t e) -> p t e", t=QT),
                                             br[:].unsqueeze(1).to_broadcast([P, QT, E0]), ALU.add))
                then(nc.vector.tensor_reduce(lmax[:], lg[:], AX.X, ALU.max))
                then(nc.vector.tensor_tensor(lg[:], lg[:], lmax[:].unsqueeze(2).to_broadcast([P, QT, E0]),
                                             ALU.subtract))
                eng.wait_ge(le_ok, b + 1)
                then(nc.vector.reduce_sum(lsum[:], le[:], AX.X))
                then(nc.vector.reciprocal(lsum[:], lsum[:]))
                then(nc.vector.tensor_tensor(pr[:], le[:], lsum[:].unsqueeze(2).to_broadcast([P, QT, E0]), ALU.mult))
                for k in range(QT):
                    by_itself(eng, waited)
                    then(nc.vector.max(top[:, k], pr[:, k]))
                for k in range(QT):
                    by_itself(eng, waited)
                    then(nc.vector.max_index(topi[:, k], top[:, k], pr[:, k]))
                then(nc.vector.tensor_copy(topf[:], topi[:, :, 0:2]))
                for k in range(QT):
                    then(nc.vector.tensor_tensor(oh[:, k], iota_e[:].unsqueeze(1).to_broadcast([P, 2, E0]),
                                                 topf[:, k].unsqueeze(2).to_broadcast([P, 2, E0]), ALU.is_equal))
                then(nc.vector.tensor_tensor(ohs[:], oh[:, :, 0], oh[:, :, 1], ALU.add))
                assert step == N_SOFT

            def place(b):
                step = 0

                def then(instruction):
                    nonlocal step
                    step += 1
                    instruction.then_inc(route, 1)
                    eng.wait_ge(route, N_ROUTE * b + step)

                at_least(eng, sent, 16 * 2 * QT * b)
                eng.wait_ge(count_ok, b + 1)
                counts = misc[:, 0:QT * E0].rearrange("p (t e) -> p t e", t=QT)
                eng.wait_ge(soft, N_SOFT * (b + 1))
                then(nc.vector.tensor_tensor(at_e[:], oh[:], counts.unsqueeze(2).to_broadcast([P, QT, 2, E0]),
                                             ALU.mult))
                then(nc.vector.reduce_sum(pos[:], at_e[:], AX.X))
                first_row = slot0[:, bass.ds(b, 1)].rearrange("p o e -> p (o e)")
                then(nc.vector.tensor_tensor(at_b[:].rearrange("p t k e -> p (t k) e"),
                                             oh[:].rearrange("p t k e -> p (t k) e"),
                                             first_row.unsqueeze(1).to_broadcast([P, QT * 2, E0]), ALU.mult))
                then(nc.vector.reduce_sum(base[:], at_b[:], AX.X))
                then(nc.vector.tensor_scalar(kept[:], pos[:], float(CAP), None, ALU.is_lt))
                then(nc.vector.tensor_tensor(wsel[:], top[:, :, 0:2], kept[:], ALU.mult))
                then(nc.vector.tensor_scalar(keep["weight"][:, bass.ds(b, 1)].rearrange("p o n -> p (o n)"),
                                             wsel[:].rearrange("p t k -> p (t k)"), tgate[:, 2:3], None, ALU.mult))
                then(nc.vector.scalar_tensor_tensor(slot[:], pos[:], float(CAP - 1), base[:], ALU.min, ALU.add))
                then(nc.vector.tensor_copy(keep["row"][:, bass.ds(b, 1)].rearrange("p o n -> p (o n)"),
                                           slot[:].rearrange("p t k -> p (t k)")))
                then(nc.vector.tensor_scalar(slot_s[:], kept[:], -float(NOWHERE), float(NOWHERE), ALU.mult, ALU.add))
                then(nc.vector.tensor_tensor(sidx[:], slot[:].rearrange("p t k -> p (t k)"),
                                             slot_s[:].rearrange("p t k -> p (t k)"), ALU.add))
                assert step == N_ROUTE

            stat(0, 0)
            normalise(0, 0)
            for n, (both, whole) in enumerate(((wq, stage_q), (wkv, stage_kv[:]), (wo, stage_o))):
                eng.wait_ge(w_high, n + 1)
                nc.vector.tensor_tensor(both[:, 1], whole, both[:, 0].bitcast(F32), ALU.subtract) \
                    .then_inc(w_low, 1)
            kvin_higher(0)
            mask_line(0, 0)
            for u in range(9):
                lower(0, 0, u)
            for u in range(16):
                row_max(0, 0, u)

            def step(b, p):
                first, last = isinstance(b, int) and b == 0, isinstance(b, int) and b == B - 1
                n, q, r = b + 1, 1 - p, b - 1
                if not last:
                    stat(n, q)
                prob_higher(b, 0)
                if not last:
                    normalise(n, q)
                if not first:
                    out_stat(r)
                prob_higher(b, 1)
                if not first:
                    out_norm(r, q)
                    x1_stat(r, q)
                if not last:
                    kvin_higher(n)
                    mask_line(n, q)
                divide(b, 0)
                if not first:
                    x1_norm(r, q)
                prob_higher(b, 2)
                if not last:
                    lower(n, q, 0)
                    lower(n, q, 1)
                divide(b, 1)
                prob_higher(b, 3)
                if not last:
                    lower(n, q, 2)
                    lower(n, q, 3)
                divide(b, 2)
                for h in range(4, H0):
                    u = 4 * (h - 4)
                    prob_higher(b, h)
                    if not last:
                        row_max(n, q, u)
                        if h == 4:
                            lower(n, q, 4)
                            lower(n, q, 5)
                        else:
                            lower(n, q, h + 1)
                        row_max(n, q, u + 1)
                    divide(b, h - 1)
                    if not last:
                        row_max(n, q, u + 2)
                        row_max(n, q, u + 3)
                    if not first:
                        if h == 4:
                            choose(r)
                        if h == 5:
                            place(r)
                divide(b, H0 - 1)

            batches(eng, step)
            out_stat(B - 1)
            out_norm(B - 1, 1)
            x1_stat(B - 1, 1)
            x1_norm(B - 1, 1)
            choose(B - 1)
            place(B - 1)

        @block.tensor
        def _(eng):
            def turn(b):
                eng.wait_ge(xh_ok, 3 * (b + 1))
                at_least(eng, proj_low, 9 * b)
                for k in range(KD):
                    for i in range(QT):
                        last = nc.tensor.transpose(proj[0][:, k * S + i * P:k * S + (i + 1) * P],
                                                   xh[:, i, k * P:(k + 1) * P], ident[:])
                last.then_inc(xT_ok, 1)
                for k in range(KD):
                    last = nc.tensor.transpose(proj[1][:, k * C:(k + 1) * C],
                                               xh[0:C, 2, k * P:(k + 1) * P], ident[0:C, 0:C])
                last.then_inc(xT_ok, 1)

            def project(b, u):
                if u == 0:
                    eng.wait_ge(kvin_low, b + 1)
                    eng.wait_ge(kvin_ok, 4 * (b + 1))
                if u >= 2:
                    eng.wait_ge(proj_low, 9 * b + u - 1)
                out = proj[u % 2]
                if u < 2:
                    for m in range(2):
                        cols = slice((2 * u + m) * P, (2 * u + m + 1) * P)
                        last = split_product(nc, out[:, m * S:(m + 1) * S], lambda a, k: wq[:, a, k, cols],
                                             lambda a, k: kvin2[:, a, k, C:NKV], KD)
                elif u < 6:
                    cols = slice((u - 2) * P, (u - 1) * P)
                    last = split_product(nc, out[:, 0:NKV], lambda a, k: wkv[:, a, k, cols],
                                         lambda a, k: kvin2[:, a, k, :], KD)
                else:
                    lo, hi = ((0, C), (C, C + P), (C + P, NKV))[u - 6]
                    last = split_product(nc, out[0:hi - lo, :], lambda a, k: kvin2[:, a, k, lo:hi],
                                         lambda a, k: wkv[:, a, k, INNER:], KD)
                last.then_inc(proj_ok, 1)

            def probe_max(b, p, u):
                h, i = u // 2, u % 2
                rows = slice(64 * (h % 2), 64 * (h % 2) + 64)
                if i == 0:
                    eng.wait_ge(proj_high, 9 * b + 3 + h // 2)
                if u == 0:
                    eng.wait_ge(mrow_ok, b + 1)
                at_least(eng, nmax_ok, 16 * b + u - 1)
                nc.tensor.matmul(probe[i][:, 0:NKV], qT[rows, p, 0, h // 2, i * P:(i + 1) * P],
                                 kT[rows, p, 0, h // 2, :], start=True, stop=False)
                nc.tensor.matmul(probe[i][:, 0:C], firstrow[rows], mask_row[rows, p], start=False, stop=True) \
                    .then_inc(probe_ok, 1)

            def turn_max(b, p):
                eng.wait_ge(nmax_ok, 16 * (b + 1))
                at_least(eng, route, N_ROUTE * (b - 1))
                for i in range(QT):
                    last = nc.tensor.transpose(misc[0:H0, i * P:(i + 1) * P], nmax[:, p, i], ident[:])
                last.then_inc(nmT_ok, 1)

            def score(b, p, h):
                rows = slice(64 * (h % 2), 64 * (h % 2) + 64)
                if h == 0:
                    eng.wait_ge(nmT_out, 2 * (b + 1))
                    eng.wait_ge(proj_low, 9 * b + 6)
                for i, lo, hi in ((0, C, C + P), (1, C + P, NKV), (2, 0, C)):
                    out = score_x[:, i] if i < 2 else score_c[0:C, 0:S]
                    if i != 1:
                        at_least(eng, exp_ok, 2 * (H0 * b + h) - (1 if i == 0 else 0))
                    nc.tensor.matmul(out, headrow[rows, h, 0:hi - lo], nmaxT[rows, p], start=True, stop=False)
                    last = split_product(nc, out, lambda a, _: kT[rows, p, a, h // 2, lo:hi],
                                         lambda a, _: qT[rows, p, a, h // 2, :], 1, start=False)
                    if i >= 1:
                        last.then_inc(score_ok, 1)

            def times_v(b, p, h):
                eng.wait_ge(prob_low, H0 * b + h + 1)
                at_least(eng, att_ok, H0 * b + h)
                if h == 0:
                    eng.wait_ge(proj_low, 9 * (b + 1))
                first = 64 * (h % 2)

                def v_and_ones(a, i):
                    rows = P if i < 2 else C
                    return vo[0:rows, p, a, i, h // 2].rearrange("p c d -> p (c d)")[:, first:first + P]

                split_product(nc, ctxv[:, 0:S], v_and_ones,
                              lambda a, i: prob2[0:P if i < 2 else C, h % 2, a, i], 3).then_inc(ctxv_ok, 1)

            def output(b):
                eng.wait_ge(att_low, KI * (b + 1))
                eng.wait_ge(nmT_out, 2 * min_batches(b + 2))
                at_least(eng, route, N_ROUTE * b)
                for i in range(QT):
                    last = split_product(nc, misc[:, i * D:(i + 1) * D],
                                         lambda a, k: att2[:, a, k, i * P:(i + 1) * P],
                                         lambda a, k: wo[:, a, k], KI)
                last.then_inc(out_ok, 1)

            def min_batches(n):
                return min(n, B) if isinstance(n, int) else n

            def router_turn(b):
                eng.wait_ge(x2h_ok, QT * (b + 1))
                eng.wait_ge(y1_ok, QT * (b + 1))
                for k in range(KD):
                    for i in range(QT):
                        last = nc.tensor.transpose(misc[:, k * S + i * P:k * S + (i + 1) * P],
                                                   x2h[:, i, k * P:(k + 1) * P], ident[:])
                last.then_inc(rT_ok, 1)

            def router_logits(b):
                eng.wait_ge(rT_out, b + 1)
                for i in range(QT):
                    for k in range(KD):
                        last = nc.tensor.matmul(misc[:, i * E0:(i + 1) * E0], rT[:, k, i * P:(i + 1) * P],
                                                wr[:, k], start=k == 0, stop=k == KD - 1)
                last.then_inc(logit_ok, 1)

            def router_count(b):
                eng.wait_ge(soft, N_SOFT * (b + 1))
                for i in range(QT):
                    for k in range(i + 1):
                        last = nc.tensor.matmul(misc[:, i * E0:(i + 1) * E0], tri[:, 0 if k == i else 1],
                                                ohs[:, k], start=k == 0, stop=k == i)
                last.then_inc(count_ok, 1)

            eng.wait_ge(small_in, 16 * N_SMALL)
            eng.wait_ge(const_ok, N_CONST)
            turn(0)
            eng.wait_ge(w_low, N_W)
            for u in range(9):
                project(0, u)
            for u in range(16):
                probe_max(0, 0, u)
            turn_max(0, 0)

            def step(b, p):
                first, last = isinstance(b, int) and b == 0, isinstance(b, int) and b == B - 1
                n, q, r = b + 1, 1 - p, b - 1
                score(b, p, 0)
                if not first:
                    output(r)
                score(b, p, 1)
                if not last:
                    turn(n)
                times_v(b, p, 0)
                score(b, p, 2)
                if not last:
                    project(n, 0)
                    project(n, 1)
                times_v(b, p, 1)
                score(b, p, 3)
                if not last:
                    project(n, 2)
                if not first:
                    router_turn(r)
                if not last:
                    project(n, 3)
                times_v(b, p, 2)
                for h in range(4, H0):
                    u = 4 * (h - 4)
                    score(b, p, h)
                    if not last:
                        probe_max(n, q, u)
                        project(n, h if h == 4 else h + 1)
                        if h == 4:
                            project(n, 5)
                        probe_max(n, q, u + 1)
                    if not first and h == 4:
                        router_logits(r)
                    times_v(b, p, h - 1)
                    if not last:
                        probe_max(n, q, u + 2)
                    if not first and h == 5:
                        router_count(r)
                    if not last:
                        probe_max(n, q, u + 3)
                times_v(b, p, H0 - 1)
                if not last:
                    turn_max(n, q)

            batches(eng, step)
            output(B - 1)
            router_turn(B - 1)
            router_logits(B - 1)
            router_count(B - 1)


N_SMALL = 18
N_CONST = 8
N_W = 4


CH = 2 * P
NC = SLOTS // CH


def experts(nc, t):
    ctx = ExitStack()
    with ctx:
        def sb(name, shape, dt=F32):
            return ctx.enter_context(nc.sbuf_tensor(name, shape, dt))

        def pb(name, shape):
            return ctx.enter_context(nc.psum_tensor(name, shape, F32))

        sems = []

        def sem(name):
            sems.append(ctx.enter_context(nc.semaphore(name)))
            return sems[-1]

        w1_in = sb("e_w1_in", [P, KD, HID])
        w2_in = sb("e_w2_in", [P, KH, D])
        w1 = sb("e_w1", [P, 2, 2, KD, HID], F32R)
        w2 = sb("e_w2", [P, 2, 2, KH, D], F32R)
        b1 = sb("e_b1", [P, KH, E0])
        b2 = sb("e_b2", [P, E0, D])
        ident = sb("e_ident", [P, P])
        rows = sb("e_rows", [P, 2, 2, D])
        rowsT = sb("e_rowsT", [P, 2, 2, KD, CH], F32R)
        hidden = sb("e_hidden", [P, KH, CH])
        hidden2 = sb("e_hidden2", [P, 2, 2, KH, CH], F32R)
        y = sb("e_y", [P, 2, 2, D])

        turned = pb("e_turned", [P, KD * CH])
        first = pb("e_first", [P, 4, 512])
        second = [pb(f"e_second{i}", [P, 2, D]) for i in range(2)]

        small_in = sem("e_small_in")
        w_in = sem("e_w_in")
        waited = sem("e_waited")
        w_high, w_low = sem("e_w_high"), sem("e_w_low")
        rows_in = [sem(f"e_rows_in{i}") for i in range(2)]
        turned_ok, rows_high, rows_low = sem("e_turned_ok"), sem("e_rows_high"), sem("e_rows_low")
        first_ok, relu_ok, hid_high, hid_low = (sem("e_" + s) for s in
                                                ("first_ok", "relu_ok", "hid_high", "hid_low"))
        second_ok, y_ok = sem("e_second_ok"), sem("e_y_ok")
        y_out = [sem(f"e_y_out{i}") for i in range(2)]
        PIECES = 4

        def piece(p, n, plane):
            if n < 2:
                return w1_in[:, n], w1[:, p, plane, n]
            half = slice((n - 2) * KH // 2, (n - 1) * KH // 2)
            return w2_in[:, half], w2[:, p, plane, half]

        def rounds(eng, step):
            def pair(e0, last):
                for p in range(2):
                    for c in range(NC):
                        step((e0 + p) * NC + c, e0 + p, p, c, (p * NC + c) % 2,
                             NC * (1 - p) + NC - 1 - c if last else NC)
            pair(0, False)
            with eng.Fori(1, E0 // 2 - 1) as n:
                pair(n * 2, False)
            pair(E0 - 2, True)

        ctx.callback(zero_semaphores, nc, sems)
        block = ctx.enter_context(nc.Block())

        @block.sync
        def _(eng):
            def load_weights(e):
                at_least(eng, w_low, PIECES * e)
                eng.dma_start(w1_in[:], t["W1"][bass.ds(e, 1)].rearrange("o (k p) h -> p (o k) h", p=P)) \
                    .then_inc(w_in, 16)
                eng.dma_start(w2_in[:], t["W2"][bass.ds(e, 1)].rearrange("o (k p) d -> p (o k) d", p=P)) \
                    .then_inc(w_in, 16)

            def load_rows(g, q):
                at_least(eng, turned_ok, g - 1)
                eng.dma_start(rows[:, q], t["slots"][bass.ts(g, CH)].rearrange("(k p) d -> p k d", p=P)) \
                    .then_inc(rows_in[q], 16)

            load_rows(0, 0)
            load_weights(0)
            load_rows(1, 1)
            for dst, src in ((ident[:], t["ident"]), (b1[:], t["b1"]), (b2[:], t["b2"].partition_broadcast(P))):
                eng.dma_start(dst, src).then_inc(small_in, 16)
            load_weights(1)

            def step(g, e, p, c, q, left):
                if left >= 2:
                    load_rows(g + 2, q)
                eng.wait_ge(y_ok, g + 1)
                eng.dma_start(t["answers"][bass.ts(g, CH)].rearrange("(k p) d -> p k d", p=P), y[:, q]) \
                    .then_inc(y_out[q], 16)
                if c == NC - 1 and not (isinstance(e, int) and e + 2 >= E0):
                    load_weights(e + 2)

            rounds(eng, step)
            for q in range(2):
                eng.wait_ge(y_out[q], 16 * (E0 * NC // 2))

        @block.scalar
        def _(eng):
            def split(e, p, n):
                if n == 0:
                    eng.wait_ge(w_in, 32 * (e + 1))
                    at_least(eng, second_ok, NC * (e - 1))
                src, dst = piece(p, n, 0)
                nc.scalar.activation(dst, src, ACT.Copy).then_inc(w_high, 1)

            def rows_higher(g, q):
                eng.wait_ge(turned_ok, g + 1)
                at_least(eng, first_ok, 4 * (g - 1))
                nc.scalar.activation(rowsT[:, q, 0], turned[:], ACT.Copy).then_inc(rows_high, 1)

            def relu(g, e, j):
                eng.wait_ge(first_ok, 4 * g + j + 1)
                at_least(eng, hid_low, 4 * (g - 1) + j + 1)
                by_itself(eng, waited)
                for i in range(2):
                    nc.scalar.activation(hidden[:, 2 * j + i], first[:, j, i * CH:(i + 1) * CH], ACT.Relu,
                                         bias=b1[:, 2 * j + i, bass.ds(e, 1)]).then_inc(relu_ok, 1)

            for n in range(PIECES):
                split(0, 0, n)
            eng.wait_ge(small_in, 48)
            rows_higher(0, 0)
            rows_higher(1, 1)
            for j in range(4):
                relu(0, 0, j)

            def step(g, e, p, c, q, left):
                if left >= 1:
                    for j in range(4):
                        relu(g + 1, e if c < NC - 1 else e + 1, j)
                if left >= 2:
                    rows_higher(g + 2, q)
                if c < PIECES and left >= NC:
                    split(e + 1, 1 - p, c)

            rounds(eng, step)

        @block.vector
        def _(eng):
            def split(e, p, n):
                eng.wait_ge(w_high, PIECES * e + n + 1)
                src, dst = piece(p, n, 1)
                nc.vector.tensor_tensor(dst, src, piece(p, n, 0)[1].bitcast(F32), ALU.subtract).then_inc(w_low, 1)

            def rows_lower(g, q):
                eng.wait_ge(rows_high, g + 1)
                nc.vector.tensor_tensor(rowsT[:, q, 1], turned[:].rearrange("p (k s) -> p k s", k=KD),
                                        rowsT[:, q, 0].bitcast(F32), ALU.subtract).then_inc(rows_low, 1)

            def hidden_split(g, q, j):
                eng.wait_ge(relu_ok, 8 * g + 2 * j + 2)
                at_least(eng, second_ok, g - 1)
                mine = slice(2 * j, 2 * j + 2)
                nc.vector.tensor_copy(hidden2[:, q, 0, mine], hidden[:, mine]).then_inc(hid_high, 1)
                eng.wait_ge(hid_high, 4 * g + j + 1)
                nc.vector.tensor_tensor(hidden2[:, q, 1, mine], hidden[:, mine],
                                        hidden2[:, q, 0, mine].bitcast(F32), ALU.subtract).then_inc(hid_low, 1)

            def answer(g, e, q):
                eng.wait_ge(second_ok, g + 1)
                at_least(eng, y_out[q], 16 * (g // 2))
                nc.vector.tensor_tensor(y[:, q], second[q][:], b2[:, bass.ds(e, 1)].to_broadcast([P, 2, D]),
                                        ALU.add).then_inc(y_ok, 1)

            for n in range(PIECES):
                split(0, 0, n)
            eng.wait_ge(small_in, 48)
            rows_lower(0, 0)
            rows_lower(1, 1)
            for j in range(4):
                hidden_split(0, 0, j)

            def step(g, e, p, c, q, left):
                if left >= 1:
                    for j in range(4):
                        hidden_split(g + 1, 1 - q, j)
                if left >= 2:
                    rows_lower(g + 2, q)
                if c < PIECES and left >= NC:
                    split(e + 1, 1 - p, c)
                answer(g, e, q)

            rounds(eng, step)

        @block.tensor
        def _(eng):
            def turn(g, q):
                eng.wait_ge(rows_in[q], 16 * (g // 2 + 1))
                at_least(eng, rows_low, g)
                for k in range(KD):
                    for i in range(2):
                        last = nc.tensor.transpose(turned[:, k * CH + i * P:k * CH + (i + 1) * P],
                                                   rows[:, q, i, k * P:(k + 1) * P], ident[:])
                last.then_inc(turned_ok, 1)

            def product1(g, e, p, q):
                eng.wait_ge(w_low, PIECES * (e + 1))
                eng.wait_ge(rows_low, g + 1)
                for j in range(4):
                    at_least(eng, relu_ok, 8 * (g - 1) + 2 * j + 2)
                    for i in range(2):
                        cols = slice((2 * j + i) * P, (2 * j + i + 1) * P)
                        last = split_product(nc, first[:, j, i * CH:(i + 1) * CH],
                                             lambda a, k: w1[:, p, a, k, cols],
                                             lambda a, k: rowsT[:, q, a, k], KD)
                    last.then_inc(first_ok, 1)

            def product2(g, p, q):
                eng.wait_ge(hid_low, 4 * (g + 1))
                at_least(eng, y_ok, g - 1)
                for i in range(2):
                    last = split_product(nc, second[q][:, i],
                                         lambda a, k: hidden2[:, q, a, k, i * P:(i + 1) * P],
                                         lambda a, k: w2[:, p, a, k], KH)
                last.then_inc(second_ok, 1)

            eng.wait_ge(small_in, 48)
            turn(0, 0)
            turn(1, 1)
            product1(0, 0, 0, 0)

            def step(g, e, p, c, q, left):
                if left >= 1:
                    if c < NC - 1:
                        product1(g + 1, e, p, 1 - q)
                    else:
                        product1(g + 1, e + 1, 1 - p, 1 - q)
                if left >= 2:
                    turn(g + 2, q)
                product2(g, p, q)

            rounds(eng, step)


def finish(nc, t, keep):
    ctx = ExitStack()
    with ctx:
        def sb(name, shape, dt=F32):
            return ctx.enter_context(nc.sbuf_tensor(name, shape, dt))

        def pb(name, shape):
            return ctx.enter_context(nc.psum_tensor(name, shape, F32))

        sems = []

        def sem(name):
            sems.append(ctx.enter_context(nc.semaphore(name)))
            return sems[-1]

        parts = (("WqT", KD * D), ("WkT", KD * D), ("WvT", KD * D), ("WoT", KD * D),
                 ("Wg", EM * KD * P), ("Wu", EM * KD * P), ("Wd", EM * D), ("Wr1", KD * E1))
        at, total = {}, 0
        for name, size in parts:
            at[name] = total
            total += size
        w_in = sb("f_w_in", [P, total])
        w = sb("f_w", [P, 2, total], F32R)
        ident = sb("f_ident", [P, P])
        iota_e = sb("f_iota_e", [P, E1])
        heads = sb("f_heads", [P, P])
        bq = sb("f_bq", [P, KD])
        bk = sb("f_bk", [P, KD])
        bv = sb("f_bv", [P, D])
        bo = sb("f_bo", [P, D])
        rbias = sb("f_rbias", [P, E1])
        conv_w = sb("f_conv_w", [P, KD, KC])
        conv_b = sb("f_conv_b", [P, KD])
        minus_half = sb("f_minus_half", [P, 2])

        x1 = sb("f_x1", [P, 2, QT, D])
        picked = [sb(f"f_picked{i}", [P, QT * 2, D]) for i in range(2)]
        row = [sb(f"f_row{i}", [P, QT * 2], U32) for i in range(2)]
        cin = sb("f_cin", [P, 2, D])
        xa = sb("f_xa", [P, QT, D])
        x2 = sb("f_x2", [P, 2, QT, D])
        stats3 = sb("f_stats3", [P, QT, 6])
        mv3 = sb("f_mv3", [P, QT, 2])
        var3 = sb("f_var3", [P, QT])
        rs3 = sb("f_rs3", [P, QT])
        x3h = sb("f_x3h", [P, QT, D])
        xT = sb("f_xT", [P, 2, KD, S], F32R)
        cT = sb("f_cT", [P, 2, KD, C], F32R)
        qT = sb("f_qT", [P, 2, KD, S], F32R)
        kf = sb("f_kf", [P, KD, C])
        kmax = sb("f_kmax", [P, KD])
        ke = sb("f_ke", [P, KD, C])
        ksum = sb("f_ksum", [P, KD])
        kn = sb("f_kn", [P, KD, C])
        kp = sb("f_kp", [C, 2, D], F32R)
        vf = sb("f_vf", [C, D])
        v = sb("f_v", [C, 2, D], F32R)
        cf = sb("f_cf", [P, KD, P])
        cx = sb("f_cx", [P, 2, KD, P], F32R)
        aT = sb("f_aT", [P, 2, KD, S], F32R)
        xb = sb("f_xb", [P, QT, D])
        x3 = sb("f_x3", [P, 2, QT, D])
        stats4 = sb("f_stats4", [P, QT, 6])
        mv4 = sb("f_mv4", [P, QT, 2])
        var4 = sb("f_var4", [P, QT])
        rs4 = sb("f_rs4", [P, QT])
        x4h = sb("f_x4h", [P, QT, D])
        x4r = sb("f_x4r", [P, QT, D])
        x4p = sb("f_x4p", [P, KD, KC - 1 + S])
        x4T = sb("f_x4T", [P, 2, KD, S], F32R)
        cv = sb("f_cv", [P, KD, S])
        cvr = sb("f_cvr", [P, QT, D])
        re = sb("f_re", [P, QT, E1])
        rsg = sb("f_rsg", [P, QT, E1])
        sel = sb("f_sel", [P, QT, E1])
        top = sb("f_top", [P, QT, E1])
        topi = sb("f_topi", [P, QT, E1], U32)
        topf = sb("f_topf", [P, QT, 2])
        oh = sb("f_oh", [P, QT, 2, E1])
        cw = sb("f_cw", [P, QT, E1])
        cws = sb("f_cws", [P, QT])
        th = sb("f_th", [P, EM, S])
        hs = sb("f_hs", [P, EM, S])
        hid = sb("f_hid", [P, EM, S])
        hid2 = sb("f_hid2", [P, 2, EM, S], F32R)
        acc = sb("f_acc", [P, QT, D])
        yo = sb("f_yo", [P, 2, QT, D])

        mlp = pb("f_mlp", [P, EM, 512])
        bank_x = pb("f_bank_x", [P, 512])
        bank_c = pb("f_bank_c", [P, 512])
        bank_v = pb("f_bank_v", [P, 512])
        bank_t = pb("f_bank_t", [P, 512])

        small_in, weights_in, w_high, w_low, const_g, bo_ok = (sem("f_" + s) for s in (
            "small_in", "weights_in", "w_high", "w_low", "const_g", "bo_ok"))
        x1_in = [sem(f"f_x1_in{i}") for i in range(2)]
        cin_in = [sem(f"f_cin_in{i}") for i in range(2)]
        picked_in = keep["picked_in"]
        row_ok = sem("f_row_ok")
        waited = sem("f_waited")
        xa_ok, x2_ok, stats3_ok, mv3_ok, var3_ok, rs3_ok, x3h_ok = (sem("f_" + s) for s in (
            "xa_ok", "x2_ok", "stats3_ok", "mv3_ok", "var3_ok", "rs3_ok", "x3h_ok"))
        x3T_ok, cT_ok, xT_high, xT_low, cT_high, cT_low = (sem("f_" + s) for s in (
            "x3T_ok", "cT_ok", "xT_high", "xT_low", "cT_high", "cT_low"))
        q_ok, q_high, q_low, k_ok, kf_ok, kmax_ok, ke_ok, kr_ok, kn_ok, kT_ok, kp_high, kp_low = (
            sem("f_" + s) for s in ("q_ok", "q_high", "q_low", "k_ok", "kf_ok", "kmax_ok", "ke_ok", "kr_ok",
                                    "kn_ok", "kT_ok", "kp_high", "kp_low"))
        v_ok, vf_ok, v_high, v_low, cx_ok, cf_ok, cx_high, cx_low, a_ok, a_high, a_low = (
            sem("f_" + s) for s in ("v_ok", "vf_ok", "v_high", "v_low", "cx_ok", "cf_ok", "cx_high", "cx_low",
                                    "a_ok", "a_high", "a_low"))
        out_ok, xb_ok, x3_ok, stats4_ok, mv4_ok, var4_ok, rs4_ok, x4h_ok, x4r_ok = (
            sem("f_" + s) for s in ("out_ok", "xb_ok", "x3_ok", "stats4_ok", "mv4_ok", "var4_ok", "rs4_ok",
                                    "x4h_ok", "x4r_ok"))
        x4T_ok, x4p_ok, x4T_high, x4T_low, logit_ok, re_ok, route = (
            sem("f_" + s) for s in ("x4T_ok", "x4p_ok", "x4T_high", "x4T_low", "logit_ok", "re_ok", "route"))
        cv_ok, cvT_ok, cvr_ok, gu_ok, th_ok, hs_ok, hid_ok, hid_high, hid_low, down_ok, acc_ok, yo_ok = (
            sem("f_" + s) for s in ("cv_ok", "cvT_ok", "cvr_ok", "gu_ok", "th_ok", "hs_ok", "hid_ok",
                                    "hid_high", "hid_low", "down_ok", "acc_ok", "yo_ok"))
        yo_out = [sem(f"f_yo_out{i}") for i in range(2)]
        N_ROUTE = 17
        N_CV = 2 * KC
        N_ACC = QT * (EM + 2)
        N_SMALL_F = 10

        def weight(name, plane, *index):
            base = at[name]
            if name in ("WqT", "WkT"):
                k, m = index
                return w[:, plane, base + k * D + m * P:base + k * D + (m + 1) * P]
            if name in ("WvT", "WoT"):
                return w[:, plane, base + index[0] * D:base + (index[0] + 1) * D]
            if name in ("Wg", "Wu"):
                e, k = index
                return w[:, plane, base + (e * KD + k) * P:base + (e * KD + k + 1) * P]
            if name == "Wd":
                return w[:, plane, base + index[0] * D:base + (index[0] + 1) * D]
            return w[:, plane, base + index[0] * E1:base + (index[0] + 1) * E1]

        def bounds(b):
            return not isinstance(b, int) or b + 1 < B, not isinstance(b, int) or b + 2 < B

        ctx.callback(zero_semaphores, nc, sems)
        block = ctx.enter_context(nc.Block())

        @block.sync
        def _(eng):
            def load(b, p):
                at_least(eng, xa_ok, QT * (b - 1))
                eng.dma_start(x1[:, p], t["x1"][bass.ds(b, 1)].rearrange("o (k p) d -> p (o k) d", p=P)) \
                    .then_inc(x1_in[p], 16)
                at_least(eng, cT_ok, b - 1)
                eng.dma_start(cin[0:C, p], t["ctx"][bass.ds(b, 1)].rearrange("o c d -> c (o d)")) \
                    .then_inc(cin_in[p], 16)

            load(0, 0)
            small = [(ident[:], t["ident"]), (iota_e[:], t["iota_e"]), (heads[:], t["heads1"]),
                     (bq[:], t["bq"]), (bk[:], t["bk"]), (bv[:], t["bv"].partition_broadcast(P)),
                     (bo[:], t["bo1"].partition_broadcast(P)), (rbias[:], t["rbias"].partition_broadcast(P)),
                     (conv_w[:].unsqueeze(2), t["conv_w"]), (conv_b[:], t["conv_b"])]
            assert len(small) == N_SMALL_F
            for dst, src in small:
                eng.dma_start(dst, src).then_inc(small_in, 16)
            for name, size in parts:
                dst = w_in[:, at[name]:at[name] + size]
                if name in ("Wg", "Wu"):
                    src = t[name].rearrange("e (k p) i -> p (e k) i", p=P)
                    dst = dst.rearrange("p (n i) -> p n i", i=P)
                elif name == "Wd":
                    src, dst = t[name].rearrange("e p d -> p e d"), dst.rearrange("p (e d) -> p e d", e=EM)
                else:
                    src = t[name].rearrange("(k p) d -> p k d", p=P)
                    dst = dst.rearrange("p (k d) -> p k d", k=KD)
                eng.dma_start(dst, src).then_inc(weights_in, 16)
            load(1, 1)

            def step(b, p):
                if bounds(b)[1]:
                    load(b + 2, p)
                eng.wait_ge(yo_ok, b + 1)
                eng.dma_start(t["out"][bass.ds(b, 1)].rearrange("o (k p) d -> p (o k) d", p=P), yo[:, p]) \
                    .then_inc(yo_out[p], 16)

            batches(eng, step)
            for p in range(2):
                eng.wait_ge(yo_out[p], 16 * (B // 2))

        @block.gpsimd
        def _(eng):
            nc.gpsimd.memset(minus_half[:], -0.5).then_inc(const_g, 1)
            nc.gpsimd.memset(x4p[:, :, 0:KC - 1], 0.0).then_inc(const_g, 1)
            eng.wait_ge(const_g, 2)

            def gather(b, p):
                at_least(eng, x2_ok, QT * (b - 1))
                nc.gpsimd.tensor_copy(row[p][:], keep["row"][:, bass.ds(b, 1)].rearrange("p o n -> p (o n)")) \
                    .then_inc(row_ok, 1)
                eng.wait_ge(row_ok, b + 1)
                by_itself(eng, waited)
                for n in range(QT * 2):
                    nc.gpsimd.indirect_dma_start(
                        out=picked[p][:, n], out_offset=None, in_=t["answers"],
                        in_offset=bass.IndirectOffsetOnAxis(ap=row[p][:, n:n + 1], axis=0),
                        bounds_check=E0 * SLOTS - 1, oob_is_err=False).then_inc(picked_in[p], 16)

            def rsqrt(b, mean_var, mean_var_ok, var, var_ok, r, r_ok, read_ok):
                eng.wait_ge(mean_var_ok, QT * (b + 1))
                at_least(eng, read_ok, QT * b)
                by_itself(eng, waited)
                nc.gpsimd.tensor_scalar(var[:], mean_var[:, :, 1], 1.0, EPS, ALU.mult, ALU.add).then_inc(var_ok, 1)
                eng.wait_ge(var_ok, b + 1)
                nc.gpsimd.tensor_tensor(r[:], var[:], minus_half[:], ALU.pow).then_inc(r_ok, 1)

            def norm3(b):
                rsqrt(b, mv3, mv3_ok, var3, var3_ok, rs3, rs3_ok, x3h_ok)

            def norm4(b):
                rsqrt(b, mv4, mv4_ok, var4, var4_ok, rs4, rs4_ok, x4h_ok)

            def residual(b, p):
                eng.wait_ge(x2_ok, QT * (b + 1))
                at_least(eng, x3_ok, b)
                nc.gpsimd.tensor_tensor(xb[:], x2[:, p], bo[:].unsqueeze(1).to_broadcast([P, QT, D]),
                                        ALU.add).then_inc(xb_ok, 1)

            def lower(b, high_ok, done, dst, src, high, low_ok, count=1):
                eng.wait_ge(high_ok, count)
                if done is not None:
                    at_least(eng, *done)
                nc.gpsimd.tensor_tensor(dst, src, high.bitcast(F32), ALU.subtract).then_inc(low_ok, 1)

            def v_lower(b):
                lower(b, v_high, (cx_ok, b), v[:, 1], vf[:], v[:, 0], v_low, b + 1)

            def cx_lower(b):
                lower(b, cx_high, (a_ok, b), cx[:, 1], cf[:], cx[:, 0], cx_low, b + 1)

            def hid_lower(b, j):
                es = slice(2 * j, 2 * j + 2)
                lower(b, hid_high, (down_ok, 2 * b), hid2[:, 1, es], hid[:, es], hid2[:, 0, es], hid_low,
                      2 * b + j + 1)

            gather(0, 0)
            gather(1, 1)
            norm3(0)
            eng.wait_ge(bo_ok, 1)
            residual(0, 0)
            v_lower(0)
            cx_lower(0)
            norm3(1)

            def step(b, p):
                has1, has2 = bounds(b)
                if has1:
                    residual(b + 1, 1 - p)
                norm4(b)
                if has1:
                    v_lower(b + 1)
                if has2:
                    gather(b + 2, p)
                for j in range(2):
                    hid_lower(b, j)
                if has1:
                    cx_lower(b + 1)
                if has2:
                    norm3(b + 2)

            batches(eng, step)

        @block.scalar
        def _(eng):
            eng.wait_ge(weights_in, 16 * len(parts))
            nc.scalar.activation(w[:, 0], w_in[:], ACT.Copy).then_inc(w_high, 1)
            eng.wait_ge(small_in, 16 * N_SMALL_F)
            eng.wait_ge(const_g, 2)

            def xT_higher(b):
                eng.wait_ge(x3T_ok, b + 1)
                at_least(eng, q_ok, b)
                nc.scalar.activation(xT[:, 0], bank_x[:].rearrange("p (k s) -> p k s", k=KD), ACT.Copy) \
                    .then_inc(xT_high, 1)

            def cT_higher(b):
                eng.wait_ge(cT_ok, b + 1)
                at_least(eng, v_ok, b)
                nc.scalar.activation(cT[:, 0], bank_c[:, 0:KD * C].rearrange("p (k s) -> p k s", k=KD),
                                     ACT.Copy).then_inc(cT_high, 1)

            def q_higher(b):
                eng.wait_ge(q_ok, b + 1)
                at_least(eng, a_ok, b)
                for k in range(KD):
                    nc.scalar.activation(qT[:, 0, k], bank_x[:, k * S:(k + 1) * S], ACT.Identity,
                                         bias=bq[:, k:k + 1]).then_inc(q_high, 1)

            def k_bias(b):
                eng.wait_ge(k_ok, b + 1)
                at_least(eng, ke_ok, KD * b)
                for k in range(KD):
                    nc.scalar.activation(kf[:, k], bank_c[:, k * C:(k + 1) * C], ACT.Identity,
                                         bias=bk[:, k:k + 1]).then_inc(kf_ok, 1)

            def k_exp(b):
                eng.wait_ge(kmax_ok, b + 1)
                at_least(eng, kn_ok, KD * b)
                for k in range(KD):
                    nc.scalar.activation(ke[:, k], kf[:, k], ACT.Exp, bias=kmax[:, k:k + 1],
                                         accum_out=ksum[:, k:k + 1]).then_inc(ke_ok, 1)

            def kp_higher(b):
                eng.wait_ge(kT_ok, b + 1)
                at_least(eng, cx_ok, b)
                nc.scalar.activation(kp[:, 0], bank_v[0:C, 0:D], ACT.Copy).then_inc(kp_high, 1)

            def v_higher(b):
                eng.wait_ge(vf_ok, b + 1)
                at_least(eng, cx_ok, b)
                nc.scalar.activation(v[:, 0], vf[:], ACT.Copy).then_inc(v_high, 1)

            def cx_higher(b):
                eng.wait_ge(cf_ok, b + 1)
                at_least(eng, a_ok, b)
                nc.scalar.activation(cx[:, 0], cf[:], ACT.Copy).then_inc(cx_high, 1)

            def a_higher(b):
                eng.wait_ge(a_ok, b + 1)
                at_least(eng, out_ok, b)
                nc.scalar.activation(aT[:, 0], bank_x[:].rearrange("p (k s) -> p k s", k=KD), ACT.Copy) \
                    .then_inc(a_high, 1)

            def x4_turned(b):
                eng.wait_ge(x4T_ok, b + 1)
                at_least(eng, gu_ok, 4 * b)
                at_least(eng, cv_ok, N_CV * b)
                turned = bank_t[:].rearrange("p (k s) -> p k s", k=KD)
                nc.scalar.activation(x4T[:, 0], turned, ACT.Copy).then_inc(x4T_high, 1)
                nc.scalar.activation(x4p[:, :, KC - 1:], turned, ACT.Copy).then_inc(x4p_ok, 1)

            def x4_relu(b):
                eng.wait_ge(x4h_ok, QT * (b + 1))
                at_least(eng, acc_ok, N_ACC * b)
                nc.scalar.activation(x4r[:], x4h[:], ACT.Relu).then_inc(x4r_ok, 1)

            def router_exp(b):
                eng.wait_ge(logit_ok, b + 1)
                at_least(eng, route, N_ROUTE * b)
                nc.scalar.activation(re[:], bank_t[:, 0:QT * E1].rearrange("p (t e) -> p t e", t=QT), ACT.Exp,
                                     scale=-1.0).then_inc(re_ok, 1)

            def tanh(b, j):
                eng.wait_ge(gu_ok, 4 * b + 2 * j + 2)
                at_least(eng, hs_ok, 2 * (b - 1) + j + 1)
                nc.scalar.activation(th[:, 2 * j:2 * j + 2], mlp[:, 2 * j:2 * j + 2, 0:S], ACT.Tanh,
                                     scale=0.5).then_inc(th_ok, 1)

            def hid_higher(b, j):
                eng.wait_ge(hid_ok, 2 * b + j + 1)
                at_least(eng, down_ok, 2 * b)
                nc.scalar.activation(hid2[:, 0, 2 * j:2 * j + 2], hid[:, 2 * j:2 * j + 2], ACT.Copy) \
                    .then_inc(hid_high, 1)

            def conv_rows(b):
                eng.wait_ge(cvT_ok, b + 1)
                at_least(eng, acc_ok, N_ACC * b)
                nc.scalar.activation(cvr[:], bank_t[:].rearrange("p (t d) -> p t d", t=QT), ACT.Copy) \
                    .then_inc(cvr_ok, 1)

            def attention1(b):
                xT_higher(b)
                cT_higher(b)
                q_higher(b)
                k_bias(b)
                k_exp(b)

            attention1(0)
            v_higher(0)
            kp_higher(0)
            cx_higher(0)
            a_higher(0)

            def step(b, p):
                has1, _ = bounds(b)
                if has1:
                    attention1(b + 1)
                    v_higher(b + 1)
                x4_turned(b)
                x4_relu(b)
                router_exp(b)
                tanh(b, 0)
                tanh(b, 1)
                if has1:
                    kp_higher(b + 1)
                conv_rows(b)
                hid_higher(b, 0)
                hid_higher(b, 1)
                if has1:
                    cx_higher(b + 1)
                    a_higher(b + 1)

            batches(eng, step)

        @block.vector
        def _(eng):
            def combine(b, p):
                eng.wait_ge(x1_in[p], 16 * (b // 2 + 1))
                eng.wait_ge(picked_in[p], 16 * QT * 2 * (b // 2 + 1))
                at_least(eng, xb_ok, b - 1)
                share = keep["weight"][:, bass.ds(b, 1)].rearrange("p o n -> p (o n)")
                for i in range(QT):
                    nc.vector.scalar_tensor_tensor(xa[:, i], picked[p][:, 2 * i], share[:, 2 * i:2 * i + 1],
                                                   x1[:, p, i], ALU.mult, ALU.add).then_inc(xa_ok, 1)
                for i in range(QT):
                    eng.wait_ge(xa_ok, QT * b + i + 1)
                    nc.vector.scalar_tensor_tensor(x2[:, p, i], picked[p][:, 2 * i + 1],
                                                   share[:, 2 * i + 1:2 * i + 2], xa[:, i],
                                                   ALU.mult, ALU.add).then_inc(x2_ok, 1)
                for i in range(QT):
                    eng.wait_ge(x2_ok, QT * b + i + 1)
                    nc.vector.bn_stats(stats3[:, i], x2[:, p, i]).then_inc(stats3_ok, 1)
                for i in range(QT):
                    eng.wait_ge(stats3_ok, QT * b + i + 1)
                    by_itself(eng, waited)
                    nc.vector.bn_aggr(mv3[:, i], stats3[:, i]).then_inc(mv3_ok, 1)

            def normalise3(b, p):
                eng.wait_ge(rs3_ok, b + 1)
                at_least(eng, x3T_ok, b)
                for i in range(QT):
                    nc.vector.tensor_scalar(x3h[:, i], x2[:, p, i], mv3[:, i, 0:1], rs3[:, i:i + 1],
                                            ALU.subtract, ALU.mult).then_inc(x3h_ok, 1)

            def xT_lower(b):
                eng.wait_ge(xT_high, b + 1)
                nc.vector.tensor_tensor(xT[:, 1], bank_x[:].rearrange("p (k s) -> p k s", k=KD),
                                        xT[:, 0].bitcast(F32), ALU.subtract).then_inc(xT_low, 1)

            def cT_lower(b):
                eng.wait_ge(cT_high, b + 1)
                nc.vector.tensor_tensor(cT[:, 1], bank_c[:, 0:KD * C].rearrange("p (k s) -> p k s", k=KD),
                                        cT[:, 0].bitcast(F32), ALU.subtract).then_inc(cT_low, 1)

            def q_lower(b):
                eng.wait_ge(q_high, KD * (b + 1))
                for k in range(KD):
                    nc.vector.scalar_tensor_tensor(qT[:, 1, k], bank_x[:, k * S:(k + 1) * S], bq[:, k:k + 1],
                                                   qT[:, 0, k].bitcast(F32), ALU.add, ALU.subtract) \
                        .then_inc(q_low, 1)

            def k_max(b):
                eng.wait_ge(kf_ok, KD * (b + 1))
                nc.vector.tensor_reduce(kmax[:], kf[:], AX.X, ALU.max, negate=True).then_inc(kmax_ok, 1)

            def k_norm(b):
                eng.wait_ge(ke_ok, KD * (b + 1))
                nc.vector.reciprocal(ksum[:], ksum[:]).then_inc(kr_ok, 1)
                eng.wait_ge(kr_ok, b + 1)
                at_least(eng, kT_ok, b)
                for k in range(KD):
                    nc.vector.tensor_scalar(kn[:, k], ke[:, k], ksum[:, k:k + 1], None, ALU.mult).then_inc(kn_ok, 1)

            def v_bias(b):
                eng.wait_ge(v_ok, b + 1)
                at_least(eng, v_low, b)
                nc.vector.tensor_tensor(vf[:], bank_v[0:C, 0:D], bv[0:C], ALU.add).then_inc(vf_ok, 1)

            def kp_lower(b):
                eng.wait_ge(kp_high, b + 1)
                nc.vector.tensor_tensor(kp[:, 1], bank_v[0:C, 0:D], kp[:, 0].bitcast(F32), ALU.subtract) \
                    .then_inc(kp_low, 1)

            def own_heads(b):
                eng.wait_ge(cx_ok, b + 1)
                at_least(eng, cx_low, b)
                nc.vector.tensor_tensor(cf[:], bank_v[:, 0:KD * P].rearrange("p (k e) -> p k e", k=KD),
                                        heads[:].unsqueeze(1).to_broadcast([P, KD, P]), ALU.mult) \
                    .then_inc(cf_ok, 1)

            def a_lower(b):
                eng.wait_ge(a_high, b + 1)
                nc.vector.tensor_tensor(aT[:, 1], bank_x[:].rearrange("p (k s) -> p k s", k=KD),
                                        aT[:, 0].bitcast(F32), ALU.subtract).then_inc(a_low, 1)

            def x3_new(b, p):
                eng.wait_ge(out_ok, b + 1)
                eng.wait_ge(xb_ok, b + 1)
                nc.vector.scalar_tensor_tensor(x3[:, p], bank_c[:].rearrange("p (t d) -> p t d", t=QT),
                                               keep["gate"][:, 1:2], xb[:], ALU.mult, ALU.add).then_inc(x3_ok, 1)
                eng.wait_ge(x3_ok, b + 1)
                for i in range(QT):
                    nc.vector.bn_stats(stats4[:, i], x3[:, p, i]).then_inc(stats4_ok, 1)
                for i in range(QT):
                    eng.wait_ge(stats4_ok, QT * b + i + 1)
                    by_itself(eng, waited)
                    nc.vector.bn_aggr(mv4[:, i], stats4[:, i]).then_inc(mv4_ok, 1)

            def normalise4(b, p):
                eng.wait_ge(rs4_ok, b + 1)
                at_least(eng, x4r_ok, b)
                at_least(eng, x4T_ok, b)
                for i in range(QT):
                    nc.vector.tensor_scalar(x4h[:, i], x3[:, p, i], mv4[:, i, 0:1], rs4[:, i:i + 1],
                                            ALU.subtract, ALU.mult).then_inc(x4h_ok, 1)

            def x4_lower(b):
                eng.wait_ge(x4p_ok, b + 1)
                nc.vector.tensor_tensor(x4T[:, 1], bank_t[:].rearrange("p (k s) -> p k s", k=KD),
                                        x4T[:, 0].bitcast(F32), ALU.subtract).then_inc(x4T_low, 1)

            def convolve(b):
                step = N_CV * b
                at_least(eng, cvT_ok, b)
                for k in range(KD):
                    nc.vector.tensor_scalar(cv[:, k], x4p[:, k, 0:S], conv_w[:, k, 0:1], conv_b[:, k:k + 1],
                                            ALU.mult, ALU.add).then_inc(cv_ok, 1)
                for j in range(1, KC):
                    for k in range(KD):
                        eng.wait_ge(cv_ok, step + KD * (j - 1) + k + 1)
                        nc.vector.scalar_tensor_tensor(cv[:, k], x4p[:, k, j:j + S], conv_w[:, k, j:j + 1],
                                                       cv[:, k], ALU.mult, ALU.add).then_inc(cv_ok, 1)

            def router(b):
                step = 0

                def then(instruction):
                    nonlocal step
                    step += 1
                    instruction.then_inc(route, 1)
                    eng.wait_ge(route, N_ROUTE * b + step)

                def wide(ap):
                    return ap.unsqueeze(2).to_broadcast([P, QT, E1])

                eng.wait_ge(re_ok, b + 1)
                then(nc.vector.tensor_scalar(re[:], re[:], 1.0, None, ALU.add))
                then(nc.vector.reciprocal(rsg[:], re[:]))
                then(nc.vector.tensor_tensor(sel[:], rsg[:], rbias[:].unsqueeze(1).to_broadcast([P, QT, E1]),
                                             ALU.add))
                for i in range(QT):
                    by_itself(eng, waited)
                    then(nc.vector.max(top[:, i], sel[:, i]))
                for i in range(QT):
                    by_itself(eng, waited)
                    then(nc.vector.max_index(topi[:, i], top[:, i], sel[:, i]))
                then(nc.vector.tensor_copy(topf[:], topi[:, :, 0:2]))
                for i in range(QT):
                    then(nc.vector.tensor_tensor(oh[:, i], iota_e[:].unsqueeze(1).to_broadcast([P, 2, E1]),
                                                 topf[:, i].unsqueeze(2).to_broadcast([P, 2, E1]), ALU.is_equal))
                then(nc.vector.tensor_tensor(cw[:], oh[:, :, 0], oh[:, :, 1], ALU.add))
                then(nc.vector.tensor_tensor(cw[:], cw[:], rsg[:], ALU.mult))
                then(nc.vector.reduce_sum(cws[:], cw[:], AX.X))
                then(nc.vector.tensor_scalar(cws[:], cws[:], 1e-9, None, ALU.add))
                then(nc.vector.reciprocal(cws[:], cws[:]))
                then(nc.vector.tensor_tensor(cw[:], cw[:], wide(cws[:]), ALU.mult))
                then(nc.vector.tensor_tensor(cws[:], cw[:, :, EM], cw[:, :, EM + 2], ALU.add))
                assert step == N_ROUTE

            def silu(b, j):
                es = slice(2 * j, 2 * j + 2)
                eng.wait_ge(th_ok, 2 * b + j + 1)
                at_least(eng, hid_low, 2 * (b - 1) + j + 1)
                nc.vector.scalar_tensor_tensor(hs[:, es], th[:, es], 1.0, mlp[:, es, 0:S], ALU.add, ALU.mult) \
                    .then_inc(hs_ok, 1)
                eng.wait_ge(hs_ok, 2 * b + j + 1)
                nc.vector.scalar_tensor_tensor(hid[:, es], hs[:, es], 0.5, mlp[:, es, S:2 * S], ALU.mult, ALU.mult) \
                    .then_inc(hid_ok, 1)

            def weigh(b, j):
                for e in (2 * j, 2 * j + 1):
                    if e % 2 == 0:
                        eng.wait_ge(down_ok, 2 * b + j + 1)
                    if e == 0:
                        eng.wait_ge(cvr_ok, b + 1)
                        at_least(eng, yo_ok, b)
                    for i in range(QT):
                        at_least(eng, acc_ok, N_ACC * b + QT * (e - 1) + i + 1 if e else N_ACC * b)
                        nc.vector.scalar_tensor_tensor(acc[:, i], mlp[:, e, i * D:(i + 1) * D], cw[:, i, e:e + 1],
                                                       (acc if e else cvr)[:, i], ALU.mult, ALU.add) \
                            .then_inc(acc_ok, 1)

            def close(b, p):
                eng.wait_ge(x4r_ok, b + 1)
                for n, (src, share) in enumerate(((x4h, cws[:].unsqueeze(2)), (x4r, cw[:, :, EM + 3:EM + 4]))):
                    for i in range(QT):
                        eng.wait_ge(acc_ok, N_ACC * b + QT * (EM + n - 1) + i + 1)
                        nc.vector.scalar_tensor_tensor(acc[:, i], src[:, i], share[:, i], acc[:, i],
                                                       ALU.mult, ALU.add).then_inc(acc_ok, 1)
                eng.wait_ge(acc_ok, N_ACC * (b + 1))
                at_least(eng, yo_out[p], 16 * (b // 2))
                nc.vector.scalar_tensor_tensor(yo[:, p], acc[:], keep["gate"][:, 3:4], x3[:, p],
                                               ALU.mult, ALU.add).then_inc(yo_ok, 1)

            def attention1(b):
                xT_lower(b)
                cT_lower(b)
                q_lower(b)
                k_max(b)
                v_bias(b)

            eng.wait_ge(small_in, 16 * N_SMALL_F)
            nc.vector.tensor_scalar(bo[:], bo[:], keep["gate"][:, 1:2], None, ALU.mult).then_inc(bo_ok, 1)
            combine(0, 0)
            normalise3(0, 0)
            eng.wait_ge(w_high, 1)
            nc.vector.tensor_tensor(w[:, 1], w_in[:], w[:, 0].bitcast(F32), ALU.subtract).then_inc(w_low, 1)
            attention1(0)
            k_norm(0)
            kp_lower(0)
            own_heads(0)
            combine(1, 1)
            normalise3(1, 1)
            a_lower(0)
            x3_new(0, 0)

            def step(b, p):
                has1, has2 = bounds(b)
                if has1:
                    xT_lower(b + 1)
                    cT_lower(b + 1)
                normalise4(b, p)
                if has1:
                    q_lower(b + 1)
                    k_max(b + 1)
                    v_bias(b + 1)
                x4_lower(b)
                if has1:
                    k_norm(b + 1)
                router(b)
                convolve(b)
                silu(b, 0)
                silu(b, 1)
                if has1:
                    kp_lower(b + 1)
                    own_heads(b + 1)
                if has2:
                    combine(b + 2, p)
                weigh(b, 0)
                if has1:
                    a_lower(b + 1)
                weigh(b, 1)
                close(b, p)
                if has2:
                    normalise3(b + 2, p)
                if has1:
                    x3_new(b + 1, 1 - p)

            batches(eng, step)

        @block.tensor
        def _(eng):
            def turn3(b, p):
                eng.wait_ge(x3h_ok, QT * (b + 1))
                at_least(eng, a_low, b)
                for k in range(KD):
                    for i in range(QT):
                        last = nc.tensor.transpose(bank_x[:, k * S + i * P:k * S + (i + 1) * P],
                                                   x3h[:, i, k * P:(k + 1) * P], ident[:])
                last.then_inc(x3T_ok, 1)
                eng.wait_ge(cin_in[p], 16 * (b // 2 + 1))
                at_least(eng, x3_ok, b)
                for k in range(KD):
                    last = nc.tensor.transpose(bank_c[:, k * C:(k + 1) * C], cin[0:C, p, k * P:(k + 1) * P],
                                               ident[0:C, 0:C])
                last.then_inc(cT_ok, 1)

            def queries(b):
                eng.wait_ge(xT_low, b + 1)
                for m in range(KD):
                    last = split_product(nc, bank_x[:, m * S:(m + 1) * S], lambda a, k: weight("WqT", a, k, m),
                                         lambda a, k: xT[:, a, k], KD)
                last.then_inc(q_ok, 1)

            def keys_values(b):
                eng.wait_ge(cT_low, b + 1)
                for m in range(KD):
                    last = split_product(nc, bank_c[:, m * C:(m + 1) * C], lambda a, k: weight("WkT", a, k, m),
                                         lambda a, k: cT[:, a, k], KD)
                last.then_inc(k_ok, 1)
                at_least(eng, cf_ok, b)
                split_product(nc, bank_v[0:C, 0:D], lambda a, k: cT[:, a, k], lambda a, k: weight("WvT", a, k),
                              KD).then_inc(v_ok, 1)

            def turn_k(b):
                eng.wait_ge(kn_ok, KD * (b + 1))
                eng.wait_ge(vf_ok, b + 1)
                for k in range(KD):
                    last = nc.tensor.transpose(bank_v[0:C, k * P:(k + 1) * P], kn[:, k], ident[:])
                last.then_inc(kT_ok, 1)

            def context(b):
                eng.wait_ge(kp_low, b + 1)
                eng.wait_ge(v_low, b + 1)
                for m in range(KD):
                    cols = slice(m * P, (m + 1) * P)
                    last = split_product(nc, bank_v[:, cols], lambda a, _: kp[:, a, cols],
                                         lambda a, _: v[:, a, cols], 1)
                last.then_inc(cx_ok, 1)

            def attended(b):
                eng.wait_ge(cx_low, b + 1)
                eng.wait_ge(q_low, KD * (b + 1))
                for m in range(KD):
                    last = split_product(nc, bank_x[:, m * S:(m + 1) * S], lambda a, _: cx[:, a, m],
                                         lambda a, _: qT[:, a, m], 1)
                last.then_inc(a_ok, 1)

            def output(b):
                eng.wait_ge(a_low, b + 1)
                eng.wait_ge(kf_ok, KD * (b + 1))
                for i in range(QT):
                    last = split_product(nc, bank_c[:, i * D:(i + 1) * D],
                                         lambda a, k: aT[:, a, k, i * P:(i + 1) * P],
                                         lambda a, k: weight("WoT", a, k), KD)
                last.then_inc(out_ok, 1)

            def turn4(b):
                eng.wait_ge(x4h_ok, QT * (b + 1))
                at_least(eng, cvr_ok, b)
                for k in range(KD):
                    for i in range(QT):
                        last = nc.tensor.transpose(bank_t[:, k * S + i * P:k * S + (i + 1) * P],
                                                   x4h[:, i, k * P:(k + 1) * P], ident[:])
                last.then_inc(x4T_ok, 1)

            def logits(b):
                eng.wait_ge(x4T_low, b + 1)
                for i in range(QT):
                    last = split_product(nc, bank_t[:, i * E1:(i + 1) * E1],
                                         lambda a, k: x4T[:, a, k, i * P:(i + 1) * P],
                                         lambda a, k: weight("Wr1", a, k), KD)
                last.then_inc(logit_ok, 1)

            def gate_up(b, e):
                at_least(eng, acc_ok, N_ACC * (b - 1) + QT * (e + 1))
                for half, name in enumerate(("Wg", "Wu")):
                    last = split_product(nc, mlp[:, e, half * S:(half + 1) * S],
                                         lambda a, k: weight(name, a, e, k), lambda a, k: x4T[:, a, k], KD)
                last.then_inc(gu_ok, 1)

            def turn_conv(b):
                eng.wait_ge(cv_ok, N_CV * (b + 1))
                eng.wait_ge(re_ok, b + 1)
                for k in range(KD):
                    for i in range(QT):
                        last = nc.tensor.transpose(bank_t[:, i * D + k * P:i * D + (k + 1) * P],
                                                   cv[:, k, i * P:(i + 1) * P], ident[:])
                last.then_inc(cvT_ok, 1)

            def down(b, j):
                eng.wait_ge(hid_low, 2 * b + j + 1)
                for e in (2 * j, 2 * j + 1):
                    for i in range(QT):
                        last = split_product(nc, mlp[:, e, i * D:(i + 1) * D],
                                             lambda a, _: hid2[:, a, e, i * P:(i + 1) * P],
                                             lambda a, _: weight("Wd", a, e), 1)
                last.then_inc(down_ok, 1)

            eng.wait_ge(small_in, 16 * N_SMALL_F)
            turn3(0, 0)
            eng.wait_ge(w_low, 1)
            queries(0)
            keys_values(0)
            turn_k(0)
            context(0)
            attended(0)
            output(0)

            def step(b, p):
                has1, _ = bounds(b)
                if has1:
                    turn3(b + 1, 1 - p)
                    queries(b + 1)
                    keys_values(b + 1)
                turn4(b)
                logits(b)
                gate_up(b, 0)
                gate_up(b, 1)
                gate_up(b, 2)
                gate_up(b, 3)
                if has1:
                    turn_k(b + 1)
                turn_conv(b)
                if has1:
                    context(b + 1)
                down(b, 0)
                if has1:
                    attended(b + 1)
                down(b, 1)
                if has1:
                    output(b + 1)

            batches(eng, step)


def build(nc, t):
    with ExitStack() as ctx:
        keep = {
            "weight": ctx.enter_context(nc.sbuf_tensor("keep_weight", [P, B, QT * 2], F32)),
            "row": ctx.enter_context(nc.sbuf_tensor("keep_row", [P, B, QT * 2], U32)),
            "gate": ctx.enter_context(nc.sbuf_tensor("keep_gate", [P, 4], F32)),
            "sent": ctx.enter_context(nc.semaphore("sent")),
            "picked_in": [ctx.enter_context(nc.semaphore(f"picked_in{i}")) for i in range(2)],
        }
        attend(nc, t, keep)
        experts(nc, t)
        finish(nc, t, keep)



def constants():
    one = 0x3F80
    eye = np.eye(P, dtype=np.float32)
    headrow = np.zeros((P, H0, P), np.uint16)
    for h in range(H0):
        headrow[h, h] = headrow[64 + h, h] = one
    firstrow = np.zeros((P, P), np.uint16)
    firstrow[0] = firstrow[64] = one
    tri = np.stack([np.triu(np.ones((P, P)), 1), np.ones((P, P))], 1).astype(np.uint16) * np.uint16(one)
    slot0 = np.arange(B)[:, None] * CAP + np.arange(E0)[None] * SLOTS
    heads1 = np.kron(np.eye(P // HD1), np.ones((HD1, HD1))).astype(np.float32)
    return {
        "ident": eye, "headrow": headrow, "firstrow": firstrow, "tri": tri, "heads1": heads1,
        "iota_e": np.tile(np.arange(E0, dtype=np.float32), (P, 1)),
        "slot0": np.tile(slot0.astype(np.float32), (P, 1, 1)),
    }


NAMES = {
    "x": "x", "ctx": "ctx_1024", "g_xattn": "g_xattn", "g_ffn": "g_ffn",
    "g_x": "L0_xattn_g_x", "b_x": "L0_xattn_b_x", "g_l": "L0_xattn_g_l", "b_l": "L0_xattn_b_l",
    "w_q": "L0_xattn_w_q", "w_kv": "L0_xattn_w_kv", "w_out": "L0_xattn_w_out",
    "g_o": "L0_xattn_g_o", "b_o": "L0_xattn_b_o",
    "Wr0": "L0_ffn_Wr", "br": "L0_ffn_br", "W1": "L0_ffn_W1", "b1": "L0_ffn_b1", "W2": "L0_ffn_W2",
    "b2": "L0_ffn_b2",
    "bq": "L1_xattn_bq", "bk": "L1_xattn_bk", "bv": "L1_xattn_bv", "bo1": "L1_xattn_bo",
    "Wr1": "L1_ffn_Wr", "rbias": "L1_ffn_router_bias", "Wg": "L1_ffn_Wg", "Wu": "L1_ffn_Wu", "Wd": "L1_ffn_Wd",
    "conv_w": "L1_ffn_conv_w", "conv_b": "L1_ffn_conv_b",
}
TURNED = {"WqT": "L1_xattn_Wq", "WkT": "L1_xattn_Wk", "WvT": "L1_xattn_Wv", "WoT": "L1_xattn_Wo"}


def layout(inputs):
    arrays = {n: np.ascontiguousarray(inputs[full]) for n, full in NAMES.items()}
    arrays.update({n: np.ascontiguousarray(np.asarray(inputs[full]).T) for n, full in TURNED.items()})
    for n in ("g_l", "b_l", "g_x", "b_x", "bq", "bk", "b1", "conv_w", "conv_b"):
        a = arrays[n]
        arrays[n] = np.ascontiguousarray(a.reshape(*a.shape[:-1], a.shape[-1] // P, P).T)
    mask = np.ascontiguousarray(inputs["mask_BxS2_bf1"]).view(np.uint8)
    arrays["mask"] = mask
    arrays["mask_t"] = np.ascontiguousarray(mask.T)
    arrays.update(constants())
    return arrays


def kernel(**inputs):
    import concourse.bacc as bacc
    from concourse.bass_utils import run_bass_kernel_spmd

    nc = bacc.Bacc("TRN2", target_bir_lowering=False, num_devices=1)
    arrays = layout(inputs)
    t = {n: nc.dram_tensor(n, a.shape, mybir.dt.from_np(a.dtype), kind="ExternalInput").ap()
         for n, a in arrays.items()}
    t["out"] = nc.dram_tensor("out", (B, S, D), F32, kind="ExternalOutput").ap()
    t["x1"] = nc.dram_tensor("x1", (B, S, D), F32, kind="Internal").ap()
    t["slots"] = nc.dram_tensor("slots", (E0 * SLOTS, D), F32, kind="Internal").ap()
    t["answers"] = nc.dram_tensor("answers", (E0 * SLOTS, D), F32, kind="Internal").ap()
    build(nc, t)
    r = run_bass_kernel_spmd(nc, [arrays], core_ids=[0])
    return r.results[0]["out"]
```

```python
from contextlib import ExitStack

import numpy as np

import concourse.bass as bass
from concourse import mybir

F32 = mybir.dt.float32
F32R = mybir.dt.float32r
BF16 = mybir.dt.bfloat16
U8 = mybir.dt.uint8
U16 = mybir.dt.uint16
U32 = mybir.dt.uint32
ALU = mybir.AluOpType
ACT = mybir.ActivationFunctionType
AX = mybir.AxisListType

B, S, D = 32, 256, 256
C = 120
P = 128
KD = D // P
QT = S // P
H0, DH = 8, 64
INNER = H0 * DH
KI = INNER // P
NKV = C + S
EPS = 1e-5
E0, CAP = 8, max(1, int(S / 8 * 1.25))
SLOTS = B * CAP
HID = 1024
KH = HID // P
HD1 = 16
E1, EM = 8, 4
KC = 4
MASKED = 1e30
NOWHERE = 1 << 20
PASSES = ((0, 0), (0, 1), (1, 0))


def at_least(eng, sem, value):
    if not (isinstance(value, int) and value <= 0):
        eng.wait_ge(sem, value)


def by_itself(eng, waited):
    eng.sem_inc(waited, 1)


def batches(eng, step, tail=1):
    step(0, 0)
    step(1, 1)
    with eng.Fori(1, B // 2 - tail) as pair:
        step(pair * 2, 0)
        step(pair * 2 + 1, 1)
    for b in range(B - 2 * tail, B):
        step(b, b % 2)


def split_product(nc, out, stationary, moving, tiles, start=True, stop=True):
    todo = [(a, b, t) for t in range(tiles) for a, b in PASSES]
    for n, (a, b, t) in enumerate(todo):
        last = nc.tensor.matmul(out, stationary(a, t), moving(b, t),
                                start=start and n == 0, stop=stop and n == len(todo) - 1)
    return last


def zero_semaphores(nc, sems):
    with nc.Block() as block:
        @block.gpsimd
        def _(pool):
            nums = sorted(s.num for s in sems)
            first = nums[0]
            for num, following in zip(nums, nums[1:] + [-1]):
                if following != num + 1:
                    pool.sem_clear(range(first, num + 1))
                    first = following


def attend(nc, t, keep):
    ctx = ExitStack()
    with ctx:
        def sb(name, shape, dt=F32):
            return ctx.enter_context(nc.sbuf_tensor(name, shape, dt))

        def pb(name, shape):
            return ctx.enter_context(nc.psum_tensor(name, shape, F32))

        sems = []

        def sem(name):
            sems.append(ctx.enter_context(nc.semaphore(name)))
            return sems[-1]

        stage_kv = keep["w1_in"]
        wq = sb("a_wq", [P, 2, KD, INNER], F32R)
        wkv = sb("a_wkv", [P, 2, KD, 2 * INNER], F32R)
        wo = sb("a_wo", [P, 2, KI, D], F32R)
        wr = sb("a_wr", [P, KD, E0])
        ident = sb("a_ident", [P, P])
        tri = sb("a_tri", [P, 2, P], BF16)
        headrow_f = sb("a_headrow_f", [P, H0, P], BF16)
        headrow = sb("a_headrow", [P, H0, P], F32R)
        firstrow = sb("a_firstrow", [P, P], BF16)
        iota_e = sb("a_iota_e", [P, E0])
        slot0 = sb("a_slot0", [P, B, E0])
        mask_u8 = sb("a_mask_u8", [P, B, C], U8)
        mask_t8 = sb("a_mask_t8", [C, B], U8)
        mask_bias = sb("a_mask_bias", [C, B])
        mask_col = sb("a_mask_col", [C, 2])
        mask_row = sb("a_mask_row", [P, 2, C], BF16)
        aff = sb("a_aff", [P, 4, KD])
        go = sb("a_go", [P, D])
        bo = sb("a_bo", [P, D])
        br = sb("a_br", [P, E0])
        gate = sb("a_gate", [P, 4])
        tgate = sb("a_tgate", [P, 4])
        minus_half = sb("a_minus_half", [P, 4])
        zeros = sb("a_zeros", [P, 2 * D])
        xn = sb("a_xn", [P, 2, QT, D])
        cn = sb("a_cn", [P, 2, D])
        xr = sb("a_xr", [P, 2, QT, D])
        stats = sb("a_stats", [P, 3, 6])
        mv = sb("a_mv", [P, 3, 2])
        var = sb("a_var", [P, 3])
        rs = sb("a_rs", [P, 3])
        xh = sb("a_xh", [P, 3, D])
        kvin = sb("a_kvin", [P, KD, NKV])
        kvin2 = sb("a_kvin2", [P, 2, KD, NKV], F32R)
        qT = sb("a_qT", [P, 2, 2, KI, S], F32R)
        kT = sb("a_kT", [P, 2, 2, KI, NKV], F32R)
        vo = sb("a_vo", [P, 2, 2, 3, KI, 3, DH], F32R)
        nmax = sb("a_nmax", [P, 2, QT, H0])
        nmaxT = sb("a_nmaxT", [P, 2, S], F32R)
        prob = sb("a_prob", [P, 2, 3, S])
        prob2 = sb("a_prob2", [P, 2, 2, 3, S], F32R)
        den = sb("a_den", [P, 2, S])
        rden = sb("a_rden", [P, S])
        att = sb("a_att", [P, KI, S])
        att2 = sb("a_att2", [P, 2, KI, S], F32R)
        y1 = sb("a_y1", [P, QT, D])
        xb = sb("a_xb", [P, QT, D])
        x1 = sb("a_x1", [P, 2, QT, D])
        stage_q = att[:].rearrange("p m s -> p (m s)").rearrange("p (k n) -> p k n", k=KD)
        stage_o = x1[:].rearrange("p a k d -> p (a k) d")
        stats1 = sb("a_stats1", [P, QT, 6])
        mv1 = sb("a_mv1", [P, QT, 2])
        var1 = sb("a_var1", [P, QT])
        rs1 = sb("a_rs1", [P, QT])
        stats2 = sb("a_stats2", [P, QT, 6])
        mv2 = sb("a_mv2", [P, QT, 2])
        var2 = sb("a_var2", [P, QT])
        rs2 = sb("a_rs2", [P, QT])
        x2h = sb("a_x2h", [P, 2, QT, D])
        rT = sb("a_rT", [P, KD, S])
        lg = sb("a_lg", [P, QT, E0])
        lmax = sb("a_lmax", [P, QT])
        le = sb("a_le", [P, QT, E0])
        lsum = sb("a_lsum", [P, QT])
        pr = sb("a_pr", [P, QT, E0])
        top = sb("a_top", [P, QT, E0])
        topi = sb("a_topi", [P, QT, E0], U32)
        topf = sb("a_topf", [P, QT, 2])
        oh = sb("a_oh", [P, QT, 2, E0])
        ohs = sb("a_ohs", [P, QT, E0], BF16)
        at_e = sb("a_at_e", [P, QT, 2, E0])
        pos = sb("a_pos", [P, QT, 2])
        at_b = sb("a_at_b", [P, QT, 2, E0])
        base = sb("a_base", [P, QT, 2])
        kept = sb("a_kept", [P, QT, 2])
        slot = sb("a_slot", [P, QT, 2])
        slot_s = sb("a_slot_s", [P, QT, 2])
        wsel = sb("a_wsel", [P, QT, 2])
        sidx = sb("a_sidx", [P, 2, QT * 2], U32)

        score_x = pb("a_score_x", [P, QT, S])
        score_c = pb("a_score_c", [P, 512])
        ctxv = pb("a_ctxv", [P, 512])
        probe = [pb(f"a_probe{i}", [P, 512]) for i in range(2)]
        proj = [pb(f"a_proj{i}", [P, 512]) for i in range(2)]
        misc = pb("a_misc", [P, 512])

        w_in = [sem(f"a_w_in{i}") for i in range(3)]
        first_in, small_in = sem("a_first_in"), sem("a_small_in")
        w_high, w_low = sem("a_w_high"), sem("a_w_low")
        const_ok = sem("a_const_ok")
        const_g = sem("a_const_g")
        waited = sem("a_waited")
        gate_ok = sem("a_gate_ok")
        zero_ok = sem("a_zero_ok")
        zeroed = sem("a_zeroed")
        xn_in = [sem(f"a_xn_in{i}") for i in range(2)]
        cn_in = [sem(f"a_cn_in{i}") for i in range(2)]
        xr_in = [sem(f"a_xr_in{i}") for i in range(2)]
        stats_ok, mv_ok, var_ok, rs_ok, xh_ok = (sem("a_" + s) for s in
                                                 ("stats_ok", "mv_ok", "var_ok", "rs_ok", "xh_ok"))
        xT_ok, kvin_ok, kvin_low = (sem("a_" + s) for s in ("xT_ok", "kvin_ok", "kvin_low"))
        proj_ok, proj_high, proj_low = (sem("a_" + s) for s in ("proj_ok", "proj_high", "proj_low"))
        mrow_ok, probe_ok, nmax_ok, nmT_ok, nmT_out = (sem("a_" + s) for s in
                                                       ("mrow_ok", "probe_ok", "nmax_ok", "nmT_ok", "nmT_out"))
        score_ok, exp_ok, prob_low = (sem("a_" + s) for s in ("score_ok", "exp_ok", "prob_low"))
        evac_ok = sem("a_evac_ok")
        ctxv_ok, rden_ok, att_ok, att_high, att_low = (sem("a_" + s) for s in
                                                       ("ctxv_ok", "rden_ok", "att_ok", "att_high", "att_low"))
        out_ok, stats1_ok, mv1_ok, var1_ok, rs1_ok = (sem("a_" + s) for s in
                                                      ("out_ok", "stats1_ok", "mv1_ok", "var1_ok", "rs1_ok"))
        y1_ok, xb_ok, x1_ok = (sem("a_" + s) for s in ("y1_ok", "xb_ok", "x1_ok"))
        x1_out = [sem(f"a_x1_out{i}") for i in range(2)]
        stats2_ok, mv2_ok, var2_ok, rs2_ok, x2h_ok = (sem("a_" + s) for s in
                                                      ("stats2_ok", "mv2_ok", "var2_ok", "rs2_ok", "x2h_ok"))
        rT_ok, rT_out, logit_ok, count_ok = (sem("a_" + s) for s in ("rT_ok", "rT_out", "logit_ok", "count_ok"))
        soft, le_ok, route = (sem("a_" + s) for s in ("soft", "le_ok", "route"))
        sent = keep["sent"]

        N_SOFT = 14
        N_ROUTE = 11

        UNITS = (("q", 0), ("k", 0), ("k", 1), ("q", 1), ("k", 2), ("k", 3), ("v", 2), ("v", 0), ("v", 1))
        NU, N_QK = len(UNITS), 6
        MADE = ((), (), (0, 1), (2, 3, 4), (5,), (6,), (), (7,))

        def unit(kind, i):
            return UNITS.index((kind, i))

        def projection(p, u, plane):
            kind, i = UNITS[u]
            if kind == "q":
                return (proj[u % 2][:].rearrange("p (m s) -> p m s", m=2), qT[:, p, plane, 2 * i:2 * i + 2],
                        DH ** -0.5)
            if kind == "k":
                return proj[u % 2][:, 0:NKV], kT[:, p, plane, i], 1.0
            rows = C if i == 2 else P
            return (proj[u % 2][0:rows].rearrange("p (m v d) -> p m v d", m=KI, v=2),
                    vo[0:rows, p, plane, i, :, 0:3:2], 1.0)

        ctx.callback(zero_semaphores, nc, sems)
        block = ctx.enter_context(nc.Block())

        @block.sync
        def _(eng):
            def load(b, p):
                at_least(eng, xh_ok, 3 * (b - 1))
                eng.dma_start(xn[:, p], t["x"][bass.ds(b, 1)].rearrange("o (k p) d -> p (o k) d", p=P)) \
                    .then_inc(xn_in[p], 16)
                eng.dma_start(cn[0:C, p], t["ctx"][bass.ds(b, 1)].rearrange("o c d -> c (o d)")) \
                    .then_inc(cn_in[p], 16)

            load(0, 0)
            eng.dma_start(ident[:], t["ident"]).then_inc(first_in, 16)
            for i, name in enumerate(("g_l", "b_l", "g_x", "b_x")):
                eng.dma_start(aff[:, i], t[name]).then_inc(first_in, 16)
            eng.dma_start(stage_q, t["w_q"].rearrange("(k p) n -> p k n", p=P)).then_inc(w_in[0], 16)
            eng.dma_start(stage_kv[:], t["w_kv"].rearrange("(k p) n -> p k n", p=P)).then_inc(w_in[1], 16)
            load(1, 1)
            small = [(tri[:].bitcast(U16), t["tri"]), (headrow_f[:].bitcast(U16), t["headrow"]),
                     (firstrow[:].bitcast(U16), t["firstrow"]), (iota_e[:], t["iota_e"]), (slot0[:], t["slot0"]),
                     (mask_u8[:], t["mask"].partition_broadcast(P)), (mask_t8[:], t["mask_t"]),
                     (go[:], t["g_o"].partition_broadcast(P)), (bo[:], t["b_o"].partition_broadcast(P)),
                     (br[:], t["br"].partition_broadcast(P)),
                     (gate[:, 0:2], t["g_xattn"].partition_broadcast(P)),
                     (gate[:, 2:4], t["g_ffn"].partition_broadcast(P)),
                     (wr[:], t["Wr0"].rearrange("(k p) n -> p k n", p=P))]
            assert len(small) == N_SMALL
            for dst, src in small:
                eng.dma_start(dst, src).then_inc(small_in, 16)
            eng.dma_start(stage_o, t["w_out"].rearrange("(k p) n -> p k n", p=P)).then_inc(w_in[2], 16)
            eng.wait_ge(w_low, 2)
            for n in range(KD):
                eng.dma_start(stage_kv[:, n], t["W1"][0, n * P:(n + 1) * P]).then_inc(keep["w1_loaded"], 16)
            eng.wait_ge(zero_ok, 1)
            rows = P * 10
            with eng.Fori(0, E0 * SLOTS // rows) as n:
                eng.dma_start(t["slots"][bass.ts(n, rows)].rearrange("(p r t) d -> p r (t d)", p=P, t=2),
                              zeros[:].unsqueeze(1).to_broadcast([P, 5, 2 * D])) \
                    .then_inc(zeroed, 16)

            def step(b, p):
                at_least(eng, x1_ok, QT * (b - 1))
                eng.dma_start(xr[:, p], t["x"][bass.ds(b, 1)].rearrange("o (k p) d -> p (o k) d", p=P)) \
                    .then_inc(xr_in[p], 16)
                if not isinstance(b, int) or b + 2 < B:
                    load(b + 2, p)
                if not (isinstance(b, int) and b < 1):
                    store(b - 1, 1 - p)

            def store(b, p):
                eng.wait_ge(x1_ok, QT * (b + 1))
                eng.dma_start(t["x1"][bass.ds(b, 1)].rearrange("o (k p) d -> p (o k) d", p=P), x1[:, p]) \
                    .then_inc(x1_out[p], 16)

            batches(eng, step)
            store(B - 1, 1)
            for p in range(2):
                eng.wait_ge(x1_out[p], 16 * (B // 2))

        @block.gpsimd
        def _(eng):
            nc.gpsimd.memset(zeros[:], 0.0).then_inc(zero_ok, 1)
            nc.gpsimd.memset(minus_half[:], -0.5).then_inc(const_g, 1)
            nc.gpsimd.memset(var[:], 1.0).then_inc(const_g, 1)
            eng.wait_ge(const_g, 2)

            def rsqrt(b, mean_var, mean_var_ok, n, v, v_ok, r, r_ok, scales):
                eng.wait_ge(mean_var_ok, n * (b + 1))
                at_least(eng, r_ok, b)
                by_itself(eng, waited)
                for lo, hi, rows, mul, add in scales:
                    nc.gpsimd.tensor_scalar(v[0:rows, lo:hi], mean_var[0:rows, lo:hi, 1], mul, add,
                                            ALU.mult, ALU.add).then_inc(v_ok, 1)
                eng.wait_ge(v_ok, len(scales) * (b + 1))
                nc.gpsimd.tensor_tensor(r[:], v[:], minus_half[:, 0:v.shape[1]], ALU.pow).then_inc(r_ok, 1)

            def norm(b):
                at_least(eng, xh_ok, 3 * b)
                rsqrt(b, mv, mv_ok, 3, var, var_ok, rs, rs_ok,
                      ((0, 2, P, 1.0 + EPS, EPS * EPS), (2, 3, C, 1.0, EPS)))

            def prob_lower(b, h):
                eng.wait_ge(exp_ok, 4 * (H0 * b + h + 1))
                at_least(eng, ctxv_ok, H0 * b + h - 1)
                nc.gpsimd.tensor_tensor(prob2[:, h % 2, 1], prob[:, h % 2],
                                        prob2[:, h % 2, 0].bitcast(F32), ALU.subtract).then_inc(prob_low, 1)

            def att_lower(b, m):
                eng.wait_ge(att_high, KI * b + m + 1)
                at_least(eng, out_ok, b)
                nc.gpsimd.tensor_tensor(att2[:, 1, m], att[:, m], att2[:, 0, m].bitcast(F32),
                                        ALU.subtract).then_inc(att_low, 1)

            def residual(b, p):
                eng.wait_ge(xr_in[p], 16 * (b // 2 + 1))
                at_least(eng, x1_ok, QT * b)
                nc.gpsimd.tensor_tensor(xb[:], xr[:, p], bo[:].unsqueeze(1).to_broadcast([P, QT, D]),
                                        ALU.add).then_inc(xb_ok, 1)

            def norm1(b):
                at_least(eng, x1_ok, QT * b)
                rsqrt(b, mv1, mv1_ok, QT, var1, var1_ok, rs1, rs1_ok, ((0, QT, P, 1.0, EPS),))

            def norm2(b):
                rsqrt(b, mv2, mv2_ok, QT, var2, var2_ok, rs2, rs2_ok, ((0, QT, P, 1.0, EPS),))

            def dispatch(b, p, lo, hi):
                if lo == 0:
                    eng.wait_ge(route, N_ROUTE * (b + 1))
                    by_itself(eng, waited)
                for n in range(lo, hi):
                    nc.gpsimd.indirect_dma_start(
                        out=t["slots"], out_offset=bass.IndirectOffsetOnAxis(ap=sidx[:, p, n:n + 1], axis=0),
                        in_=x2h[:, p, n // 2], in_offset=None, bounds_check=E0 * SLOTS - 1,
                        oob_is_err=False).then_inc(sent[p], 16)

            norm(0)
            norm(1)
            eng.wait_ge(zeroed, 16 * (E0 * SLOTS // (P * 10)))
            eng.wait_ge(const_ok, N_CONST)

            def step(b, p):
                first, last = isinstance(b, int) and b == 0, isinstance(b, int) and b == B - 1
                last2 = isinstance(b, int) and b >= B - 2
                first2 = isinstance(b, int) and b < 2
                for h in range(H0):
                    prob_lower(b, h)
                    if not first:
                        if h == 0:
                            att_lower(b - 1, KI - 2)
                            att_lower(b - 1, KI - 1)
                            residual(b - 1, 1 - p)
                        if h == 1:
                            norm1(b - 1)
                        if h == 2:
                            norm2(b - 1)
                    if h in (6, 7):
                        att_lower(b, h - 6)
                    if h == 6 and not last2:
                        norm(b + 2)
                    if h in (3, 4, 5, 7) and not first2:
                        n = (3, 4, 5, 7).index(h)
                        dispatch(b - 2, p, n, n + 1)

            batches(eng, step)
            att_lower(B - 1, KI - 2)
            att_lower(B - 1, KI - 1)
            dispatch(B - 2, 0, 0, 2 * QT)
            residual(B - 1, 1)
            norm1(B - 1)
            norm2(B - 1)
            dispatch(B - 1, 1, 0, 2 * QT)
            for p in range(2):
                eng.wait_ge(sent[p], 16 * 2 * QT * (B // 2))

        @block.scalar
        def _(eng):
            eng.wait_ge(w_in[0], 16)
            nc.scalar.activation(wq[:, 0], stage_q, ACT.Copy).then_inc(w_high, 1)
            eng.wait_ge(w_in[1], 16)
            nc.scalar.activation(wkv[:, 0], stage_kv[:], ACT.Copy).then_inc(w_high, 1)
            eng.wait_ge(first_in, 16 * N_FIRST)

            def affine(b, part):
                source, lo, hi, shift, gain = ((proj[1], C, NKV, 1, 0), (proj[0], 0, C, 3, 2))[part]
                at_least(eng, kvin_low, 2 * b)
                at_least(eng, proj_ok, NU * b)
                eng.wait_ge(xT_ok, 2 * b + part + 1)
                for dst in (kvin, kvin2[:, 0]):
                    for k in range(KD):
                        nc.scalar.activation(dst[:, k, lo:hi], source[:, k * (hi - lo):(k + 1) * (hi - lo)],
                                             ACT.Identity, bias=aff[:, shift, k:k + 1],
                                             scale=aff[:, gain, k:k + 1]).then_inc(kvin_ok, 1)

            def high(b, p, u):
                eng.wait_ge(proj_ok, NU * b + u + 1)
                src, dst, scale = projection(p, u, 0)
                if u == 0:
                    at_least(eng, score_ok, 2 * H0 * (b - 1))
                if u == N_QK:
                    at_least(eng, ctxv_ok, H0 * (b - 1))
                nc.scalar.activation(dst, src, ACT.Copy, scale=scale).then_inc(proj_high, 1)

            def maxima(b, p):
                eng.wait_ge(nmT_ok, b + 1)
                at_least(eng, score_ok, 2 * H0 * (b - 1))
                for row in (0, 64):
                    nc.scalar.activation(nmaxT[row:row + H0, p], probe[0][0:H0, 0:S], ACT.Copy).then_inc(nmT_out, 1)

            def exps(b, q, h):
                p = h % 2
                at_least(eng, prob_low, H0 * b + h - 1)
                at_least(eng, ctxv_ok, H0 * b + h - 1)
                eng.wait_ge(score_ok, 2 * (H0 * b + h) + 1)
                nc.scalar.activation(prob[:, p, 0:2], score_x[:], ACT.Exp).then_inc(exp_ok, 1)
                nc.scalar.activation(prob2[:, p, 0, 0:2], score_x[:], ACT.Exp).then_inc(exp_ok, 1)
                eng.wait_ge(score_ok, 2 * (H0 * b + h) + 2)
                if h == 0:
                    eng.wait_ge(mrow_ok, 2 * (b + 1))
                bias = mask_col[:, q:q + 1]
                nc.scalar.activation(prob[0:C, p, 2], score_c[0:C, 0:S], ACT.Exp, bias=bias).then_inc(exp_ok, 1)
                nc.scalar.activation(prob2[0:C, p, 0, 2], score_c[0:C, 0:S], ACT.Exp, bias=bias).then_inc(exp_ok, 1)

            def evacuate(b, h):
                mine, sums = (slice(0, 64), slice(64, 128)) if h % 2 == 0 else (slice(64, 128), slice(0, 64))
                m = h // 2
                eng.wait_ge(ctxv_ok, H0 * b + h + 1)
                if h % 2 == 0:
                    at_least(eng, att_ok, KI * b + m - 1)
                    at_least(eng, att_low, KI * (b - 1) + m + 1)
                nc.scalar.activation(den[mine, m % 2], ctxv[sums, 0:S], ACT.Copy).then_inc(evac_ok, 1)
                nc.scalar.activation(att[mine, m], ctxv[mine, 0:S], ACT.Copy).then_inc(evac_ok, 1)

            def att_higher(b, m):
                eng.wait_ge(att_ok, KI * b + m + 1)
                at_least(eng, out_ok, b)
                nc.scalar.activation(att2[:, 0, m], att[:, m], ACT.Copy).then_inc(att_high, 1)

            def router_in(b):
                eng.wait_ge(rT_ok, b + 1)
                nc.scalar.activation(rT[:], misc[:], ACT.Copy).then_inc(rT_out, 1)

            def router_exp(b):
                eng.wait_ge(soft, N_SOFT * b + 3)
                nc.scalar.activation(le[:], lg[:], ACT.Exp).then_inc(le_ok, 1)

            affine(0, 0)
            affine(0, 1)
            eng.wait_ge(small_in, 16 * N_SMALL)
            nc.scalar.activation(tgate[:], gate[:], ACT.Tanh).then_inc(gate_ok, 1)
            for u in range(NU - 1):
                high(0, 0, u)
            eng.wait_ge(w_in[2], 16)
            nc.scalar.activation(wo[:, 0], stage_o, ACT.Copy).then_inc(w_high, 1)
            eng.wait_ge(const_ok, N_CONST)
            maxima(0, 0)

            def step(b, p):
                first, last = isinstance(b, int) and b == 0, isinstance(b, int) and b == B - 1
                for h in range(H0):
                    exps(b, p, h)
                    if h == 0:
                        high(b, p, NU - 1)
                        if not first:
                            evacuate(b - 1, H0 - 1)
                        if not last:
                            affine(b + 1, 0)
                        if not first:
                            att_higher(b - 1, KI - 2)
                            att_higher(b - 1, KI - 1)
                        if not last:
                            affine(b + 1, 1)
                    else:
                        if not last:
                            for u in MADE[h]:
                                high(b + 1, 1 - p, u)
                            if h == 7:
                                maxima(b + 1, 1 - p)
                        if not first:
                            if h == 4:
                                router_in(b - 1)
                            if h == 5:
                                router_exp(b - 1)
                        evacuate(b, h - 1)
                    if h in (5, 7):
                        att_higher(b, h // 2 - 2)

            batches(eng, step)
            evacuate(B - 1, H0 - 1)
            att_higher(B - 1, KI - 2)
            att_higher(B - 1, KI - 1)
            router_in(B - 1)
            router_exp(B - 1)

        @block.vector
        def _(eng):
            def stat(b, p):
                eng.wait_ge(xn_in[p], 16 * (b // 2 + 1))
                eng.wait_ge(cn_in[p], 16 * (b // 2 + 1))
                at_least(eng, xh_ok, 3 * b)
                for k in range(QT):
                    nc.vector.bn_stats(stats[:, k], xn[:, p, k]).then_inc(stats_ok, 1)
                nc.vector.bn_stats(stats[0:C, 2], cn[0:C, p]).then_inc(stats_ok, 1)
                eng.wait_ge(stats_ok, 3 * (b + 1))
                by_itself(eng, waited)
                for k, rows in ((0, P), (1, P), (2, C)):
                    nc.vector.bn_aggr(mv[0:rows, k], stats[0:rows, k]).then_inc(mv_ok, 1)

            def normalise(b, p):
                eng.wait_ge(rs_ok, b + 1)
                at_least(eng, xT_ok, 2 * b)
                for k in range(QT):
                    nc.vector.tensor_scalar(xh[:, k], xn[:, p, k], mv[:, k, 0:1], rs[:, k:k + 1],
                                            ALU.subtract, ALU.mult).then_inc(xh_ok, 1)
                nc.vector.tensor_scalar(xh[0:C, 2], cn[0:C, p], mv[0:C, 2, 0:1], rs[0:C, 2:3],
                                        ALU.subtract, ALU.mult).then_inc(xh_ok, 1)

            def kvin_lower(b):
                at_least(eng, proj_ok, NU * b)
                for lo, hi, made in ((C, NKV, 4), (0, C, 8)):
                    eng.wait_ge(kvin_ok, 8 * b + made)
                    nc.vector.tensor_tensor(kvin2[:, 1, :, lo:hi], kvin[:, :, lo:hi],
                                            kvin2[:, 0, :, lo:hi].bitcast(F32), ALU.subtract) \
                        .then_inc(kvin_low, 1)

            def lower(b, p, u):
                eng.wait_ge(proj_high, NU * b + u + 1)
                src, dst, scale = projection(p, u, 1)
                high = projection(p, u, 0)[1].bitcast(F32)
                if scale == 1.0:
                    low = nc.vector.tensor_tensor(dst, src, high, ALU.subtract)
                else:
                    low = nc.vector.scalar_tensor_tensor(dst, src, scale, high, ALU.mult, ALU.subtract)
                low.then_inc(proj_low, 1)

            def mask_line(b, p):
                at_least(eng, probe_ok, 16 * (b - 1))
                at_least(eng, exp_ok, 4 * H0 * (b - 1))
                nc.vector.tensor_copy(mask_col[:, p:p + 1], mask_bias[:, bass.ds(b, 1)]).then_inc(mrow_ok, 1)
                nc.vector.tensor_scalar(mask_row[:, p], mask_u8[:, bass.ds(b, 1)].rearrange("p o c -> p (o c)"),
                                        -1.0, MASKED, ALU.add, ALU.mult).then_inc(mrow_ok, 1)

            def row_max(b, p, u):
                eng.wait_ge(probe_ok, 16 * b + u + 1)
                if u == 0:
                    at_least(eng, nmT_ok, b - 1)
                nc.vector.tensor_reduce(nmax[:, p, u % 2, u // 2:u // 2 + 1], probe[u % 2][:, 0:NKV], AX.X,
                                        ALU.max, negate=True).then_inc(nmax_ok, 1)

            def divide(b, m):
                eng.wait_ge(evac_ok, 2 * H0 * b + 4 * (m + 1))
                at_least(eng, att_ok, KI * b + m)
                nc.vector.reciprocal(rden[:], den[:, m % 2]).then_inc(rden_ok, 1)
                eng.wait_ge(rden_ok, KI * b + m + 1)
                nc.vector.tensor_tensor(att[:, m], att[:, m], rden[:], ALU.mult).then_inc(att_ok, 1)

            def out_stat(b):
                eng.wait_ge(out_ok, b + 1)
                for k in range(QT):
                    nc.vector.bn_stats(stats1[:, k], misc[:, k * D:(k + 1) * D]).then_inc(stats1_ok, 1)
                eng.wait_ge(stats1_ok, QT * (b + 1))
                by_itself(eng, waited)
                for k in range(QT):
                    nc.vector.bn_aggr(mv1[:, k], stats1[:, k]).then_inc(mv1_ok, 1)

            def out_norm(b, p):
                eng.wait_ge(rs1_ok, b + 1)
                for k in range(QT):
                    nc.vector.scalar_tensor_tensor(y1[:, k], misc[:, k * D:(k + 1) * D], mv1[:, k, 0:1], go[:],
                                                   ALU.subtract, ALU.mult).then_inc(y1_ok, 1)
                eng.wait_ge(xb_ok, b + 1)
                at_least(eng, x1_out[p], 16 * (b // 2))
                for k in range(QT):
                    eng.wait_ge(y1_ok, QT * b + k + 1)
                    nc.vector.scalar_tensor_tensor(x1[:, p, k], y1[:, k], rs1[:, k:k + 1], xb[:, k],
                                                   ALU.mult, ALU.add).then_inc(x1_ok, 1)

            def x1_stat(b, p):
                for k in range(QT):
                    eng.wait_ge(x1_ok, QT * b + k + 1)
                    nc.vector.bn_stats(stats2[:, k], x1[:, p, k]).then_inc(stats2_ok, 1)
                eng.wait_ge(stats2_ok, QT * (b + 1))
                by_itself(eng, waited)
                for k in range(QT):
                    nc.vector.bn_aggr(mv2[:, k], stats2[:, k]).then_inc(mv2_ok, 1)

            def x1_norm(b, p):
                eng.wait_ge(rs2_ok, b + 1)
                at_least(eng, sent[p], 16 * 2 * QT * (b // 2))
                for k in range(QT):
                    nc.vector.tensor_scalar(x2h[:, p, k], x1[:, p, k], mv2[:, k, 0:1], rs2[:, k:k + 1],
                                            ALU.subtract, ALU.mult).then_inc(x2h_ok, 1)

            def logits_in(b):
                step = 0

                def then(*instructions):
                    nonlocal step
                    step += len(instructions)
                    for instruction in instructions:
                        instruction.then_inc(soft, 1)
                    eng.wait_ge(soft, N_SOFT * b + step)

                eng.wait_ge(logit_ok, b + 1)
                then(nc.vector.tensor_tensor(lg[:], misc[:, 0:QT * E0].rearrange("p (t e) -> p t e", t=QT),
                                             br[:].unsqueeze(1).to_broadcast([P, QT, E0]), ALU.add))
                then(nc.vector.tensor_reduce(lmax[:], lg[:], AX.X, ALU.max))
                then(nc.vector.tensor_tensor(lg[:], lg[:], lmax[:].unsqueeze(2).to_broadcast([P, QT, E0]),
                                             ALU.subtract))

            def choose(b):
                step = 3

                def then(*instructions):
                    nonlocal step
                    step += len(instructions)
                    for instruction in instructions:
                        instruction.then_inc(soft, 1)
                    eng.wait_ge(soft, N_SOFT * b + step)

                at_least(eng, count_ok, b)
                eng.wait_ge(le_ok, b + 1)
                then(nc.vector.reduce_sum(lsum[:], le[:], AX.X))
                then(nc.vector.reciprocal(lsum[:], lsum[:]))
                then(nc.vector.tensor_tensor(pr[:], le[:], lsum[:].unsqueeze(2).to_broadcast([P, QT, E0]), ALU.mult))
                by_itself(eng, waited)
                then(*[nc.vector.max(top[:, k], pr[:, k]) for k in range(QT)])
                by_itself(eng, waited)
                then(*[nc.vector.max_index(topi[:, k], top[:, k], pr[:, k]) for k in range(QT)])
                then(nc.vector.tensor_copy(topf[:], topi[:, :, 0:2]))
                then(*[nc.vector.tensor_tensor(oh[:, k], iota_e[:].unsqueeze(1).to_broadcast([P, 2, E0]),
                                               topf[:, k].unsqueeze(2).to_broadcast([P, 2, E0]), ALU.is_equal)
                       for k in range(QT)])
                then(nc.vector.tensor_tensor(ohs[:], oh[:, :, 0], oh[:, :, 1], ALU.add))
                assert step == N_SOFT

            def place(b, p):
                step = 0

                def then(*instructions):
                    nonlocal step
                    step += len(instructions)
                    for instruction in instructions:
                        instruction.then_inc(route, 1)
                    eng.wait_ge(route, N_ROUTE * b + step)

                at_least(eng, sent[p], 16 * 2 * QT * (b // 2))
                eng.wait_ge(count_ok, b + 1)
                counts = probe[1][:, 0:QT * E0].rearrange("p (t e) -> p t e", t=QT)
                eng.wait_ge(soft, N_SOFT * (b + 1))
                first_row = slot0[:, bass.ds(b, 1)].rearrange("p o e -> p (o e)")
                then(nc.vector.tensor_tensor(at_e[:], oh[:], counts.unsqueeze(2).to_broadcast([P, QT, 2, E0]),
                                             ALU.mult),
                     nc.vector.tensor_tensor(at_b[:].rearrange("p t k e -> p (t k) e"),
                                             oh[:].rearrange("p t k e -> p (t k) e"),
                                             first_row.unsqueeze(1).to_broadcast([P, QT * 2, E0]), ALU.mult))
                then(nc.vector.reduce_sum(pos[:], at_e[:], AX.X),
                     nc.vector.reduce_sum(base[:], at_b[:], AX.X))
                then(nc.vector.tensor_scalar(kept[:], pos[:], float(CAP), None, ALU.is_lt),
                     nc.vector.scalar_tensor_tensor(slot[:], pos[:], float(CAP - 1), base[:], ALU.min, ALU.add))
                then(nc.vector.tensor_scalar(slot_s[:], kept[:], -float(NOWHERE), float(NOWHERE), ALU.mult, ALU.add),
                     nc.vector.tensor_tensor(wsel[:], top[:, :, 0:2], kept[:], ALU.mult))
                then(nc.vector.tensor_tensor(sidx[:, p], slot[:].rearrange("p t k -> p (t k)"),
                                             slot_s[:].rearrange("p t k -> p (t k)"), ALU.add),
                     nc.vector.tensor_scalar(keep["weight"][:, bass.ds(b, 1)].rearrange("p o n -> p (o n)"),
                                             wsel[:].rearrange("p t k -> p (t k)"), tgate[:, 2:3], None, ALU.mult),
                     nc.vector.tensor_copy(keep["row"][:, bass.ds(b, 1)].rearrange("p o n -> p (o n)"),
                                           slot[:].rearrange("p t k -> p (t k)")))
                assert step == N_ROUTE

            stat(0, 0)
            nc.vector.memset(prob[:, :, 2], 0.0).then_inc(const_ok, 1)
            nc.vector.memset(prob2[:, :, 0, 2].bitcast(F32), 0.0).then_inc(const_ok, 1)
            nc.vector.memset(nmaxT[:].bitcast(F32), 0.0).then_inc(const_ok, 1)
            normalise(0, 0)
            nc.vector.memset(vo[:, :, 0, :, :, 1].bitcast(F32), 1.0).then_inc(const_ok, 1)
            nc.vector.memset(vo[:, :, 1, :, :, 1].bitcast(F32), 0.0).then_inc(const_ok, 1)

            def weights_lower(n, both, whole):
                eng.wait_ge(w_high, n + 1)
                nc.vector.tensor_tensor(both[:, 1], whole, both[:, 0].bitcast(F32), ALU.subtract) \
                    .then_inc(w_low, 1)

            weights_lower(0, wq, stage_q)
            weights_lower(1, wkv, stage_kv[:])
            kvin_lower(0)
            stat(1, 1)
            eng.wait_ge(small_in, 16 * N_SMALL)
            nc.vector.tensor_copy(headrow[:], headrow_f[:]).then_inc(const_ok, 1)
            nc.vector.tensor_scalar(mask_bias[:], mask_t8[:], -1.0, MASKED, ALU.add, ALU.mult).then_inc(const_ok, 1)
            for u in range(NU - 1):
                lower(0, 0, u)
                if u == 2:
                    normalise(1, 1)
            eng.wait_ge(gate_ok, 1)
            nc.vector.tensor_scalar(go[:], go[:], tgate[:, 0:1], None, ALU.mult).then_inc(const_ok, 1)
            nc.vector.tensor_scalar(bo[:], bo[:], tgate[:, 0:1], None, ALU.mult).then_inc(const_ok, 1)
            eng.wait_ge(const_ok, N_CONST - 1)
            nc.vector.tensor_copy(keep["gate"][:], tgate[:]).then_inc(const_ok, 1)
            mask_line(0, 0)
            for u in range(16):
                row_max(0, 0, u)
            weights_lower(2, wo, stage_o)

            def step(b, p):
                first, last = isinstance(b, int) and b == 0, isinstance(b, int) and b == B - 1
                last2 = isinstance(b, int) and b >= B - 2
                n, q, r = b + 1, 1 - p, b - 1
                if not first:
                    divide(r, KI - 2)
                lower(b, p, NU - 1)
                if not last:
                    mask_line(n, q)
                if not first:
                    divide(r, KI - 1)
                if not last:
                    kvin_lower(n)
                if not (isinstance(b, int) and b < 2):
                    place(b - 2, p)
                if not first:
                    out_stat(r)
                if not first:
                    out_norm(r, q)
                if not first:
                    x1_stat(r, q)
                if not last:
                    lower(n, q, 0)
                if not last:
                    lower(n, q, 1)
                for h in range(3, H0):
                    u = 4 * (h - 3)
                    made = list(MADE[h])
                    if not last:
                        if h < 7:
                            row_max(n, q, u)
                            row_max(n, q, u + 1)
                        if made:
                            lower(n, q, made.pop(0))
                    if not first and h == 3:
                        x1_norm(r, q)
                    if not last:
                        if h < 7:
                            row_max(n, q, u + 2)
                            row_max(n, q, u + 3)
                        for v in made:
                            lower(n, q, v)
                    if not first and h == 5:
                        logits_in(r)
                    if not last2 and h == 7:
                        normalise(b + 2, p)
                    if not first and h == 6:
                        choose(r)
                    if h in (4, 6):
                        divide(b, h // 2 - 2)
                    if not last2 and h == 4:
                        stat(b + 2, p)

            batches(eng, step)
            divide(B - 1, KI - 2)
            divide(B - 1, KI - 1)
            place(B - 2, 0)
            out_stat(B - 1)
            out_norm(B - 1, 1)
            x1_stat(B - 1, 1)
            x1_norm(B - 1, 1)
            logits_in(B - 1)
            choose(B - 1)
            place(B - 1, 1)

        @block.tensor
        def _(eng):
            def turn(b):
                eng.wait_ge(xh_ok, 3 * (b + 1))
                at_least(eng, proj_low, NU * b - 1)
                for k in range(KD):
                    for i in range(QT):
                        last = nc.tensor.transpose(proj[1][:, k * S + i * P:k * S + (i + 1) * P],
                                                   xh[:, i, k * P:(k + 1) * P], ident[:])
                last.then_inc(xT_ok, 1)
                at_least(eng, proj_low, NU * b)
                for k in range(KD):
                    last = nc.tensor.transpose(proj[0][:, k * C:(k + 1) * C],
                                               xh[0:C, 2, k * P:(k + 1) * P], ident[0:C, 0:C])
                last.then_inc(xT_ok, 1)

            def project(b, u):
                if u == 0:
                    eng.wait_ge(kvin_low, 2 * (b + 1))
                    eng.wait_ge(kvin_ok, 8 * (b + 1))
                if u >= 2:
                    eng.wait_ge(proj_low, NU * b + u - 1)
                out = proj[u % 2]
                kind, i = UNITS[u]
                if kind == "q":
                    for m in range(2):
                        cols = slice((2 * i + m) * P, (2 * i + m + 1) * P)
                        last = split_product(nc, out[:, m * S:(m + 1) * S], lambda a, k: wq[:, a, k, cols],
                                             lambda a, k: kvin2[:, a, k, C:NKV], KD)
                elif kind == "k":
                    cols = slice(i * P, (i + 1) * P)
                    last = split_product(nc, out[:, 0:NKV], lambda a, k: wkv[:, a, k, cols],
                                         lambda a, k: kvin2[:, a, k, :], KD)
                else:
                    lo, hi = ((C, C + P), (C + P, NKV), (0, C))[i]
                    last = split_product(nc, out[0:hi - lo, :], lambda a, k: kvin2[:, a, k, lo:hi],
                                         lambda a, k: wkv[:, a, k, INNER:], KD)
                last.then_inc(proj_ok, 1)

            def probe_max(b, p, u):
                h, i = u // 2, u % 2
                rows = slice(64 * (h % 2), 64 * (h % 2) + 64)
                if i == 0:
                    both = max(unit("q", h // 4), unit("k", h // 2))
                    eng.wait_ge(proj_high, NU * b + both + 1)
                if u == 1:
                    at_least(eng, route, N_ROUTE * (b - 2))
                if u == 0:
                    eng.wait_ge(mrow_ok, 2 * (b + 1))
                    at_least(eng, nmT_out, 2 * b)
                at_least(eng, nmax_ok, 16 * b + u - 1)
                nc.tensor.matmul(probe[i][:, 0:NKV], qT[rows, p, 0, h // 2, i * P:(i + 1) * P],
                                 kT[rows, p, 0, h // 2, :], start=True, stop=False)
                nc.tensor.matmul(probe[i][:, 0:C], firstrow[rows], mask_row[rows, p], start=False, stop=True) \
                    .then_inc(probe_ok, 1)

            def turn_max(b, p):
                eng.wait_ge(nmax_ok, 16 * (b + 1))
                for i in range(QT):
                    last = nc.tensor.transpose(probe[0][0:H0, i * P:(i + 1) * P], nmax[:, p, i], ident[:])
                last.then_inc(nmT_ok, 1)

            def score(b, p, h):
                rows = slice(64 * (h % 2), 64 * (h % 2) + 64)
                if h == 0:
                    eng.wait_ge(nmT_out, 2 * (b + 1))
                    eng.wait_ge(proj_low, NU * b + N_QK)
                for i, lo, hi in ((0, C, C + P), (1, C + P, NKV), (2, 0, C)):
                    out = score_x[:, i] if i < 2 else score_c[0:C, 0:S]
                    if i != 1:
                        at_least(eng, exp_ok, 4 * (H0 * b + h) - (2 if i == 0 else 0))
                    nc.tensor.matmul(out, headrow[rows, h, 0:hi - lo], nmaxT[rows, p], start=True, stop=False)
                    last = split_product(nc, out, lambda a, _: kT[rows, p, a, h // 2, lo:hi],
                                         lambda a, _: qT[rows, p, a, h // 2, :], 1, start=False)
                    if i >= 1:
                        last.then_inc(score_ok, 1)

            def times_v(b, p, h):
                eng.wait_ge(prob_low, H0 * b + h + 1)
                at_least(eng, evac_ok, 2 * (H0 * b + h))
                if h == 0:
                    eng.wait_ge(proj_low, NU * (b + 1))
                first = 64 * (h % 2)

                def v_and_ones(a, i):
                    rows = P if i < 2 else C
                    return vo[0:rows, p, a, i, h // 2].rearrange("p c d -> p (c d)")[:, first:first + P]

                split_product(nc, ctxv[:, 0:S], v_and_ones,
                              lambda a, i: prob2[0:P if i < 2 else C, h % 2, a, i], 3).then_inc(ctxv_ok, 1)

            def output(b):
                if isinstance(b, int) and b == 0:
                    eng.wait_ge(w_low, 3)
                at_least(eng, soft, N_SOFT * b)
                for i in range(QT):
                    for k in range(KI):
                        if i == 0:
                            eng.wait_ge(att_low, KI * b + k + 1)
                        last = split_product(nc, misc[:, i * D:(i + 1) * D],
                                             lambda a, _: att2[:, a, k, i * P:(i + 1) * P],
                                             lambda a, _: wo[:, a, k], 1, start=k == 0, stop=k == KI - 1)
                last.then_inc(out_ok, 1)

            def router_turn(b, p):
                eng.wait_ge(x2h_ok, QT * (b + 1))
                eng.wait_ge(y1_ok, QT * (b + 1))
                for k in range(KD):
                    for i in range(QT):
                        last = nc.tensor.transpose(misc[:, k * S + i * P:k * S + (i + 1) * P],
                                                   x2h[:, p, i, k * P:(k + 1) * P], ident[:])
                last.then_inc(rT_ok, 1)

            def router_logits(b):
                eng.wait_ge(rT_out, b + 1)
                for i in range(QT):
                    for k in range(KD):
                        last = nc.tensor.matmul(misc[:, i * E0:(i + 1) * E0], rT[:, k, i * P:(i + 1) * P],
                                                wr[:, k], start=k == 0, stop=k == KD - 1)
                last.then_inc(logit_ok, 1)

            def router_count(b):
                eng.wait_ge(soft, N_SOFT * (b + 1))
                for i in range(QT):
                    for k in range(i + 1):
                        last = nc.tensor.matmul(probe[1][:, i * E0:(i + 1) * E0], tri[:, 0 if k == i else 1],
                                                ohs[:, k], start=k == 0, stop=k == i)
                last.then_inc(count_ok, 1)

            eng.wait_ge(first_in, 16 * N_FIRST)
            turn(0)
            eng.wait_ge(w_low, 2)
            for u in range(NU - 1):
                project(0, u)
            eng.wait_ge(small_in, 16 * N_SMALL)
            eng.wait_ge(const_ok, N_CONST)
            for u in range(16):
                probe_max(0, 0, u)
            turn_max(0, 0)

            def step(b, p):
                first, last = isinstance(b, int) and b == 0, isinstance(b, int) and b == B - 1
                n, q, r = b + 1, 1 - p, b - 1
                for h in range(H0):
                    u = 4 * (h - 3)
                    probes = 3 <= h < 7 and not last
                    made = list(MADE[h]) if not last else []
                    score(b, p, h)
                    if h == 0:
                        project(b, NU - 1)
                        if not first:
                            times_v(r, q, H0 - 1)
                        if not last:
                            turn(n)
                    if h == 1:
                        times_v(b, p, 0)
                        if not first:
                            output(r)
                    if probes:
                        probe_max(n, q, u)
                        probe_max(n, q, u + 1)
                    if made:
                        project(n, made.pop(0))
                    if h == 4 and not first:
                        router_turn(r, q)
                    if probes:
                        probe_max(n, q, u + 2)
                        probe_max(n, q, u + 3)
                    for v in made:
                        project(n, v)
                    if h == 7 and not last:
                        turn_max(n, q)
                    if not first and h == 7:
                        router_count(r)
                    if h > 1:
                        times_v(b, p, h - 1)
                    if not first and h == 4:
                        router_logits(r)

            batches(eng, step)
            times_v(B - 1, 1, H0 - 1)
            output(B - 1)
            router_turn(B - 1, 1)
            router_logits(B - 1)
            router_count(B - 1)


N_FIRST = 5
N_SMALL = 13
N_CONST = 10


CH = 2 * P
NC = SLOTS // CH
PIECES = 4

LATE = (("WqT", KD * D), ("WkT", KD * D), ("WvT", KD * D), ("WoT", KD * D),
        ("Wg", EM * KD * P), ("Wu", EM * KD * P), ("Wd", EM * D), ("Wr1", KD * E1))
LATE_AT = {name: sum(size for _, size in LATE[:n]) for n, (name, _) in enumerate(LATE)}
LATE_SIZE = sum(size for _, size in LATE)


def experts(nc, t, keep):
    ctx = ExitStack()
    with ctx:
        def sb(name, shape, dt=F32):
            return ctx.enter_context(nc.sbuf_tensor(name, shape, dt))

        def pb(name, shape):
            return ctx.enter_context(nc.psum_tensor(name, shape, F32))

        sems = []

        def sem(name):
            sems.append(ctx.enter_context(nc.semaphore(name)))
            return sems[-1]

        w1_in = keep["w1_in"]
        w2_in = sb("e_w2_in", [P, KH, D])
        w1 = sb("e_w1", [P, 2, 2, KD, HID], F32R)
        w2 = sb("e_w2", [P, 2, 2, KH, D], F32R)
        b1 = sb("e_b1", [P, KH, E0])
        b2 = sb("e_b2", [P, E0, D])
        ident = sb("e_ident", [P, P])
        rows = sb("e_rows", [P, 2, 2, D])
        rowsT = sb("e_rowsT", [P, 2, 2, KD, CH], F32R)
        hidden = sb("e_hidden", [P, KH, CH])
        hidden2 = sb("e_hidden2", [P, 2, 2, KH, CH], F32R)
        y = sb("e_y", [P, 2, 2, D])

        turned = pb("e_turned", [P, KD * CH])
        first = pb("e_first", [P, 4, 512])
        second = [pb(f"e_second{i}", [P, 2, D]) for i in range(2)]

        ident_in, small_in = sem("e_ident_in"), sem("e_small_in")
        w_in = [sem(f"e_w_in{i}") for i in range(PIECES)]
        waited = sem("e_waited")
        w_high, w_low = sem("e_w_high"), sem("e_w_low")
        rows_in = [sem(f"e_rows_in{i}") for i in range(2)]
        turned_ok, rows_high, rows_low = sem("e_turned_ok"), sem("e_rows_high"), sem("e_rows_low")
        first_ok, relu_ok, hid_high, hid_low = (sem("e_" + s) for s in
                                                ("first_ok", "relu_ok", "hid_high", "hid_low"))
        second_ok, y_ok = sem("e_second_ok"), sem("e_y_ok")
        y_out = [sem(f"e_y_out{i}") for i in range(2)]
        late_w = sb("e_late_w", [P, LATE_SIZE])
        late = keep["late"]
        late_in, late_high, late_low = keep["late_in"], keep["late_high"], keep["late_low"]

        def late_piece(n):
            cols = slice(n * LATE_SIZE // PIECES, (n + 1) * LATE_SIZE // PIECES)
            return late_w[:, cols], late[:, 0, cols], late[:, 1, cols]

        def piece(p, n, plane):
            if n < 2:
                return w1_in[:, n], w1[:, p, plane, n]
            half = slice((n - 2) * KH // 2, (n - 1) * KH // 2)
            return w2_in[:, half], w2[:, p, plane, half]

        def rounds(eng, step):
            def pair(e0, last):
                for p in range(2):
                    for c in range(NC):
                        step((e0 + p) * NC + c, e0 + p, p, c, (p * NC + c) % 2,
                             NC * (1 - p) + NC - 1 - c if last else NC)
            pair(0, False)
            with eng.Fori(1, E0 // 2 - 1) as n:
                pair(n * 2, False)
            pair(E0 - 2, True)

        ctx.callback(zero_semaphores, nc, sems)
        block = ctx.enter_context(nc.Block())

        @block.sync
        def _(eng):
            def load_piece(e, n):
                at_least(eng, w_low, PIECES * (e - 1) + n + 1)
                if n < 2:
                    src = t["W1"][bass.ds(e, 1), n * P:(n + 1) * P].rearrange("o p h -> p (o h)")
                else:
                    rows_of = slice((n - 2) * HID // 2, (n - 1) * HID // 2)
                    src = t["W2"][bass.ds(e, 1), rows_of].rearrange("o (k p) d -> p (o k) d", p=P)
                eng.dma_start(piece(0, n, 0)[0], src).then_inc(w_in[n], 16)

            def load_rows(g, q):
                at_least(eng, turned_ok, g - 1)
                eng.dma_start(rows[:, q], t["slots"][bass.ts(g, CH)].rearrange("(k p) d -> p k d", p=P)) \
                    .then_inc(rows_in[q], 16)

            load_rows(0, 0)
            eng.dma_start(ident[:], t["ident"]).then_inc(ident_in, 16)
            load_rows(1, 1)
            for n in range(KD, PIECES):
                load_piece(0, n)
            for dst, src in ((b1[:], t["b1"]), (b2[:], t["b2"].partition_broadcast(P))):
                eng.dma_start(dst, src).then_inc(small_in, 16)
            load_rows(2, 0)
            for n in range(PIECES):
                load_piece(1, n)
            for name, size in LATE:
                dst = late_w[:, LATE_AT[name]:LATE_AT[name] + size]
                if name in ("Wg", "Wu"):
                    src = t[name].rearrange("e (k p) i -> p (e k) i", p=P)
                    dst = dst.rearrange("p (n i) -> p n i", i=P)
                elif name == "Wd":
                    src, dst = t[name].rearrange("e p d -> p e d"), dst.rearrange("p (e d) -> p e d", e=EM)
                else:
                    src = t[name].rearrange("(k p) d -> p k d", p=P)
                    dst = dst.rearrange("p (k d) -> p k d", k=KD)
                eng.dma_start(dst, src).then_inc(late_in, 16)

            def step(g, e, p, c, q, left):
                if left >= 3:
                    load_rows(g + 3, 1 - q)
                eng.wait_ge(y_ok, g + 1)
                eng.dma_start(t["answers"][bass.ts(g, CH)].rearrange("(k p) d -> p k d", p=P), y[:, q]) \
                    .then_inc(y_out[q], 16)
                if c < PIECES and not (isinstance(e, int) and e + 2 >= E0):
                    load_piece(e + 2, c)

            rounds(eng, step)
            for q in range(2):
                eng.wait_ge(y_out[q], 16 * (E0 * NC // 2))

        @block.scalar
        def _(eng):
            def split(e, p, n):
                if isinstance(e, int) and e == 0 and n < KD:
                    eng.wait_ge(keep["w1_loaded"], 16 * KD)
                else:
                    eng.wait_ge(w_in[n], 16 * (e + 1 if n >= KD else e))
                if n == 0:
                    at_least(eng, second_ok, NC * (e - 1))
                src, dst = piece(p, n, 0)
                nc.scalar.activation(dst, src, ACT.Copy).then_inc(w_high, 1)

            def rows_higher(g, q):
                eng.wait_ge(turned_ok, g + 1)
                at_least(eng, first_ok, 4 * (g - 1))
                nc.scalar.activation(rowsT[:, q, 0], turned[:], ACT.Copy).then_inc(rows_high, 1)

            def relu(g, e, j):
                eng.wait_ge(first_ok, 4 * g + j + 1)
                at_least(eng, hid_low, 4 * (g - 1) + j + 1)
                by_itself(eng, waited)
                for i in range(2):
                    nc.scalar.activation(hidden[:, 2 * j + i], first[:, j, i * CH:(i + 1) * CH], ACT.Relu,
                                         bias=b1[:, 2 * j + i, bass.ds(e, 1)]).then_inc(relu_ok, 1)

            split(0, 0, 0)
            split(0, 0, 1)
            rows_higher(0, 0)
            rows_higher(1, 1)
            split(0, 0, 2)
            split(0, 0, 3)
            eng.wait_ge(small_in, 32)
            for j in range(4):
                relu(0, 0, j)

            def step(g, e, p, c, q, left):
                if left >= 1:
                    for j in range(4):
                        relu(g + 1, e if c < NC - 1 else e + 1, j)
                if left >= 2:
                    rows_higher(g + 2, q)
                if c < PIECES and left >= NC:
                    split(e + 1, 1 - p, c)
                elif c < PIECES:
                    eng.wait_ge(late_in, 16 * len(LATE))
                    nc.scalar.activation(late_piece(c)[1], late_piece(c)[0], ACT.Copy).then_inc(late_high, 1)

            rounds(eng, step)

        @block.vector
        def _(eng):
            def split(e, p, n):
                eng.wait_ge(w_high, PIECES * e + n + 1)
                src, dst = piece(p, n, 1)
                nc.vector.tensor_tensor(dst, src, piece(p, n, 0)[1].bitcast(F32), ALU.subtract).then_inc(w_low, 1)

            def rows_lower(g, q):
                eng.wait_ge(rows_high, g + 1)
                nc.vector.tensor_tensor(rowsT[:, q, 1], turned[:].rearrange("p (k s) -> p k s", k=KD),
                                        rowsT[:, q, 0].bitcast(F32), ALU.subtract).then_inc(rows_low, 1)

            def hidden_split(g, q, j):
                eng.wait_ge(relu_ok, 8 * g + 2 * j + 2)
                at_least(eng, second_ok, g - 1)
                mine = slice(2 * j, 2 * j + 2)
                nc.vector.tensor_copy(hidden2[:, q, 0, mine], hidden[:, mine]).then_inc(hid_high, 1)
                eng.wait_ge(hid_high, 4 * g + j + 1)
                nc.vector.tensor_tensor(hidden2[:, q, 1, mine], hidden[:, mine],
                                        hidden2[:, q, 0, mine].bitcast(F32), ALU.subtract).then_inc(hid_low, 1)

            def answer(g, e, q):
                eng.wait_ge(second_ok, g + 1)
                at_least(eng, y_out[q], 16 * (g // 2))
                nc.vector.tensor_tensor(y[:, q], second[q][:], b2[:, bass.ds(e, 1)].to_broadcast([P, 2, D]),
                                        ALU.add).then_inc(y_ok, 1)

            split(0, 0, 0)
            split(0, 0, 1)
            rows_lower(0, 0)
            rows_lower(1, 1)
            split(0, 0, 2)
            split(0, 0, 3)
            eng.wait_ge(small_in, 32)
            for j in range(4):
                hidden_split(0, 0, j)

            def step(g, e, p, c, q, left):
                if left >= 1:
                    for j in range(4):
                        hidden_split(g + 1, 1 - q, j)
                if left >= 2:
                    rows_lower(g + 2, q)
                if c < PIECES and left >= NC:
                    split(e + 1, 1 - p, c)
                elif c < PIECES:
                    src, high, low = late_piece(c)
                    eng.wait_ge(late_high, c + 1)
                    nc.vector.tensor_tensor(low, src, high.bitcast(F32), ALU.subtract).then_inc(late_low, 1)
                answer(g, e, q)

            rounds(eng, step)

        @block.tensor
        def _(eng):
            def turn(g, q):
                eng.wait_ge(rows_in[q], 16 * (g // 2 + 1))
                at_least(eng, rows_low, g)
                for k in range(KD):
                    for i in range(2):
                        last = nc.tensor.transpose(turned[:, k * CH + i * P:k * CH + (i + 1) * P],
                                                   rows[:, q, i, k * P:(k + 1) * P], ident[:])
                last.then_inc(turned_ok, 1)

            def product1(g, e, p, q):
                eng.wait_ge(w_low, PIECES * e + KD)
                eng.wait_ge(rows_low, g + 1)
                for j in range(4):
                    at_least(eng, relu_ok, 8 * (g - 1) + 2 * j + 2)
                    for i in range(2):
                        cols = slice((2 * j + i) * P, (2 * j + i + 1) * P)
                        last = split_product(nc, first[:, j, i * CH:(i + 1) * CH],
                                             lambda a, k: w1[:, p, a, k, cols],
                                             lambda a, k: rowsT[:, q, a, k], KD)
                    last.then_inc(first_ok, 1)

            def product2(g, e, p, q):
                eng.wait_ge(w_low, PIECES * (e + 1))
                eng.wait_ge(hid_low, 4 * (g + 1))
                at_least(eng, y_ok, g - 1)
                for i in range(2):
                    last = split_product(nc, second[q][:, i],
                                         lambda a, k: hidden2[:, q, a, k, i * P:(i + 1) * P],
                                         lambda a, k: w2[:, p, a, k], KH)
                last.then_inc(second_ok, 1)

            eng.wait_ge(ident_in, 16)
            turn(0, 0)
            turn(1, 1)
            product1(0, 0, 0, 0)

            def step(g, e, p, c, q, left):
                if left >= 1:
                    if c < NC - 1:
                        product1(g + 1, e, p, 1 - q)
                    else:
                        product1(g + 1, e + 1, 1 - p, 1 - q)
                if left >= 2:
                    turn(g + 2, q)
                product2(g, e, p, q)

            rounds(eng, step)


def finish(nc, t, keep):
    ctx = ExitStack()
    with ctx:
        def sb(name, shape, dt=F32):
            return ctx.enter_context(nc.sbuf_tensor(name, shape, dt))

        def pb(name, shape):
            return ctx.enter_context(nc.psum_tensor(name, shape, F32))

        sems = []

        def sem(name):
            sems.append(ctx.enter_context(nc.semaphore(name)))
            return sems[-1]

        w = keep["late"]
        ident = sb("f_ident", [P, P])
        iota_e = sb("f_iota_e", [P, E1])
        heads = sb("f_heads", [P, P])
        bq = sb("f_bq", [P, KD])
        bk = sb("f_bk", [P, KD])
        bias_in = sb("f_bias_in", [1, 2, D])
        bias = sb("f_bias", [1, 2, 2, D], F32R)
        ones = sb("f_ones", [1, P], F32R)
        rbias = sb("f_rbias", [P, E1])
        conv_w = sb("f_conv_w", [P, KD, KC])
        conv_b = sb("f_conv_b", [P, KD])
        minus_half = sb("f_minus_half", [P, 2])

        x1 = sb("f_x1", [P, 2, QT, D])
        picked = [sb(f"f_picked{i}", [P, QT * 2, D]) for i in range(2)]
        row = [sb(f"f_row{i}", [P, QT * 2], U32) for i in range(2)]
        cin = sb("f_cin", [P, 2, D])
        xa = sb("f_xa", [P, QT, D])
        x2 = sb("f_x2", [P, 2, QT, D])
        stats3 = sb("f_stats3", [P, QT, 6])
        mv3 = sb("f_mv3", [P, QT, 2])
        var3 = sb("f_var3", [P, QT])
        nm3 = sb("f_nm3", [P, QT])
        rs3 = sb("f_rs3", [P, QT])
        sh3 = sb("f_sh3", [P, QT])
        x3h = sb("f_x3h", [P, QT, D])
        xT = sb("f_xT", [P, 2, KD, S], F32R)
        cT = sb("f_cT", [P, 2, KD, C], F32R)
        qT = sb("f_qT", [P, 2, 2, KD, S], F32R)
        kf = sb("f_kf", [P, KD, C])
        kmax = sb("f_kmax", [P, KD])
        ke = sb("f_ke", [P, KD, C])
        ksum = sb("f_ksum", [P, KD])
        kn = sb("f_kn", [P, KD, C])
        kp = sb("f_kp", [C, 2, D], F32R)
        v = sb("f_v", [C, 2, D], F32R)
        cf = sb("f_cf", [P, KD, P])
        cx = sb("f_cx", [P, 2, KD, P], F32R)
        aT = sb("f_aT", [P, 2, KD, S], F32R)
        x2k = sb("f_x2k", [P, QT, D])
        x3 = sb("f_x3", [P, 2, QT, D])
        stats4 = sb("f_stats4", [P, QT, 6])
        mv4 = sb("f_mv4", [P, QT, 2])
        var4 = sb("f_var4", [P, QT])
        rs4 = sb("f_rs4", [P, QT])
        x4h = sb("f_x4h", [P, 2, QT, D])
        x4r = sb("f_x4r", [P, QT, D])
        x4p = sb("f_x4p", [P, KD, KC - 1 + S])
        x4T = sb("f_x4T", [P, 2, KD, S], F32R)
        cv = sb("f_cv", [P, KD, S])
        cvr = sb("f_cvr", [P, QT, D])
        taps = sb("f_taps", [P, KC, KD, S])
        re = sb("f_re", [P, QT, E1])
        rsg = sb("f_rsg", [P, QT, E1])
        sel = sb("f_sel", [P, QT, E1])
        top = sb("f_top", [P, QT, E1])
        topi = sb("f_topi", [P, QT, E1], U32)
        topf = sb("f_topf", [P, QT, 2])
        oh = sb("f_oh", [P, QT, 2, E1])
        cw = sb("f_cw", [P, QT, E1])
        cws = sb("f_cws", [P, QT])
        th = sb("f_th", [P, EM, S])
        hs = sb("f_hs", [P, EM, S])
        hid = sb("f_hid", [P, EM, S])
        hid2 = sb("f_hid2", [P, 2, EM, S], F32R)
        acc = sb("f_acc", [P, QT, D])
        yo = sb("f_yo", [P, 2, QT, D])

        mlp = pb("f_mlp", [P, EM, 512])
        bank_x = pb("f_bank_x", [P, 512])
        bank_c = pb("f_bank_c", [P, 512])
        bank_v = pb("f_bank_v", [P, 512])
        bank_t = pb("f_bank_t", [P, 512])

        small_in, bias_high, bias_low, const_g, ones_ok = (sem("f_" + s) for s in (
            "small_in", "bias_high", "bias_low", "const_g", "ones_ok"))
        x1_in = [sem(f"f_x1_in{i}") for i in range(2)]
        cin_in = [sem(f"f_cin_in{i}") for i in range(2)]
        picked_in = keep["picked_in"]
        row_ok = sem("f_row_ok")
        waited = sem("f_waited")
        xa_ok, x2_ok, stats3_ok, mv3_ok, var3_ok, rs3_ok, x3h_ok = (sem("f_" + s) for s in (
            "xa_ok", "x2_ok", "stats3_ok", "mv3_ok", "var3_ok", "rs3_ok", "x3h_ok"))
        x3T_ok, cT_ok, xT_high, xT_low, cT_high, cT_low = (sem("f_" + s) for s in (
            "x3T_ok", "cT_ok", "xT_high", "xT_low", "cT_high", "cT_low"))
        q_ok, q_high, q_low, k_ok, kf_ok, kmax_ok, ke_ok, kr_ok, kn_ok, kT_ok, kp_high, kp_low = (
            sem("f_" + s) for s in ("q_ok", "q_high", "q_low", "k_ok", "kf_ok", "kmax_ok", "ke_ok", "kr_ok",
                                    "kn_ok", "kT_ok", "kp_high", "kp_low"))
        v_ok, v_high, v_low, cx_ok, cf_ok, cx_high, cx_low, a_ok, a_high, a_low = (
            sem("f_" + s) for s in ("v_ok", "v_high", "v_low", "cx_ok", "cf_ok", "cx_high", "cx_low",
                                    "a_ok", "a_high", "a_low"))
        out_ok, x2k_ok, x3_ok, stats4_ok, mv4_ok, var4_ok, rs4_ok, x4h_ok, x4r_ok = (
            sem("f_" + s) for s in ("out_ok", "x2k_ok", "x3_ok", "stats4_ok", "mv4_ok", "var4_ok", "rs4_ok",
                                    "x4h_ok", "x4r_ok"))
        x4T_ok, x4p_ok, x4T_high, x4T_low, logit_ok, re_ok, route = (
            sem("f_" + s) for s in ("x4T_ok", "x4p_ok", "x4T_high", "x4T_low", "logit_ok", "re_ok", "route"))
        tap_ok, cv_ok, cvT_ok, cvr_ok, mix_ok, gu_ok, th_ok, hs_ok, hid_ok, hid_high, hid_low, down_ok, acc_ok, yo_ok = (
            sem("f_" + s) for s in ("tap_ok", "cv_ok", "cvT_ok", "cvr_ok", "mix_ok", "gu_ok", "th_ok", "hs_ok", "hid_ok",
                                    "hid_high", "hid_low", "down_ok", "acc_ok", "yo_ok"))
        yo_out = [sem(f"f_yo_out{i}") for i in range(2)]
        N_ROUTE = 17
        N_CV = KC - 1
        N_ACC = QT + QT * EM
        N_SMALL_F = 10

        def weight(name, plane, *index):
            base = LATE_AT[name]
            if name in ("WqT", "WkT"):
                k, m = index
                return w[:, plane, base + k * D + m * P:base + k * D + (m + 1) * P]
            if name in ("WvT", "WoT"):
                return w[:, plane, base + index[0] * D:base + (index[0] + 1) * D]
            if name in ("Wg", "Wu"):
                e, k = index
                return w[:, plane, base + (e * KD + k) * P:base + (e * KD + k + 1) * P]
            if name == "Wd":
                return w[:, plane, base + index[0] * D:base + (index[0] + 1) * D]
            return w[:, plane, base + index[0] * E1:base + (index[0] + 1) * E1]

        def bounds(b):
            return tuple(not isinstance(b, int) or b + n < B for n in (1, 2, 3, 4))

        ctx.callback(zero_semaphores, nc, sems)
        block = ctx.enter_context(nc.Block())

        @block.sync
        def _(eng):
            def load(b, p):
                at_least(eng, xa_ok, QT * (b - 1))
                eng.dma_start(x1[:, p], t["x1"][bass.ds(b, 1)].rearrange("o (k p) d -> p (o k) d", p=P)) \
                    .then_inc(x1_in[p], 16)
                at_least(eng, cT_ok, b - 1)
                eng.dma_start(cin[0:C, p], t["ctx"][bass.ds(b, 1)].rearrange("o c d -> c (o d)")) \
                    .then_inc(cin_in[p], 16)

            load(0, 0)
            small = [(ident[:], t["ident"]), (iota_e[:], t["iota_e"]), (heads[:], t["heads1"]),
                     (bq[:], t["bq"]), (bk[:], t["bk"]), (bias_in[:, 0], t["bv"].partition_broadcast(1)),
                     (bias_in[:, 1], t["bo1"].partition_broadcast(1)), (rbias[:], t["rbias"].partition_broadcast(P)),
                     (conv_w[:].unsqueeze(2), t["conv_w"]), (conv_b[:], t["conv_b"])]
            assert len(small) == N_SMALL_F
            for dst, src in small:
                eng.dma_start(dst, src).then_inc(small_in, 16)
            load(1, 1)
            load(2, 0)
            load(3, 1)

            def store(b, p):
                eng.wait_ge(yo_ok, b + 1)
                eng.dma_start(t["out"][bass.ds(b, 1)].rearrange("o (k p) d -> p (o k) d", p=P), yo[:, p]) \
                    .then_inc(yo_out[p], 16)

            def step(b, p):
                if bounds(b)[3]:
                    load(b + 4, p)
                if not (isinstance(b, int) and b < 1):
                    store(b - 1, 1 - p)

            batches(eng, step, 2)
            store(B - 1, 1)
            for p in range(2):
                eng.wait_ge(yo_out[p], 16 * (B // 2))

        @block.gpsimd
        def _(eng):
            nc.gpsimd.memset(minus_half[:], -0.5).then_inc(const_g, 1)
            nc.gpsimd.memset(x4p[:, :, 0:KC - 1], 0.0).then_inc(const_g, 1)
            eng.wait_ge(const_g, 2)

            def gather(b, p):
                at_least(eng, x2_ok, QT * (b - 1))
                nc.gpsimd.tensor_copy(row[p][:], keep["row"][:, bass.ds(b, 1)].rearrange("p o n -> p (o n)")) \
                    .then_inc(row_ok, 1)
                eng.wait_ge(row_ok, b + 1)
                by_itself(eng, waited)
                for n in range(QT * 2):
                    nc.gpsimd.indirect_dma_start(
                        out=picked[p][:, n], out_offset=None, in_=t["answers"],
                        in_offset=bass.IndirectOffsetOnAxis(ap=row[p][:, n:n + 1], axis=0),
                        bounds_check=E0 * SLOTS - 1, oob_is_err=False).then_inc(picked_in[p], 16)

            def rsqrt(b, mean_var, mean_var_ok, var, var_ok, r, r_ok, read_ok, nm=None, sh=None):
                steps = 1 if nm is None else 2
                eng.wait_ge(mean_var_ok, QT * (b + 1))
                at_least(eng, read_ok, QT * b)
                by_itself(eng, waited)
                nc.gpsimd.tensor_scalar(var[:], mean_var[:, :, 1], 1.0, EPS, ALU.mult, ALU.add).then_inc(var_ok, 1)
                if nm is not None:
                    nc.gpsimd.tensor_scalar(nm[:], mean_var[:, :, 0], -1.0, 0.0, ALU.mult, ALU.add) \
                        .then_inc(var_ok, 1)
                eng.wait_ge(var_ok, steps * (b + 1))
                nc.gpsimd.tensor_tensor(r[:], var[:], minus_half[:], ALU.pow).then_inc(r_ok, 1)
                if nm is not None:
                    eng.wait_ge(r_ok, steps * b + 1)
                    nc.gpsimd.tensor_tensor(sh[:], nm[:], r[:], ALU.mult).then_inc(r_ok, 1)

            def norm3(b):
                rsqrt(b, mv3, mv3_ok, var3, var3_ok, rs3, rs3_ok, x3h_ok, nm3, sh3)

            def norm4(b):
                rsqrt(b, mv4, mv4_ok, var4, var4_ok, rs4, rs4_ok, x4h_ok)

            def lower(b, high_ok, done, dst, src, high, low_ok, count=1):
                eng.wait_ge(high_ok, count)
                if done is not None:
                    at_least(eng, *done)
                nc.gpsimd.tensor_tensor(dst, src, high.bitcast(F32), ALU.subtract).then_inc(low_ok, 1)

            def cx_lower(b):
                lower(b, cx_high, (a_ok, b), cx[:, 1], cf[:], cx[:, 0], cx_low, b + 1)

            def hid_lower(b, j):
                es = slice(2 * j, 2 * j + 2)
                lower(b, hid_high, (down_ok, 2 * b), hid2[:, 1, es], hid[:, es], hid2[:, 0, es], hid_low,
                      2 * b + j + 1)

            def convolve(b, j):
                eng.wait_ge(tap_ok, KC * KD * b + KD * (j + 1))
                if j == 1:
                    at_least(eng, cvT_ok, b)
                at_least(eng, cv_ok, N_CV * b + j - 1)
                nc.gpsimd.tensor_tensor(cv[:], cv[:] if j > 1 else taps[:, 0], taps[:, j], ALU.add) \
                    .then_inc(cv_ok, 1)

            def mix(b):
                eng.wait_ge(x4r_ok, QT * (b + 1))
                eng.wait_ge(cvr_ok, b + 1)
                nc.gpsimd.tensor_tensor(x4r[:], x4r[:], cvr[:], ALU.add).then_inc(mix_ok, 1)

            gather(0, 0)
            gather(1, 1)
            norm3(0)
            norm3(1)
            gather(2, 0)
            gather(3, 1)
            cx_lower(0)
            norm3(2)
            norm4(0)

            def step(b, p):
                has1, _, has3, has4 = bounds(b)
                if has1:
                    cx_lower(b + 1)
                convolve(b, 1)
                hid_lower(b, 0)
                convolve(b, 2)
                if has3:
                    norm3(b + 3)
                convolve(b, 3)
                hid_lower(b, 1)
                if has1:
                    norm4(b + 1)
                mix(b)
                if has4:
                    gather(b + 4, p)

            batches(eng, step, 2)

        @block.scalar
        def _(eng):
            eng.wait_ge(small_in, 16 * N_SMALL_F)
            nc.scalar.activation(bias[:, 0], bias_in[:], ACT.Copy).then_inc(bias_high, 1)
            eng.wait_ge(const_g, 2)

            def xT_higher(b):
                eng.wait_ge(x3T_ok, b + 1)
                at_least(eng, q_ok, b)
                nc.scalar.activation(xT[:, 0], bank_x[:].rearrange("p (k s) -> p k s", k=KD), ACT.Copy) \
                    .then_inc(xT_high, 1)

            def cT_higher(b):
                eng.wait_ge(cT_ok, b + 1)
                at_least(eng, v_ok, b)
                nc.scalar.activation(cT[:, 0], bank_c[:, 0:KD * C].rearrange("p (k s) -> p k s", k=KD),
                                     ACT.Copy).then_inc(cT_high, 1)

            def q_higher(b, p):
                eng.wait_ge(q_ok, b + 1)
                at_least(eng, a_ok, b - 1)
                for k in range(KD):
                    nc.scalar.activation(qT[:, p, 0, k], bank_x[:, k * S:(k + 1) * S], ACT.Identity,
                                         bias=bq[:, k:k + 1]).then_inc(q_high, 1)

            def k_bias(b):
                eng.wait_ge(k_ok, b + 1)
                at_least(eng, ke_ok, KD * b)
                for k in range(KD):
                    nc.scalar.activation(kf[:, k], bank_c[:, k * C:(k + 1) * C], ACT.Identity,
                                         bias=bk[:, k:k + 1]).then_inc(kf_ok, 1)

            def k_exp(b):
                eng.wait_ge(kmax_ok, b + 1)
                at_least(eng, kn_ok, KD * b)
                for k in range(KD):
                    nc.scalar.activation(ke[:, k], kf[:, k], ACT.Exp, bias=kmax[:, k:k + 1],
                                         accum_out=ksum[:, k:k + 1]).then_inc(ke_ok, 1)

            def k_norm(b):
                eng.wait_ge(kr_ok, b + 1)
                at_least(eng, kT_ok, b)
                for k in range(KD):
                    nc.scalar.activation(kn[:, k], ke[:, k], ACT.Copy, scale=ksum[:, k:k + 1]).then_inc(kn_ok, 1)

            def kp_higher(b):
                eng.wait_ge(kT_ok, b + 1)
                at_least(eng, cx_ok, b)
                nc.scalar.activation(kp[:, 0], bank_v[0:C, 0:D], ACT.Copy).then_inc(kp_high, 1)

            def v_higher(b):
                eng.wait_ge(v_ok, b + 1)
                at_least(eng, cx_ok, b)
                nc.scalar.activation(v[:, 0], bank_v[0:C, 0:D], ACT.Copy).then_inc(v_high, 1)

            def cx_higher(b):
                eng.wait_ge(cf_ok, b + 1)
                at_least(eng, a_ok, b)
                nc.scalar.activation(cx[:, 0], cf[:], ACT.Copy).then_inc(cx_high, 1)

            def a_higher(b):
                eng.wait_ge(a_ok, b + 1)
                at_least(eng, out_ok, b)
                nc.scalar.activation(aT[:, 0], bank_x[:].rearrange("p (k s) -> p k s", k=KD), ACT.Copy) \
                    .then_inc(a_high, 1)

            def x4_turned(b):
                eng.wait_ge(x4T_ok, b + 1)
                at_least(eng, gu_ok, 4 * b)
                at_least(eng, tap_ok, KC * KD * b)
                turned = bank_t[:].rearrange("p (k s) -> p k s", k=KD)
                nc.scalar.activation(x4T[:, 0], turned, ACT.Copy).then_inc(x4T_high, 1)
                nc.scalar.activation(x4p[:, :, KC - 1:], turned, ACT.Copy).then_inc(x4p_ok, 1)

            def x4_relu(b, p):
                eng.wait_ge(route, N_ROUTE * (b + 1))
                at_least(eng, acc_ok, N_ACC * (b - 1) + QT)
                for i in range(QT):
                    nc.scalar.activation(x4r[:, i], x4h[:, p, i], ACT.Relu, scale=cw[:, i, EM + 3:EM + 4]) \
                        .then_inc(x4r_ok, 1)

            def tap(b, js):
                at_least(eng, cv_ok, N_CV * b)
                if js[0] == 0:
                    eng.wait_ge(x4p_ok, b + 1)
                for j in js:
                    for k in range(KD):
                        shift = {"bias": conv_b[:, k:k + 1]} if j == 0 else {}
                        nc.scalar.activation(taps[:, j, k], x4p[:, k, j:j + S], ACT.Identity,
                                             scale=conv_w[:, k, j:j + 1], **shift).then_inc(tap_ok, 1)

            def router_exp(b):
                eng.wait_ge(logit_ok, b + 1)
                at_least(eng, route, N_ROUTE * b)
                nc.scalar.activation(re[:], bank_t[:, 0:QT * E1].rearrange("p (t e) -> p t e", t=QT), ACT.Exp,
                                     scale=-1.0).then_inc(re_ok, 1)

            def tanh(b, j):
                eng.wait_ge(gu_ok, 4 * b + 2 * j + 2)
                at_least(eng, hs_ok, 2 * (b - 1) + j + 1)
                nc.scalar.activation(th[:, 2 * j:2 * j + 2], mlp[:, 2 * j:2 * j + 2, 0:S], ACT.Tanh,
                                     scale=0.5).then_inc(th_ok, 1)

            def hid_higher(b, j):
                eng.wait_ge(hid_ok, 2 * b + j + 1)
                at_least(eng, down_ok, 2 * b)
                nc.scalar.activation(hid2[:, 0, 2 * j:2 * j + 2], hid[:, 2 * j:2 * j + 2], ACT.Copy) \
                    .then_inc(hid_high, 1)

            def conv_rows(b):
                eng.wait_ge(cvT_ok, b + 1)
                at_least(eng, mix_ok, b)
                nc.scalar.activation(cvr[:], bank_t[:].rearrange("p (t d) -> p t d", t=QT), ACT.Copy) \
                    .then_inc(cvr_ok, 1)

            def normalise3(b, p):
                eng.wait_ge(rs3_ok, 2 * (b + 1))
                at_least(eng, x3T_ok, b)
                for i in range(QT):
                    nc.scalar.activation(x3h[:, i], x2[:, p, i], ACT.Identity, scale=rs3[:, i:i + 1],
                                         bias=sh3[:, i:i + 1]).then_inc(x3h_ok, 1)

            def keep_x2(b, p):
                eng.wait_ge(x2_ok, QT * (b + 1))
                at_least(eng, x3_ok, b)
                nc.scalar.activation(x2k[:], x2[:, p], ACT.Copy).then_inc(x2k_ok, 1)

            def first_half(b, p):
                xT_higher(b)
                cT_higher(b)
                q_higher(b, p)
                k_bias(b)
                k_exp(b)
                k_norm(b)
                v_higher(b)

            normalise3(0, 0)
            first_half(0, 0)
            kp_higher(0)
            cx_higher(0)
            normalise3(1, 1)
            first_half(1, 1)
            keep_x2(0, 0)
            a_higher(0)
            normalise3(2, 0)

            def step(b, p):
                has1, has2, has3, _ = bounds(b)
                if has2:
                    xT_higher(b + 2)
                x4_turned(b)
                if has1:
                    kp_higher(b + 1)
                if has2:
                    cT_higher(b + 2)
                if has1:
                    keep_x2(b + 1, 1 - p)
                if has2:
                    q_higher(b + 2, p)
                router_exp(b)
                tap(b, (0, 1))
                tanh(b, 0)
                if has1:
                    cx_higher(b + 1)
                tap(b, (2, 3))
                hid_higher(b, 0)
                if has2:
                    k_bias(b + 2)
                if has1:
                    a_higher(b + 1)
                tanh(b, 1)
                if has2:
                    k_exp(b + 2)
                    v_higher(b + 2)
                hid_higher(b, 1)
                if has3:
                    normalise3(b + 3, 1 - p)
                conv_rows(b)
                if has2:
                    k_norm(b + 2)
                x4_relu(b, p)

            batches(eng, step, 2)

        @block.vector
        def _(eng):
            def combine(b, p):
                eng.wait_ge(x1_in[p], 16 * (b // 2 + 1))
                eng.wait_ge(picked_in[p], 16 * QT * 2 * (b // 2 + 1))
                at_least(eng, x2k_ok, b - 1)
                at_least(eng, x3h_ok, QT * (b - 1))
                share = keep["weight"][:, bass.ds(b, 1)].rearrange("p o n -> p (o n)")
                for i in range(QT):
                    nc.vector.scalar_tensor_tensor(xa[:, i], picked[p][:, 2 * i], share[:, 2 * i:2 * i + 1],
                                                   x1[:, p, i], ALU.mult, ALU.add).then_inc(xa_ok, 1)
                for i in range(QT):
                    eng.wait_ge(xa_ok, QT * b + i + 1)
                    nc.vector.scalar_tensor_tensor(x2[:, p, i], picked[p][:, 2 * i + 1],
                                                   share[:, 2 * i + 1:2 * i + 2], xa[:, i],
                                                   ALU.mult, ALU.add).then_inc(x2_ok, 1)

            def stat3(b, p):
                for i in range(QT):
                    eng.wait_ge(x2_ok, QT * b + i + 1)
                    nc.vector.bn_stats(stats3[:, i], x2[:, p, i]).then_inc(stats3_ok, 1)
                eng.wait_ge(stats3_ok, QT * (b + 1))
                by_itself(eng, waited)
                for i in range(QT):
                    nc.vector.bn_aggr(mv3[:, i], stats3[:, i]).then_inc(mv3_ok, 1)

            def xT_lower(b):
                eng.wait_ge(xT_high, b + 1)
                nc.vector.tensor_tensor(xT[:, 1], bank_x[:].rearrange("p (k s) -> p k s", k=KD),
                                        xT[:, 0].bitcast(F32), ALU.subtract).then_inc(xT_low, 1)

            def cT_lower(b):
                eng.wait_ge(cT_high, b + 1)
                nc.vector.tensor_tensor(cT[:, 1], bank_c[:, 0:KD * C].rearrange("p (k s) -> p k s", k=KD),
                                        cT[:, 0].bitcast(F32), ALU.subtract).then_inc(cT_low, 1)

            def q_lower(b, p):
                eng.wait_ge(q_high, KD * (b + 1))
                for k in range(KD):
                    nc.vector.scalar_tensor_tensor(qT[:, p, 1, k], bank_x[:, k * S:(k + 1) * S], bq[:, k:k + 1],
                                                   qT[:, p, 0, k].bitcast(F32), ALU.add, ALU.subtract) \
                        .then_inc(q_low, 1)

            def k_max(b):
                eng.wait_ge(kf_ok, KD * (b + 1))
                nc.vector.tensor_reduce(kmax[:], kf[:], AX.X, ALU.max, negate=True).then_inc(kmax_ok, 1)

            def k_sums(b):
                eng.wait_ge(ke_ok, KD * (b + 1))
                nc.vector.reciprocal(ksum[:], ksum[:]).then_inc(kr_ok, 1)

            def v_lower(b):
                eng.wait_ge(v_high, b + 1)
                nc.vector.tensor_tensor(v[:, 1], bank_v[0:C, 0:D], v[:, 0].bitcast(F32), ALU.subtract) \
                    .then_inc(v_low, 1)

            def kp_lower(b):
                eng.wait_ge(kp_high, b + 1)
                nc.vector.tensor_tensor(kp[:, 1], bank_v[0:C, 0:D], kp[:, 0].bitcast(F32), ALU.subtract) \
                    .then_inc(kp_low, 1)

            def own_heads(b):
                eng.wait_ge(cx_ok, b + 1)
                at_least(eng, cx_low, b)
                nc.vector.tensor_tensor(cf[:], bank_v[:, 0:KD * P].rearrange("p (k e) -> p k e", k=KD),
                                        heads[:].unsqueeze(1).to_broadcast([P, KD, P]), ALU.mult) \
                    .then_inc(cf_ok, 1)

            def a_lower(b):
                eng.wait_ge(a_high, b + 1)
                nc.vector.tensor_tensor(aT[:, 1], bank_x[:].rearrange("p (k s) -> p k s", k=KD),
                                        aT[:, 0].bitcast(F32), ALU.subtract).then_inc(a_low, 1)

            def x3_new(b, p):
                eng.wait_ge(out_ok, b + 1)
                eng.wait_ge(x2k_ok, b + 1)
                at_least(eng, yo_ok, b - 1)
                nc.vector.scalar_tensor_tensor(x3[:, p], bank_c[:].rearrange("p (t d) -> p t d", t=QT),
                                               keep["gate"][:, 1:2], x2k[:], ALU.mult, ALU.add).then_inc(x3_ok, 1)
                eng.wait_ge(x3_ok, b + 1)
                for i in range(QT):
                    nc.vector.bn_stats(stats4[:, i], x3[:, p, i]).then_inc(stats4_ok, 1)
                eng.wait_ge(stats4_ok, QT * (b + 1))
                by_itself(eng, waited)
                for i in range(QT):
                    nc.vector.bn_aggr(mv4[:, i], stats4[:, i]).then_inc(mv4_ok, 1)

            def normalise4(b, p):
                eng.wait_ge(rs4_ok, b + 1)
                at_least(eng, acc_ok, N_ACC * (b - 2) + QT)
                at_least(eng, x4r_ok, QT * (b - 1))
                at_least(eng, x4T_ok, b - 1)
                for i in range(QT):
                    nc.vector.tensor_scalar(x4h[:, p, i], x3[:, p, i], mv4[:, i, 0:1], rs4[:, i:i + 1],
                                            ALU.subtract, ALU.mult).then_inc(x4h_ok, 1)

            def x4_lower(b):
                eng.wait_ge(x4p_ok, b + 1)
                nc.vector.tensor_tensor(x4T[:, 1], bank_t[:].rearrange("p (k s) -> p k s", k=KD),
                                        x4T[:, 0].bitcast(F32), ALU.subtract).then_inc(x4T_low, 1)

            def wide(ap):
                return ap.unsqueeze(2).to_broadcast([P, QT, E1])

            DONE = (0, 1, 2, 3, 5, 7, 8, 10, 11, 12, 13, 14, 15, 16)

            def router(b, *parts):
                for part in parts:
                    if part == 0:
                        eng.wait_ge(re_ok, b + 1)
                        at_least(eng, x4r_ok, QT * b)
                    else:
                        eng.wait_ge(route, N_ROUTE * b + DONE[part])
                    if part in (3, 4):
                        by_itself(eng, waited)
                    for instruction in router_part(part):
                        instruction.then_inc(route, 1)

            def router_part(part):
                if part == 0:
                    return [nc.vector.tensor_scalar(re[:], re[:], 1.0, None, ALU.add)]
                if part == 1:
                    return [nc.vector.reciprocal(rsg[:], re[:])]
                if part == 2:
                    return [nc.vector.tensor_tensor(sel[:], rsg[:], rbias[:].unsqueeze(1).to_broadcast([P, QT, E1]),
                                                    ALU.add)]
                if part == 3:
                    return [nc.vector.max(top[:, i], sel[:, i]) for i in range(QT)]
                if part == 4:
                    return [nc.vector.max_index(topi[:, i], top[:, i], sel[:, i]) for i in range(QT)]
                if part == 5:
                    return [nc.vector.tensor_copy(topf[:], topi[:, :, 0:2])]
                if part == 6:
                    return [nc.vector.tensor_tensor(oh[:, i], iota_e[:].unsqueeze(1).to_broadcast([P, 2, E1]),
                                                    topf[:, i].unsqueeze(2).to_broadcast([P, 2, E1]), ALU.is_equal)
                            for i in range(QT)]
                if part == 7:
                    return [nc.vector.tensor_tensor(cw[:], oh[:, :, 0], oh[:, :, 1], ALU.add)]
                if part == 8:
                    return [nc.vector.tensor_tensor(cw[:], cw[:], rsg[:], ALU.mult)]
                if part == 9:
                    return [nc.vector.reduce_sum(cws[:], cw[:], AX.X)]
                if part == 10:
                    return [nc.vector.tensor_scalar(cws[:], cws[:], 1e-9, None, ALU.add)]
                if part == 11:
                    return [nc.vector.reciprocal(cws[:], cws[:])]
                if part == 12:
                    return [nc.vector.tensor_tensor(cw[:], cw[:], wide(cws[:]), ALU.mult)]
                return [nc.vector.tensor_tensor(cws[:], cw[:, :, EM], cw[:, :, EM + 2], ALU.add)]

            def silu(b, j):
                es = slice(2 * j, 2 * j + 2)
                eng.wait_ge(th_ok, 2 * b + j + 1)
                at_least(eng, hid_low, 2 * (b - 1) + j + 1)
                nc.vector.scalar_tensor_tensor(hs[:, es], th[:, es], 1.0, mlp[:, es, 0:S], ALU.add, ALU.mult) \
                    .then_inc(hs_ok, 1)
                eng.wait_ge(hs_ok, 2 * b + j + 1)
                nc.vector.scalar_tensor_tensor(hid[:, es], hs[:, es], 0.5, mlp[:, es, S:2 * S], ALU.mult, ALU.mult) \
                    .then_inc(hid_ok, 1)

            def simple(b, p):
                eng.wait_ge(mix_ok, b + 1)
                at_least(eng, yo_ok, b)
                for i in range(QT):
                    nc.vector.scalar_tensor_tensor(acc[:, i], x4h[:, p, i], cws[:, i:i + 1], x4r[:, i],
                                                   ALU.mult, ALU.add).then_inc(acc_ok, 1)

            def weigh(b, j):
                eng.wait_ge(down_ok, 2 * b + j + 1)
                for e in (2 * j, 2 * j + 1):
                    for i in range(QT):
                        eng.wait_ge(acc_ok, N_ACC * b + QT * e + i + 1)
                        nc.vector.scalar_tensor_tensor(acc[:, i], mlp[:, e, i * D:(i + 1) * D], cw[:, i, e:e + 1],
                                                       acc[:, i], ALU.mult, ALU.add).then_inc(acc_ok, 1)

            def close(b, p):
                eng.wait_ge(acc_ok, N_ACC * (b + 1))
                at_least(eng, yo_out[p], 16 * (b // 2))
                nc.vector.scalar_tensor_tensor(yo[:, p], acc[:], keep["gate"][:, 3:4], x3[:, p],
                                               ALU.mult, ALU.add).then_inc(yo_ok, 1)

            def first_half(b, p):
                xT_lower(b)
                cT_lower(b)
                q_lower(b, p)
                k_max(b)
                k_sums(b)
                v_lower(b)

            eng.wait_ge(small_in, 16 * N_SMALL_F)
            nc.vector.memset(ones[:].bitcast(F32), 1.0).then_inc(ones_ok, 1)
            combine(0, 0)
            stat3(0, 0)
            eng.wait_ge(bias_high, 1)
            nc.vector.tensor_tensor(bias[:, 1], bias_in[:], bias[:, 0].bitcast(F32), ALU.subtract).then_inc(bias_low, 1)
            first_half(0, 0)
            combine(1, 1)
            stat3(1, 1)
            kp_lower(0)
            own_heads(0)
            first_half(1, 1)
            a_lower(0)
            x3_new(0, 0)
            combine(2, 0)
            stat3(2, 0)
            normalise4(0, 0)

            def step(b, p):
                has1, has2, has3, _ = bounds(b)
                first = isinstance(b, int) and b == 0
                if has2:
                    xT_lower(b + 2)
                x4_lower(b)
                if has1:
                    kp_lower(b + 1)
                if has2:
                    cT_lower(b + 2)
                if not first:
                    simple(b - 1, 1 - p)
                    weigh(b - 1, 0)
                if has2:
                    q_lower(b + 2, p)
                if has1:
                    own_heads(b + 1)
                router(b, 0)
                if not first:
                    weigh(b - 1, 1)
                router(b, 1)
                silu(b, 0)
                router(b, 2)
                if has3:
                    combine(b + 3, 1 - p)
                router(b, 3)
                if has1:
                    a_lower(b + 1)
                if has3:
                    stat3(b + 3, 1 - p)
                if has2:
                    k_max(b + 2)
                router(b, 4)
                router(b, 5)
                silu(b, 1)
                if not first:
                    close(b - 1, 1 - p)
                router(b, 6)
                if has1:
                    x3_new(b + 1, 1 - p)
                router(b, 7)
                if has2:
                    k_sums(b + 2)
                router(b, 8)
                if has2:
                    v_lower(b + 2)
                router(b, 9)
                router(b, 10, 11, 12, 13)
                if has1:
                    normalise4(b + 1, 1 - p)

            batches(eng, step, 2)
            simple(B - 1, 1)
            weigh(B - 1, 0)
            weigh(B - 1, 1)
            close(B - 1, 1)

        @block.tensor
        def _(eng):
            def turn3(b, p):
                eng.wait_ge(x3h_ok, QT * (b + 1))
                at_least(eng, a_low, b - 1)
                at_least(eng, q_low, KD * b)
                for k in range(KD):
                    for i in range(QT):
                        last = nc.tensor.transpose(bank_x[:, k * S + i * P:k * S + (i + 1) * P],
                                                   x3h[:, i, k * P:(k + 1) * P], ident[:])
                last.then_inc(x3T_ok, 1)

            def turn_c(b, p):
                eng.wait_ge(cin_in[p], 16 * (b // 2 + 1))
                at_least(eng, x3_ok, b - 1)
                at_least(eng, kf_ok, KD * b)
                for k in range(KD):
                    last = nc.tensor.transpose(bank_c[:, k * C:(k + 1) * C], cin[0:C, p, k * P:(k + 1) * P],
                                               ident[0:C, 0:C])
                last.then_inc(cT_ok, 1)

            def queries(b):
                eng.wait_ge(xT_low, b + 1)
                for m in range(KD):
                    last = split_product(nc, bank_x[:, m * S:(m + 1) * S], lambda a, k: weight("WqT", a, k, m),
                                         lambda a, k: xT[:, a, k], KD)
                last.then_inc(q_ok, 1)

            def add_bias(out, which):
                for a in range(2):
                    last = nc.tensor.matmul(out, ones[:, 0:out.shape[0]], bias[:, a, which], start=False, stop=a == 1)
                return last

            def keys(b):
                eng.wait_ge(cT_low, b + 1)
                for m in range(KD):
                    last = split_product(nc, bank_c[:, m * C:(m + 1) * C], lambda a, k: weight("WkT", a, k, m),
                                         lambda a, k: cT[:, a, k], KD)
                last.then_inc(k_ok, 1)

            def values(b):
                at_least(eng, cf_ok, b)
                split_product(nc, bank_v[0:C, 0:D], lambda a, k: cT[:, a, k], lambda a, k: weight("WvT", a, k),
                              KD, stop=False)
                add_bias(bank_v[0:C, 0:D], 0).then_inc(v_ok, 1)

            def min_batches(n):
                return min(n, B) if isinstance(n, int) else n

            def turn_k(b):
                eng.wait_ge(kn_ok, KD * (b + 1))
                eng.wait_ge(v_low, b + 1)
                for k in range(KD):
                    last = nc.tensor.transpose(bank_v[0:C, k * P:(k + 1) * P], kn[:, k], ident[:])
                last.then_inc(kT_ok, 1)

            def context(b):
                eng.wait_ge(kp_low, b + 1)
                eng.wait_ge(v_low, b + 1)
                for m in range(KD):
                    cols = slice(m * P, (m + 1) * P)
                    last = split_product(nc, bank_v[:, cols], lambda a, _: kp[:, a, cols],
                                         lambda a, _: v[:, a, cols], 1)
                last.then_inc(cx_ok, 1)

            def attended(b, p):
                eng.wait_ge(cx_low, b + 1)
                eng.wait_ge(q_low, KD * min_batches(b + 2))
                for m in range(KD):
                    last = split_product(nc, bank_x[:, m * S:(m + 1) * S], lambda a, _: cx[:, a, m],
                                         lambda a, _: qT[:, p, a, m], 1)
                last.then_inc(a_ok, 1)

            def output(b):
                eng.wait_ge(a_low, b + 1)
                eng.wait_ge(kf_ok, KD * min_batches(b + 2))
                for i in range(QT):
                    last = split_product(nc, bank_c[:, i * D:(i + 1) * D],
                                         lambda a, k: aT[:, a, k, i * P:(i + 1) * P],
                                         lambda a, k: weight("WoT", a, k), KD, stop=False)
                    last = add_bias(bank_c[:, i * D:(i + 1) * D], 1)
                last.then_inc(out_ok, 1)

            def turn4(b, p):
                eng.wait_ge(x4h_ok, QT * (b + 1))
                at_least(eng, cvr_ok, b)
                for k in range(KD):
                    for i in range(QT):
                        last = nc.tensor.transpose(bank_t[:, k * S + i * P:k * S + (i + 1) * P],
                                                   x4h[:, p, i, k * P:(k + 1) * P], ident[:])
                last.then_inc(x4T_ok, 1)

            def logits(b):
                eng.wait_ge(x4T_low, b + 1)
                for i in range(QT):
                    last = split_product(nc, bank_t[:, i * E1:(i + 1) * E1],
                                         lambda a, k: x4T[:, a, k, i * P:(i + 1) * P],
                                         lambda a, k: weight("Wr1", a, k), KD)
                last.then_inc(logit_ok, 1)

            def gate_up(b, e):
                at_least(eng, acc_ok, N_ACC * (b - 1) + QT + QT * (e + 1))
                for half, name in enumerate(("Wg", "Wu")):
                    last = split_product(nc, mlp[:, e, half * S:(half + 1) * S],
                                         lambda a, k: weight(name, a, e, k), lambda a, k: x4T[:, a, k], KD)
                last.then_inc(gu_ok, 1)

            def turn_conv(b):
                eng.wait_ge(cv_ok, N_CV * (b + 1))
                eng.wait_ge(re_ok, b + 1)
                for k in range(KD):
                    for i in range(QT):
                        last = nc.tensor.transpose(bank_t[:, i * D + k * P:i * D + (k + 1) * P],
                                                   cv[:, k, i * P:(i + 1) * P], ident[:])
                last.then_inc(cvT_ok, 1)

            def down(b, j):
                eng.wait_ge(hid_low, 2 * b + j + 1)
                for e in (2 * j, 2 * j + 1):
                    for i in range(QT):
                        last = split_product(nc, mlp[:, e, i * D:(i + 1) * D],
                                             lambda a, _: hid2[:, a, e, i * P:(i + 1) * P],
                                             lambda a, _: weight("Wd", a, e), 1)
                last.then_inc(down_ok, 1)

            eng.wait_ge(small_in, 16 * N_SMALL_F)
            turn3(0, 0)
            turn_c(0, 0)
            eng.wait_ge(keep["late_low"], PIECES)
            eng.wait_ge(bias_low, 1)
            eng.wait_ge(ones_ok, 1)
            queries(0)
            keys(0)
            values(0)
            turn_k(0)
            context(0)
            turn3(1, 1)
            turn_c(1, 1)
            queries(1)
            keys(1)
            attended(0, 0)
            values(1)
            output(0)

            def step(b, p):
                has1, has2, _, _ = bounds(b)
                if has2:
                    turn3(b + 2, p)
                    turn_c(b + 2, p)
                if has1:
                    turn_k(b + 1)
                turn4(b, p)
                if has2:
                    queries(b + 2)
                logits(b)
                if has1:
                    context(b + 1)
                gate_up(b, 0)
                gate_up(b, 1)
                if has2:
                    keys(b + 2)
                gate_up(b, 2)
                if has1:
                    attended(b + 1, 1 - p)
                gate_up(b, 3)
                if has2:
                    values(b + 2)
                if has1:
                    output(b + 1)
                down(b, 0)
                turn_conv(b)
                down(b, 1)

            batches(eng, step, 2)


def build(nc, t):
    with ExitStack() as ctx:
        keep = {
            "weight": ctx.enter_context(nc.sbuf_tensor("keep_weight", [P, B, QT * 2], F32)),
            "row": ctx.enter_context(nc.sbuf_tensor("keep_row", [P, B, QT * 2], U32)),
            "gate": ctx.enter_context(nc.sbuf_tensor("keep_gate", [P, 4], F32)),
            "sent": [ctx.enter_context(nc.semaphore(f"sent{i}")) for i in range(2)],
            "picked_in": [ctx.enter_context(nc.semaphore(f"picked_in{i}")) for i in range(2)],
            "late_in": ctx.enter_context(nc.semaphore("late_in")),
            "late_high": ctx.enter_context(nc.semaphore("late_high")),
            "late_low": ctx.enter_context(nc.semaphore("late_low")),
        }
        keep["w1_in"] = ctx.enter_context(nc.sbuf_tensor("w1_in", [P, KD, HID], F32))
        keep["w1_loaded"] = ctx.enter_context(nc.semaphore("w1_loaded"))
        attend(nc, t, keep)
        keep["late"] = ctx.enter_context(nc.sbuf_tensor("late", [P, 2, LATE_SIZE], F32R))
        experts(nc, t, keep)
        finish(nc, t, keep)



def constants():
    one = 0x3F80
    eye = np.eye(P, dtype=np.float32)
    headrow = np.zeros((P, H0, P), np.uint16)
    for h in range(H0):
        headrow[h, h] = headrow[64 + h, h] = one
    firstrow = np.zeros((P, P), np.uint16)
    firstrow[0] = firstrow[64] = one
    tri = np.stack([np.triu(np.ones((P, P)), 1), np.ones((P, P))], 1).astype(np.uint16) * np.uint16(one)
    slot0 = np.arange(B)[:, None] * CAP + np.arange(E0)[None] * SLOTS
    heads1 = np.kron(np.eye(P // HD1), np.ones((HD1, HD1))).astype(np.float32)
    return {
        "ident": eye, "headrow": headrow, "firstrow": firstrow, "tri": tri, "heads1": heads1,
        "iota_e": np.tile(np.arange(E0, dtype=np.float32), (P, 1)),
        "slot0": np.tile(slot0.astype(np.float32), (P, 1, 1)),
    }


NAMES = {
    "x": "x", "ctx": "ctx_1024", "g_xattn": "g_xattn", "g_ffn": "g_ffn",
    "g_x": "L0_xattn_g_x", "b_x": "L0_xattn_b_x", "g_l": "L0_xattn_g_l", "b_l": "L0_xattn_b_l",
    "w_q": "L0_xattn_w_q", "w_kv": "L0_xattn_w_kv", "w_out": "L0_xattn_w_out",
    "g_o": "L0_xattn_g_o", "b_o": "L0_xattn_b_o",
    "Wr0": "L0_ffn_Wr", "br": "L0_ffn_br", "W1": "L0_ffn_W1", "b1": "L0_ffn_b1", "W2": "L0_ffn_W2",
    "b2": "L0_ffn_b2",
    "bq": "L1_xattn_bq", "bk": "L1_xattn_bk", "bv": "L1_xattn_bv", "bo1": "L1_xattn_bo",
    "Wr1": "L1_ffn_Wr", "rbias": "L1_ffn_router_bias", "Wg": "L1_ffn_Wg", "Wu": "L1_ffn_Wu", "Wd": "L1_ffn_Wd",
    "conv_w": "L1_ffn_conv_w", "conv_b": "L1_ffn_conv_b",
}
TURNED = {"WqT": "L1_xattn_Wq", "WkT": "L1_xattn_Wk", "WvT": "L1_xattn_Wv", "WoT": "L1_xattn_Wo"}


def layout(inputs):
    arrays = {n: np.ascontiguousarray(inputs[full]) for n, full in NAMES.items()}
    arrays.update({n: np.ascontiguousarray(np.asarray(inputs[full]).T) for n, full in TURNED.items()})
    for n in ("g_l", "b_l", "g_x", "b_x", "bq", "bk", "b1", "conv_w", "conv_b"):
        a = arrays[n]
        arrays[n] = np.ascontiguousarray(a.reshape(*a.shape[:-1], a.shape[-1] // P, P).T)
    mask = np.ascontiguousarray(inputs["mask_BxS2_bf1"]).view(np.uint8)
    arrays["mask"] = mask
    arrays["mask_t"] = np.ascontiguousarray(mask.T)
    arrays.update(constants())
    return arrays


def kernel(**inputs):
    import concourse.bacc as bacc
    from concourse.bass_utils import run_bass_kernel_spmd

    nc = bacc.Bacc("TRN2", target_bir_lowering=False, num_devices=1)
    arrays = layout(inputs)
    t = {n: nc.dram_tensor(n, a.shape, mybir.dt.from_np(a.dtype), kind="ExternalInput").ap()
         for n, a in arrays.items()}
    t["out"] = nc.dram_tensor("out", (B, S, D), F32, kind="ExternalOutput").ap()
    t["x1"] = nc.dram_tensor("x1", (B, S, D), F32, kind="Internal").ap()
    t["slots"] = nc.dram_tensor("slots", (E0 * SLOTS, D), F32, kind="Internal").ap()
    t["answers"] = nc.dram_tensor("answers", (E0 * SLOTS, D), F32, kind="Internal").ap()
    build(nc, t)
    r = run_bass_kernel_spmd(nc, [arrays], core_ids=[0])
    return r.results[0]["out"]
```
